# Optimizing a Trainium2 kernel written in Bass

```python
import numpy as np
import jax
import jax.numpy as jnp

def _softmax(x, axis=-1):
    return jax.nn.softmax(x, axis=axis)

def _gelu(x):
    return jax.nn.gelu(x, approximate=True)

def _silu(x):
    return jax.nn.silu(x)

def _sigmoid(x):
    return jax.nn.sigmoid(x)

def _layernorm(x, axis=-1, eps=1e-05):
    m = jnp.mean(x, axis=axis, keepdims=True)
    v = jnp.var(x, axis=axis, keepdims=True)
    return (x - m) / jnp.sqrt(v + eps)

def _scatter_add(tgt, idx, src, axis=0):
    return tgt.at[idx].add(src)

def _segment_sum(src, seg, n):
    return jax.ops.segment_sum(src, seg, n)
kernel_name = 'mk_adj_ffn_d4_adj_r2_847b2b'

def setup_inputs(seed: int=0):
    np.random.seed(seed)
    _w = jnp.asarray

    def _rec_inputs():
        import jax
        import jax.numpy as jnp
        _gk = jax.random.key(seed)
        x = -0.000929 + 1 * jax.random.normal(jax.random.fold_in(_gk, 1), (3327, 128), jnp.float32)
        _a = jax.random.bernoulli(jax.random.fold_in(_gk, 2), 0.00240457, (3327, 3327))
        _a = jnp.logical_or(_a, jnp.swapaxes(_a, -1, -2))
        _a = jnp.logical_or(_a, jnp.eye(3327, dtype=bool))
        adj = _a.astype(jnp.int32)
        return (x, adj)
    x, adj = _rec_inputs()

    def _L0_gnn_setup():
        import jax, jax.numpy as jnp
        import numpy as np
        N, IN_C, OUT_C, H = (2048, 128, 128, 8)
        HD = OUT_C // H
        key = jax.random.key(seed)
        k1, k2, k3, k4, k5, k6 = jax.random.split(key, 6)
        node_features = jax.random.normal(k1, (N, IN_C), dtype=jnp.float32)
        adjacency_matrix = jax.random.randint(k2, (N, N), 0, 2, dtype=jnp.int32)
        W_w = jax.random.normal(k3, (OUT_C, IN_C), dtype=jnp.float32) * (1.0 / np.sqrt(IN_C))
        W_b = jax.random.normal(k4, (OUT_C,), dtype=jnp.float32) * 0.01
        a_w = jax.random.normal(k5, (1, 2 * HD), dtype=jnp.float32) * (1.0 / np.sqrt(2 * HD))
        a_b = jax.random.normal(k6, (1,), dtype=jnp.float32) * 0.01
        return {'node_features': node_features, 'adjacency_matrix': adjacency_matrix, 'W_w': W_w, 'W_b': W_b, 'a_w': a_w, 'a_b': a_b}
    _L0_gnn_all = _L0_gnn_setup()
    _L0_gnn_in = {k: v for k, v in _L0_gnn_all.items() if k in ('W_w', 'W_b', 'a_w', 'a_b')}
    del _L0_gnn_all

    def _L0_ffn_setup():
        import jax, jax.numpy as jnp
        import numpy as np
        E = 8
        K = 2
        D = 128
        H = 256
        DOUT = 128
        EPS = 1e-05
        key = jax.random.key(seed)
        ks = jax.random.split(key, 9)
        s = 0.02
        return {'x': jax.random.normal(ks[0], (4, 4096, D), jnp.float32), 'gamma': 1.0 + 0.05 * jax.random.normal(ks[1], (D,), jnp.float32), 'beta': 0.05 * jax.random.normal(ks[2], (D,), jnp.float32), 'Wr': 0.01 * jax.random.normal(ks[3], (D, E), jnp.float32), 'br': jnp.zeros((E,), jnp.float32), 'W1': s * jax.random.normal(ks[4], (E, D, H), jnp.float32), 'b1': s * jax.random.normal(ks[5], (E, H), jnp.float32), 'W2': s * jax.random.normal(ks[6], (E, H, DOUT), jnp.float32), 'b2': s * jax.random.normal(ks[7], (E, DOUT), jnp.float32)}
    _L0_ffn_all = _L0_ffn_setup()
    _L0_ffn_in = {k: v for k, v in _L0_ffn_all.items() if k in ('gamma', 'beta', 'Wr', 'br', 'W1', 'b1', 'W2', 'b2')}
    del _L0_ffn_all

    def _L1_gnn_setup():
        import jax, jax.numpy as jnp
        import numpy as np
        N, D, H = (4096, 128, 128)
        KEEP_RATIO = 0.5
        TEMP = 1.0
        COS_EPS = 0.0001
        NEG = -9000000000000000.0

        def _cos_normalize(x):
            n = jnp.linalg.norm(x, axis=-1, keepdims=True)
            return x / jnp.maximum(n, COS_EPS)
        key = jax.random.key(seed)
        k1, k2, k3, k4 = jax.random.split(key, 4)
        features = jax.random.normal(k1, (N, D), dtype=jnp.float32)
        adj = jax.random.randint(k2, (N, N), 0, 2, dtype=jnp.int32)
        Wq = jax.random.normal(k3, (H, D), dtype=jnp.float32) * 0.001
        Wk = jax.random.normal(k4, (H, D), dtype=jnp.float32) * 0.001
        return {'features': features, 'adj': adj, 'Wq': Wq, 'Wk': Wk}
    _L1_gnn_all = _L1_gnn_setup()
    _L1_gnn_in = {k: v for k, v in _L1_gnn_all.items() if k in ('Wq', 'Wk')}
    del _L1_gnn_all

    def _L1_ffn_setup():
        import jax, jax.numpy as jnp
        import numpy as np
        TOP_K = 2
        key = jax.random.key(seed)
        ks = jax.random.split(key, 4)
        B, L, D, H, E = (8, 2048, 128, 512, 8)
        s = 0.02
        return {'x': jax.random.normal(ks[0], (B, L, D), jnp.float32), 'Wg': jax.random.normal(ks[1], (D, E), jnp.float32) * s, 'bg': jnp.zeros((E,), jnp.float32), 'W1': jax.random.normal(ks[2], (E, D, H), jnp.float32) * s, 'b1': jnp.zeros((E, H), jnp.float32), 'W2': jax.random.normal(ks[3], (E, H, D), jnp.float32) * s, 'b2': jnp.zeros((E, D), jnp.float32)}
    _L1_ffn_all = _L1_ffn_setup()
    _L1_ffn_in = {k: v for k, v in _L1_ffn_all.items() if k in ('Wg', 'bg', 'W1', 'b1', 'W2', 'b2')}
    del _L1_ffn_all

    def _L2_gnn_setup():
        import jax, jax.numpy as jnp
        import numpy as np
        N, IN_DIM, OUT_DIM = (4096, 128, 128)
        NEG_INF = -1000000000.0
        key = jax.random.key(seed)
        k1, k2, k3, k4 = jax.random.split(key, 4)
        X = jax.random.normal(k1, (N, IN_DIM), dtype=jnp.float32)
        A = jax.random.randint(k2, (N, N), 0, 2).astype(jnp.int32)
        W_fc = jax.random.normal(k3, (IN_DIM, OUT_DIM), dtype=jnp.float32) * (1.0 / np.sqrt(IN_DIM))
        b_fc = jnp.zeros((OUT_DIM,), dtype=jnp.float32)
        w_att = jax.random.normal(k4, (2 * OUT_DIM,), dtype=jnp.float32) * (1.0 / np.sqrt(2 * OUT_DIM))
        b_att = jnp.zeros((), dtype=jnp.float32)
        return {'X': X, 'A': A, 'W_fc': W_fc, 'b_fc': b_fc, 'w_att': w_att, 'b_att': b_att}
    _L2_gnn_all = _L2_gnn_setup()
    _L2_gnn_in = {k: v for k, v in _L2_gnn_all.items() if k in ('W_fc', 'b_fc', 'w_att', 'b_att')}
    del _L2_gnn_all

    def _L2_ffn_setup():
        import jax, jax.numpy as jnp
        import numpy as np
        B, K, D = (256, 16, 128)
        E = 32
        H = int(D * 0.25)
        key = jax.random.key(seed)
        ks = jax.random.split(key, 7)
        d_rs = D ** (-0.5)
        h_rs = H ** (-0.5)
        x = jax.random.normal(ks[0], (B, K, D), dtype=jnp.float32)
        router_w = jax.random.uniform(ks[1], (E, D), jnp.float32, -d_rs, d_rs)
        router_b = jax.random.uniform(ks[2], (E,), jnp.float32, -d_rs, d_rs)
        W1 = jax.random.uniform(ks[3], (E, D, H), jnp.float32, -h_rs, h_rs)
        b1 = jax.random.uniform(ks[4], (E, H), jnp.float32, -h_rs, h_rs)
        W2 = jax.random.uniform(ks[5], (E, H, D), jnp.float32, -d_rs, d_rs)
        b2 = jax.random.uniform(ks[6], (E, D), jnp.float32, -d_rs, d_rs)
        return {'x': x, 'router_w': router_w, 'router_b': router_b, 'W1': W1, 'b1': b1, 'W2': W2, 'b2': b2}
    _L2_ffn_all = _L2_ffn_setup()
    _L2_ffn_in = {k: v for k, v in _L2_ffn_all.items() if k in ('router_w', 'router_b', 'W1', 'b1', 'W2', 'b2')}
    del _L2_ffn_all

    def _L3_gnn_setup():
        import jax, jax.numpy as jnp
        import numpy as np
        N, F = (4000, 128)
        NEG_SLOPE = 0.2
        key = jax.random.key(seed)
        k1, k2, k3, k4, k5, k6, k7 = jax.random.split(key, 7)
        node_embeddings = jax.random.normal(k1, (N, F), dtype=jnp.float32)
        adj_matrix = jax.random.randint(k2, (N, N), 0, 2, dtype=jnp.int32)
        s = 1.0 / np.sqrt(F)
        W_w = jax.random.uniform(k3, (F, F), dtype=jnp.float32, minval=-s, maxval=s)
        W_b = jax.random.uniform(k4, (F,), dtype=jnp.float32, minval=-s, maxval=s)
        s2 = 1.0 / np.sqrt(2 * F)
        a_src = jax.random.uniform(k5, (F,), dtype=jnp.float32, minval=-s2, maxval=s2)
        a_dst = jax.random.uniform(k6, (F,), dtype=jnp.float32, minval=-s2, maxval=s2)
        a_b = jax.random.uniform(k7, (), dtype=jnp.float32, minval=-s2, maxval=s2)
        return {'node_embeddings': node_embeddings, 'adj_matrix': adj_matrix, 'W_w': W_w, 'W_b': W_b, 'a_src': a_src, 'a_dst': a_dst, 'a_b': a_b}
    _L3_gnn_all = _L3_gnn_setup()
    _L3_gnn_in = {k: v for k, v in _L3_gnn_all.items() if k in ('W_w', 'W_b', 'a_src', 'a_dst', 'a_b')}
    del _L3_gnn_all

    def _L3_ffn_setup():
        import math
        import jax, jax.numpy as jnp
        import numpy as np
        CAPACITY_FACTOR = 1.25
        key = jax.random.key(seed)
        ks = jax.random.split(key, 5)
        B, L, D, F, E = (8, 4096, 128, 512, 8)
        h = jax.random.normal(ks[0], (B, L, D), dtype=jnp.float32)
        gate_w = jax.random.normal(ks[1], (D, E), dtype=jnp.float32) * 0.02
        gate_b = jnp.zeros((E,), dtype=jnp.float32)
        w1 = jax.random.normal(ks[2], (E, D, F), dtype=jnp.float32) * (1.0 / math.sqrt(D))
        b1 = jnp.zeros((E, F), dtype=jnp.float32)
        w2 = jax.random.normal(ks[3], (E, F, D), dtype=jnp.float32) * (1.0 / math.sqrt(F))
        b2 = jnp.zeros((E, D), dtype=jnp.float32)
        return {'h': h, 'gate_w': gate_w, 'gate_b': gate_b, 'w1': w1, 'b1': b1, 'w2': w2, 'b2': b2}
    _L3_ffn_all = _L3_ffn_setup()
    _L3_ffn_in = {k: v for k, v in _L3_ffn_all.items() if k in ('gate_w', 'gate_b', 'w1', 'b1', 'w2', 'b2')}
    del _L3_ffn_all
    return {'x': x, 'adj': adj, 'L0_gnn_W_w': _L0_gnn_in['W_w'], 'L0_gnn_W_b': _L0_gnn_in['W_b'], 'L0_gnn_a_w': _L0_gnn_in['a_w'], 'L0_gnn_a_b': _L0_gnn_in['a_b'], 'L0_ffn_gamma': _L0_ffn_in['gamma'], 'L0_ffn_beta': _L0_ffn_in['beta'], 'L0_ffn_Wr': _L0_ffn_in['Wr'], 'L0_ffn_br': _L0_ffn_in['br'], 'L0_ffn_W1': _L0_ffn_in['W1'], 'L0_ffn_b1': _L0_ffn_in['b1'], 'L0_ffn_W2': _L0_ffn_in['W2'], 'L0_ffn_b2': _L0_ffn_in['b2'], 'L1_gnn_Wq': _L1_gnn_in['Wq'], 'L1_gnn_Wk': _L1_gnn_in['Wk'], 'L1_ffn_Wg': _L1_ffn_in['Wg'], 'L1_ffn_bg': _L1_ffn_in['bg'], 'L1_ffn_W1': _L1_ffn_in['W1'], 'L1_ffn_b1': _L1_ffn_in['b1'], 'L1_ffn_W2': _L1_ffn_in['W2'], 'L1_ffn_b2': _L1_ffn_in['b2'], 'L2_gnn_W_fc': _L2_gnn_in['W_fc'], 'L2_gnn_b_fc': _L2_gnn_in['b_fc'], 'L2_gnn_w_att': _L2_gnn_in['w_att'], 'L2_gnn_b_att': _L2_gnn_in['b_att'], 'L2_ffn_router_w': _L2_ffn_in['router_w'], 'L2_ffn_router_b': _L2_ffn_in['router_b'], 'L2_ffn_W1': _L2_ffn_in['W1'], 'L2_ffn_b1': _L2_ffn_in['b1'], 'L2_ffn_W2': _L2_ffn_in['W2'], 'L2_ffn_b2': _L2_ffn_in['b2'], 'L3_gnn_W_w': _L3_gnn_in['W_w'], 'L3_gnn_W_b': _L3_gnn_in['W_b'], 'L3_gnn_a_src': _L3_gnn_in['a_src'], 'L3_gnn_a_dst': _L3_gnn_in['a_dst'], 'L3_gnn_a_b': _L3_gnn_in['a_b'], 'L3_ffn_gate_w': _L3_ffn_in['gate_w'], 'L3_ffn_gate_b': _L3_ffn_in['gate_b'], 'L3_ffn_w1': _L3_ffn_in['w1'], 'L3_ffn_b1': _L3_ffn_in['b1'], 'L3_ffn_w2': _L3_ffn_in['w2'], 'L3_ffn_b2': _L3_ffn_in['b2']}

def reference(x, adj, L0_gnn_W_w, L0_gnn_W_b, L0_gnn_a_w, L0_gnn_a_b, L0_ffn_gamma, L0_ffn_beta, L0_ffn_Wr, L0_ffn_br, L0_ffn_W1, L0_ffn_b1, L0_ffn_W2, L0_ffn_b2, L1_gnn_Wq, L1_gnn_Wk, L1_ffn_Wg, L1_ffn_bg, L1_ffn_W1, L1_ffn_b1, L1_ffn_W2, L1_ffn_b2, L2_gnn_W_fc, L2_gnn_b_fc, L2_gnn_w_att, L2_gnn_b_att, L2_ffn_router_w, L2_ffn_router_b, L2_ffn_W1, L2_ffn_b1, L2_ffn_W2, L2_ffn_b2, L3_gnn_W_w, L3_gnn_W_b, L3_gnn_a_src, L3_gnn_a_dst, L3_gnn_a_b, L3_ffn_gate_w, L3_ffn_gate_b, L3_ffn_w1, L3_ffn_b1, L3_ffn_w2, L3_ffn_b2):
    import jax
    import jax.numpy as jnp

    def _L0_gnn_ref(node_features, adjacency_matrix, W_w, W_b, a_w, a_b):
        import jax, jax.numpy as jnp
        import numpy as np
        N, IN_C, OUT_C, H = (2048, 128, 128, 8)
        HD = OUT_C // H
        n = node_features.shape[0]
        h = node_features @ W_w.T + W_b
        h_heads = h.reshape(n, H, HD)
        w_src = a_w[0, :HD]
        w_dst = a_w[0, HD:]
        s_src = jnp.einsum('nhd,d->hn', h_heads, w_src)
        s_dst = jnp.einsum('nhd,d->hn', h_heads, w_dst)
        scores = s_src[:, :, None] + s_dst[:, None, :] + a_b[0]
        scores = jax.nn.leaky_relu(scores, negative_slope=0.2)
        scores = jnp.where(adjacency_matrix[None, :, :] == 0, jnp.float32(-1000000000.0), scores)
        attn = jax.nn.softmax(scores, axis=-1)
        h_agg = jnp.einsum('hij,jhd->ihd', attn, h_heads)
        h_out = h_agg.reshape(n, OUT_C)
        h_out = h_out + node_features
        return jax.nn.elu(h_out)

    def _L0_ffn_ref(x, gamma, beta, Wr, br, W1, b1, W2, b2):
        import jax, jax.numpy as jnp
        import numpy as np
        E = 8
        K = 2
        D = 128
        H = 256
        DOUT = 128
        EPS = 1e-05
        mu = jnp.mean(x, axis=-1, keepdims=True)
        var = jnp.mean(jnp.square(x - mu), axis=-1, keepdims=True)
        xn = (x - mu) * jax.lax.rsqrt(var + EPS) * gamma + beta
        logits = jnp.einsum('bsd,de->bse', xn, Wr) + br
        top_vals, top_idx = jax.lax.top_k(logits, K)
        w = jax.nn.softmax(top_vals, axis=-1)
        w_full = jnp.einsum('bsk,bske->bse', w, jax.nn.one_hot(top_idx, E, dtype=w.dtype))
        y = jnp.zeros(x.shape[:-1] + (DOUT,), x.dtype)
        for e in range(E):
            h = jax.nn.gelu(jnp.einsum('bsd,dh->bsh', xn, W1[e]) + b1[e], approximate=False)
            y_e = jnp.einsum('bsh,hd->bsd', h, W2[e]) + b2[e]
            y = y + y_e * w_full[..., e, None]
        return y

    def _L1_gnn_ref(features, adj, Wq, Wk):
        import jax, jax.numpy as jnp
        import numpy as np
        N, D, H = (4096, 128, 128)
        KEEP_RATIO = 0.5
        TEMP = 1.0
        COS_EPS = 0.0001
        NEG = -9000000000000000.0

        def _cos_normalize(x):
            n = jnp.linalg.norm(x, axis=-1, keepdims=True)
            return x / jnp.maximum(n, COS_EPS)
        Qn = _cos_normalize(features @ Wq.T)
        Kn = _cos_normalize(features @ Wk.T)
        raw_att = Kn @ Qn.T
        att = jnp.where(adj > 0, raw_att, NEG) * TEMP
        att = jax.nn.softmax(att, axis=1)
        prop_fea = att @ features
        adj_mask = (jnp.sum(adj, axis=1) > 0).astype(features.dtype)[:, None]
        prop_fea = adj_mask * prop_fea + (1.0 - adj_mask) * features
        return (1.0 - KEEP_RATIO) * prop_fea + KEEP_RATIO * features

    def _L1_ffn_ref(x, Wg, bg, W1, b1, W2, b2):
        import jax, jax.numpy as jnp
        import numpy as np
        TOP_K = 2
        B, L, D = x.shape
        E = W1.shape[0]
        xf = x.reshape(-1, D)
        gate_logits = xf @ Wg + bg
        top_w, top_i = jax.lax.top_k(gate_logits, TOP_K)
        top_w = jax.nn.softmax(top_w, axis=-1)
        w_dense = jnp.sum(jax.nn.one_hot(top_i, E, dtype=xf.dtype) * top_w[..., None], axis=1)
        out = jnp.zeros_like(xf)
        for e in range(E):
            h = jax.nn.gelu(xf @ W1[e] + b1[e], approximate=False)
            out = out + w_dense[:, e:e + 1] * (h @ W2[e] + b2[e])
        return out.reshape(B, L, D)

    def _L2_gnn_ref(X, A, W_fc, b_fc, w_att, b_att):
        import jax, jax.numpy as jnp
        import numpy as np
        N, IN_DIM, OUT_DIM = (4096, 128, 128)
        NEG_INF = -1000000000.0
        H = X @ W_fc + b_fc
        d = H.shape[1]
        s_src = H @ w_att[:d]
        s_dst = H @ w_att[d:]
        scores = s_src[:, None] + s_dst[None, :] + b_att
        scores = jnp.where(A > 0, scores, jnp.float32(NEG_INF))
        alpha = jax.nn.softmax(scores, axis=1)
        return alpha @ H

    def _L2_ffn_ref(x, router_w, router_b, W1, b1, W2, b2):
        import jax, jax.numpy as jnp
        import numpy as np
        B, K, D = (256, 16, 128)
        E = 32
        H = int(D * 0.25)
        xf = x.reshape(-1, D)
        logits = xf @ router_w.T + router_b
        idx = jnp.argmax(logits, axis=-1)
        w1t = jnp.take(W1, idx, axis=0)
        h = jnp.einsum('nd,ndh->nh', xf, w1t) + jnp.take(b1, idx, axis=0)
        h = jax.nn.relu(h)
        w2t = jnp.take(W2, idx, axis=0)
        out = jnp.einsum('nh,nhd->nd', h, w2t) + jnp.take(b2, idx, axis=0)
        out = jax.nn.relu(out)
        return out.reshape(x.shape)

    def _L3_gnn_ref(node_embeddings, adj_matrix, W_w, W_b, a_src, a_dst, a_b):
        import jax, jax.numpy as jnp
        import numpy as np
        N, F = (4000, 128)
        NEG_SLOPE = 0.2
        H = node_embeddings @ W_w.T + W_b
        e = (H @ a_src)[:, None] + (H @ a_dst)[None, :] + a_b
        e = jnp.where(adj_matrix == 0, -jnp.inf, e)
        e = jnp.where(e >= 0, e, NEG_SLOPE * e)
        attn = jax.nn.softmax(e, axis=1)
        return attn @ H

    def _L3_ffn_ref(h, gate_w, gate_b, w1, b1, w2, b2):
        import math
        import jax, jax.numpy as jnp
        import numpy as np
        CAPACITY_FACTOR = 1.25
        B, L, D = h.shape
        E = gate_w.shape[1]
        T = B * L
        C = max(1, math.ceil(CAPACITY_FACTOR * T / E))
        x = h.reshape(T, D)
        logits = x @ gate_w + gate_b
        probs = jax.nn.softmax(logits, axis=-1)
        idx = jnp.argmax(probs, axis=-1)
        prb = jnp.take_along_axis(probs, idx[:, None], axis=1)[:, 0]
        one_hot = jax.nn.one_hot(idx, E, dtype=jnp.float32)
        pos = (jnp.cumsum(one_hot, axis=0) * one_hot).sum(-1).astype(jnp.int32) - 1
        kept = pos < C
        pos_safe = jnp.where(kept, pos, C)
        buf = jnp.zeros((E, C, D), dtype=h.dtype).at[idx, pos_safe].set(x, mode='drop')
        hmid = jax.nn.relu(jnp.einsum('ecd,edf->ecf', buf, w1) + b1[:, None, :])
        ybuf = jnp.einsum('ecf,efd->ecd', hmid, w2) + b2[:, None, :]
        pos_g = jnp.minimum(pos, C - 1)
        y_tok = ybuf[idx, pos_g] * (prb * kept)[:, None]
        y = y_tok.reshape(B, L, D)
        y = jnp.nan_to_num(y, nan=0.0, posinf=10000.0, neginf=-10000.0)
        return y
    x = x + _L0_gnn_ref(_layernorm(x, axis=-1), adj, L0_gnn_W_w, L0_gnn_W_b, L0_gnn_a_w, L0_gnn_a_b)
    x = x + _L0_ffn_ref(_layernorm(x, axis=-1)[None], L0_ffn_gamma, L0_ffn_beta, L0_ffn_Wr, L0_ffn_br, L0_ffn_W1, L0_ffn_b1, L0_ffn_W2, L0_ffn_b2)[0]
    x = x + _L1_gnn_ref(_layernorm(x, axis=-1), adj, L1_gnn_Wq, L1_gnn_Wk)
    x = x + _L1_ffn_ref(_layernorm(x, axis=-1)[None], L1_ffn_Wg, L1_ffn_bg, L1_ffn_W1, L1_ffn_b1, L1_ffn_W2, L1_ffn_b2)[0]
    x = x + _L2_gnn_ref(_layernorm(x, axis=-1), adj, L2_gnn_W_fc, L2_gnn_b_fc, L2_gnn_w_att, L2_gnn_b_att)
    x = x + _L2_ffn_ref(_layernorm(x, axis=-1)[None], L2_ffn_router_w, L2_ffn_router_b, L2_ffn_W1, L2_ffn_b1, L2_ffn_W2, L2_ffn_b2)[0]
    x = x + _L3_gnn_ref(_layernorm(x, axis=-1), adj, L3_gnn_W_w, L3_gnn_W_b, L3_gnn_a_src, L3_gnn_a_dst, L3_gnn_a_b)
    x = x + _L3_ffn_ref(_layernorm(x, axis=-1)[None], L3_ffn_gate_w, L3_ffn_gate_b, L3_ffn_w1, L3_ffn_b1, L3_ffn_w2, L3_ffn_b2)[0]
    return x

_drawn_inputs = setup_inputs


def setup_inputs(seed=0):
    import zlib

    import numpy as np

    out = dict(_drawn_inputs(seed))
    spreads = {'L0_ffn_br': (0.0, 0.346),
     'L1_ffn_bg': (0.0, 0.295),
     'L1_ffn_b1': (0.0, 0.6),
     'L1_ffn_b2': (0.0, 0.38),
     'L2_gnn_b_fc': (0.0, 0.291),
     'L3_ffn_gate_b': (0.0, 0.1),
     'L3_ffn_b1': (0.0, 2.0),
     'L3_ffn_b2': (0.0, 2.0)}
    factors = {'L0_gnn_W_b': 5.706,
     'L0_ffn_gamma': 8.0,
     'L0_ffn_beta': 8.0,
     'L0_ffn_Wr': 4.438,
     'L0_ffn_W1': 3.099,
     'L0_ffn_b1': 8.0,
     'L0_ffn_W2': 2.95,
     'L0_ffn_b2': 4.162,
     'L1_gnn_Wq': 53.128,
     'L1_gnn_Wk': 52.528,
     'L1_ffn_W1': 2.905,
     'L1_ffn_W2': 2.686,
     'L2_ffn_b1': 8.0,
     'L2_ffn_b2': 3.647,
     'L3_gnn_a_src': 29.042,
     'L3_gnn_a_dst': 3.636,
     'L2_ffn_router_b': 3.103,
     'L3_gnn_W_b': 4.45}
    for name, (base, spread) in spreads.items():
        noise = np.random.default_rng([zlib.crc32(name.encode()), seed]).standard_normal(out[name].shape)
        drawn = base * np.exp(spread * noise) if base else spread * noise
        out[name] = jnp.asarray(drawn.astype(out[name].dtype))
    for name, factor in factors.items():
        out[name] = (out[name] * factor).astype(out[name].dtype)
    return out
```

```python
import math
from contextlib import ExitStack

import numpy as np
import concourse.bass as bass
from concourse import mybir

F32 = mybir.dt.float32
BF16 = mybir.dt.bfloat16
FP8 = mybir.dt.float8e4
U8 = mybir.dt.uint8
U16 = mybir.dt.uint16
U32 = mybir.dt.uint32
I32 = mybir.dt.int32
ALU = mybir.AluOpType
ACT = mybir.ActivationFunctionType
AX = mybir.AxisListType

N = 3327
P = 128
T = 26
NP = T * P
HALF = T // 2
HN = HALF * P
LN_EPS = 1e-5
ONE8 = 56
TINY = 1e-30
HEADS, HD = 8, 16
HC = HD + 1
BIG = 2.0 ** 100
SLOPE = 0.2
CAPACITY = math.ceil(1.25 * N / 8)


STAGE_SEMS = 24
RETIRED = []


class Link:

    def __init__(self, eng, sem):
        self.eng, self.sem, self.n = eng, sem, 0

    def __call__(self, ins, base=0):
        self.n += 1
        ins.then_inc(self.sem, 1)
        self.eng.wait_ge(self.sem, base + self.n)

    def skip(self, n):
        self.n += n


class Core:
    pass


def bcast_mid(ap, n):
    return ap.unsqueeze(1).to_broadcast([ap.shape[0], n, ap.shape[1]])


def bcast_last(ap, n):
    return ap.unsqueeze(2).to_broadcast([ap.shape[0], ap.shape[1], n])


def open_stage(nc, name):
    ctx = ExitStack()
    if len(nc.free_semaphores) < STAGE_SEMS:
        nc.clear_and_free_semaphores(RETIRED)
        RETIRED.clear()
        nc.all_engine_barrier()

    def sb(n, shape, dt):
        return ctx.enter_context(nc.sbuf_tensor(f"{name}_{n}", shape, dt))

    def sem(n):
        RETIRED.append(nc.alloc_semaphore(f"{name}_{n}"))
        return RETIRED[-1]

    return ctx, sb, sem


def setup_stage(nc, K, A):
    ctx, sb, sem = open_stage(nc, "setup")
    with ctx:
        SEL0 = sb("sel0", [P, 16], F32)
        W0 = sb("w0", [P, P], F32)
        WT2 = sb("wt2", [P, P], F32)
        DST2 = sb("dst2", [P, 1], F32)
        W3 = sb("w3", [P, P], F32)
        A3 = sb("a3", [P, 2], F32)
        BC = sb("bc", [P, 3], F32)
        BW = sb("bw", [P, 3, P], F32)
        AB = sb("ab", [P, 2], F32)
        loaded, cols, consts, products = sem("loaded"), sem("cols"), sem("consts"), sem("products")
        loads = [
            (K.X[:], A["x"]),
            (K.WP0[:, 0:P], A["w0t"]), (W0[:], A["w0"]), (SEL0[:], A["sel0"]),
            (K.WP1[:], A["wqk"]),
            (K.WP2[:, 0:P], A["w2"]), (WT2[:], A["w2t"]), (DST2[:], A["dst2"]),
            (K.WP3[:, 0:P], A["w3t"]), (W3[:], A["w3"]), (A3[:], A["a3"]),
            (BC[:], A["bcols"]),
            (K.BP0[:, 0:P], A["b0"].partition_broadcast(P)),
            (K.BP2[:, 0:P], A["b2"].partition_broadcast(P)),
            (K.BP3[:, 0:P], A["b3"].partition_broadcast(P)),
            (AB[:], A["ab"].partition_broadcast(P)),
            (K.R[:], A["routers"]),
            (K.BR[:], A["router_b"].partition_broadcast(P)),
            (K.GB[:], A["gamma_beta"]),
        ]
        n_loads = 16 * len(loads)
        with nc.Block() as block:

            @block.scalar
            def _(act):
                for dst, src in loads:
                    act.dma_start(dst, src).then_inc(loaded, 16)
                act.wait_ge(loaded, n_loads)
                for k in range(3):
                    nc.scalar.activation(BW[:, k, :], BC[:, k:k + 1].to_broadcast([P, P]), ACT.Copy)\
                        .then_inc(cols, 1)

            @block.gpsimd
            def _(pool):
                nc.gpsimd.memset(K.ONES[:], 1.0).then_inc(consts, 1)
                nc.gpsimd.memset(K.IDENT[:], 0.0).then_inc(consts, 1)
                nc.gpsimd.memset(K.XT[:, NP:NP + 2 * P], 0.0).then_inc(consts, 1)
                nc.gpsimd.memset(K.NEG_HALF[:], -0.5).then_inc(consts, 1)
                nc.gpsimd.iota(K.IOTA[:], pattern=[[1, 32]], base=0, channel_multiplier=0,
                               allow_small_or_imprecise_dtypes=True).then_inc(consts, 1)
                pool.wait_ge(consts, 5)
                nc.gpsimd.affine_select(out=K.IDENT[:], in_=K.IDENT[:], compare_op=ALU.not_equal, fill=1.0,
                                        base=0, pattern=[[-1, P]], channel_multiplier=1).then_inc(consts, 1)
                nc.gpsimd.affine_select(out=K.LOWER[:], in_=K.ONES[:], compare_op=ALU.is_ge, fill=0.0,
                                        base=0, pattern=[[1, P]], channel_multiplier=-1).then_inc(consts, 1)
                nc.gpsimd.memset(K.COMB[:], 0.0).then_inc(consts, 1)
                pool.wait_ge(consts, 8)
                for k in range(2):
                    for s in range(3):
                        nc.gpsimd.affine_select(
                            out=K.COMB[:, k * HC:(k + 1) * HC], in_=K.COMB[:, k * HC:(k + 1) * HC],
                            compare_op=ALU.not_equal, fill=1.0, base=-(3 * HC * k + HC * s),
                            pattern=[[-1, HC]], channel_multiplier=1).then_inc(consts, 1)
                        pool.wait_ge(consts, 9 + 3 * k + s)

            @block.tensor
            def _(pe):
                pe.wait_ge(loaded, n_loads)
                nc.tensor.matmul(K.PS[:, 0, 0:16], W0[:], SEL0[:], start=True, stop=True)
                nc.tensor.matmul(K.PS[:, 1, 0:1], WT2[:], DST2[:], start=True, stop=True)
                nc.tensor.matmul(K.PS[:, 2, 0:2], W3[:], A3[:], start=True, stop=True)
                pe.wait_ge(cols, 3)
                nc.tensor.matmul(K.PS[:, 3, 0:16], BW[:, 0, :], SEL0[:], start=True, stop=True)
                nc.tensor.matmul(K.PS[:, 4, 0:1], BW[:, 1, :], DST2[:], start=True, stop=True)
                nc.tensor.matmul(K.PS[:, 5, 0:2], BW[:, 2, :], A3[:], start=True, stop=True)
                nc.tensor.matmul(K.PS[0:HEADS, 6, 0:1], SEL0[:, 0:HEADS], BC[:, 0:1], start=True, stop=True)\
                    .then_inc(products, 1)

            @block.vector
            def _(v):
                v.wait_ge(loaded, n_loads)
                v.wait_ge(products, 1)
                nc.vector.tensor_copy(K.WP0[:, P:P + 16], K.PS[:, 0, 0:16])
                nc.vector.tensor_copy(K.WP2[:, P:P + 1], K.PS[:, 1, 0:1])
                nc.vector.tensor_copy(K.WP3[:, P:P + 2], K.PS[:, 2, 0:2])
                nc.vector.tensor_scalar(K.BP0[:, P:P + 8], K.PS[:, 3, 0:8], AB[:, 0:1], None, ALU.add)
                nc.vector.tensor_copy(K.BP0[:, P + 8:P + 16], K.PS[:, 3, 8:16])
                nc.vector.tensor_copy(K.BP2[:, P:P + 1], K.PS[:, 4, 0:1])
                nc.vector.tensor_scalar(K.BP3[:, P:P + 1], K.PS[:, 5, 0:1], AB[:, 1:2], None, ALU.add)
                nc.vector.tensor_copy(K.BP3[:, P + 1:P + 2], K.PS[:, 5, 1:2])
                nc.vector.tensor_scalar(K.SB8[:], K.PS[0:HEADS, 6, 0:1], AB[0:HEADS, 0:1], None, ALU.add)


def norm_project_stage(nc, K, name, W, n, per, dest, bias=None, twice=False, affine=False, row=None,
                       loads=()):
    ctx, sb, sem = open_stage(nc, name)
    with ctx:
        ST = sb("stats", [P, T, 6], F32)
        M = sb("moments", [P, 6, T], F32)
        var_ready, rstd_ready, normed = sem("var_ready"), sem("rstd_ready"), sem("normed")
        transposed, xt_ready = sem("transposed"), sem("xt_ready")
        projected, taken, dve = sem("projected"), sem("taken"), sem("dve")
        loaded = sem("loaded")
        row_done, row_taken, row_stored = sem("row_done"), sem("row_taken"), sem("row_stored")
        passes = 2 if twice else 1
        tgroups = [(t, min(4, T - t)) for t in range(0, T, 4)]
        pgroups = [(t, min(per, T - t)) for t in range(0, T, per)]
        with nc.Block() as block:

            @block.vector
            def _(v):
                link = Link(v, dve)
                src = K.X
                for rnd in range(passes):
                    with v.Fori(0, T) as t:
                        nc.vector.bn_stats(ST[:, bass.ds(t, 1), :].rearrange("p a b -> p (a b)"),
                                           src[:, bass.ds(t, 1), :].rearrange("p a b -> p (a b)")).then_inc(dve, 1)
                    link.skip(T)
                    v.wait_ge(dve, link.n)
                    link(nc.vector.tensor_tensor(M[:, 0, :], ST[:, :, 1], ST[:, :, 4], ALU.add))
                    link(nc.vector.tensor_tensor(M[:, 1, :], ST[:, :, 1], ST[:, :, 4], ALU.subtract))
                    link(nc.vector.tensor_tensor(M[:, 2, :], ST[:, :, 2], ST[:, :, 5], ALU.add))
                    link(nc.vector.tensor_tensor(M[:, 3, :], M[:, 1, :], M[:, 1, :], ALU.mult))
                    link(nc.vector.scalar_tensor_tensor(M[:, 2, :], M[:, 3, :], P / 4.0, M[:, 2, :], ALU.mult, ALU.add))
                    nc.vector.tensor_scalar(M[:, 4, :], M[:, 2, :], 1.0 / P, LN_EPS, ALU.mult, ALU.add)\
                        .then_inc(var_ready, 1)
                    link(nc.vector.tensor_scalar(M[:, 0, :], M[:, 0, :], 0.5, None, ALU.mult))
                    for h in range(2):
                        ts = slice(HALF * h, HALF * (h + 1))
                        link(nc.vector.tensor_tensor(K.XN[:, ts, :], src[:, ts, :], bcast_last(M[:, 0, ts], P),
                                                     ALU.subtract))
                        if h == 0:
                            v.wait_ge(rstd_ready, rnd + 1)
                        last = nc.vector.tensor_tensor(K.XN[:, ts, :], K.XN[:, ts, :], bcast_last(M[:, 5, ts], P),
                                                       ALU.mult)
                        if rnd == passes - 1:
                            last.then_inc(normed, 1)
                        else:
                            link(last)
                    src = K.XN
                for g, (t, k) in enumerate(pgroups):
                    v.wait_ge(projected, g + 1)
                    ps = K.PS[:, 4 + g % 4, 0:k * n].rearrange("p (k n) -> p k n", n=n)
                    if bias is None:
                        nc.vector.tensor_copy(dest(t, k), ps).then_inc(taken, 1)
                    else:
                        nc.vector.tensor_tensor(dest(t, k), ps, bcast_mid(bias, k), ALU.add).then_inc(taken, 1)

            @block.sync
            def _(sp):
                for dst, src in loads:
                    sp.dma_start(dst, src).then_inc(loaded, 16)
                if loads:
                    sp.wait_ge(loaded, 16 * len(loads))
                if row is not None:
                    sp.wait_ge(row_taken, len(tgroups))
                    sp.dma_start(row[3], row[2]).then_inc(row_stored, 16)
                    sp.wait_ge(row_stored, 16)

            @block.gpsimd
            def _(pool):
                for rnd in range(passes):
                    pool.wait_ge(var_ready, rnd + 1)
                    nc.gpsimd.tensor_tensor(M[:, 5, :], M[:, 4, :], K.NEG_HALF[:], ALU.pow).then_inc(rstd_ready, 1)

            @block.tensor
            def _(pe):
                for g, (t, k) in enumerate(tgroups):
                    pe.wait_ge(normed, 1 if t + k <= HALF else 2)
                    if g >= 4:
                        pe.wait_ge(xt_ready, g - 3)
                    for j in range(k):
                        last = nc.tensor.transpose(K.PS[:, g % 4, j * P:(j + 1) * P], K.XN[:, t + j, :], K.IDENT[:])
                    last.then_inc(transposed, 1)
                for g, (t, k) in enumerate(pgroups):
                    pe.wait_ge(xt_ready, (t + k - 1) // 4 + 1)
                    if g >= 4:
                        pe.wait_ge(taken, g - 3)
                    for j in range(k):
                        last = nc.tensor.matmul(K.PS[:, 4 + g % 4, j * n:(j + 1) * n], K.XT[:, (t + j) * P:(t + j + 1) * P],
                                                W, start=True, stop=True)
                    last.then_inc(projected, 1)
                if row is not None:
                    m = row[0].shape[1]
                    for g, (t, k) in enumerate(tgroups):
                        pe.wait_ge(xt_ready, len(tgroups))
                        if g >= 4:
                            pe.wait_ge(row_taken, g - 3)
                        nc.tensor.matmul(K.PS[0:m, g % 4, 0:k * P], row[0], K.XT[:, t * P:(t + k) * P],
                                         start=True, stop=True).then_inc(row_done, 1)

            @block.scalar
            def _(act):
                for g, (t, k) in enumerate(tgroups):
                    act.wait_ge(transposed, g + 1)
                    out, ps = K.XT[:, t * P:(t + k) * P], K.PS[:, g % 4, 0:k * P]
                    if affine:
                        nc.scalar.activation(out, ps, ACT.Identity, bias=K.GB[:, 1:2], scale=K.GB[:, 0:1])\
                            .then_inc(xt_ready, 1)
                    else:
                        nc.scalar.activation(out, ps, ACT.Copy).then_inc(xt_ready, 1)
                if row is not None:
                    m = row[0].shape[1]
                    for g, (t, k) in enumerate(tgroups):
                        act.wait_ge(row_done, g + 1)
                        nc.scalar.activation(row[2][0:m, t * P:(t + k) * P], K.PS[0:m, g % 4, 0:k * P], ACT.Identity,
                                             bias=row[1], scale=1.0).then_inc(row_taken, 1)


def global_max(nc, eng_link, v, pe_done, ready, d, n, K, tmp):
    link = eng_link
    nc.vector.tensor_reduce(tmp.PM[:, 0:n], d, AX.X, ALU.max).then_inc(ready, 1)
    v.wait_ge(pe_done, 1)
    link(nc.vector.tensor_reduce(tmp.G8[0:n, :], K.PS[0:n, 0, 0:P], AX.X, ALU.max))
    nc.vector.tensor_scalar(tmp.DG[0:n, 0:n], K.IDENT[0:n, 0:n], tmp.G8[0:n, 0:1], None, ALU.mult).then_inc(ready, 1)
    v.wait_ge(pe_done, 2)
    link(nc.vector.tensor_copy(tmp.GB[:, 0:n], K.PS[:, 1, 0:n]))


def global_max_products(nc, pe, pe_done, ready, n, K, tmp):
    pe.wait_ge(ready, 1)
    nc.tensor.transpose(K.PS[0:n, 0, 0:P], tmp.PM[:, 0:n], K.IDENT[:]).then_inc(pe_done, 1)
    pe.wait_ge(ready, 2)
    nc.tensor.matmul(K.PS[:, 1, 0:n], K.ONES[0:n, :], tmp.DG[0:n, 0:n], start=True, stop=True).then_inc(pe_done, 1)


def max_buffers(sb, n):
    tmp = Core()
    tmp.PM, tmp.G8 = sb("pm", [P, n], F32), sb("g8", [n, 1], F32)
    tmp.DG, tmp.GB = sb("dg", [n, n], F32), sb("gb", [P, n], F32)
    return tmp


def split_stage(nc, K, name, HP, heads, hd, score_col, sets, XS, V, coef=None, keep=None, store=None):
    ctx, sb, sem = open_stage(nc, name)
    with ctx:
        tmp = max_buffers(sb, heads)
        DM = sb("dm", [P, heads, T], F32)
        EX = sb("ex", [P, len(sets), T, heads], F32)
        Y = sb("y", [P, 4, T, heads], F32) if coef else None
        ready, pe_done, dve = sem("ready"), sem("pe_done"), sem("dve")
        dm_ready, ex_ready, y_ready, coef_ready = sem("dm_ready"), sem("ex_ready"), sem("y_ready"), sem("coef_ready")
        v_ready, part_ready, stored = sem("v_ready"), sem("part_ready"), sem("stored")
        H4 = HP[:, :, 0:heads * hd].rearrange("p t (h c) -> p t h c", c=hd)
        D = HP[:, :, score_col:score_col + heads]
        with nc.Block() as block:

            @block.sync
            def _(sp):
                if store is not None:
                    sp.dma_start(*store).then_inc(stored, 16)
                    sp.wait_ge(stored, 16)

            @block.tensor
            def _(pe):
                global_max_products(nc, pe, pe_done, ready, heads, K, tmp)

            @block.vector
            def _(v):
                link = Link(v, dve)
                global_max(nc, link, v, pe_done, ready, D.rearrange("p t h -> p h t"), heads, K, tmp)
                nc.vector.tensor_tensor(DM[:].rearrange("p h t -> p t h"), D, bcast_mid(tmp.GB[:, 0:heads], T),
                                        ALU.subtract).then_inc(dm_ready, 1)
                if coef:
                    S = HP[:, :, score_col - heads:score_col]
                    link(nc.vector.tensor_tensor(Y[:, 0], S, bcast_mid(tmp.GB[:, 0:heads], T), ALU.add))
                    link(nc.vector.scalar_tensor_tensor(Y[:, 1], Y[:, 0], SLOPE, Y[:, 0], ALU.mult, ALU.max))
                    link(nc.vector.tensor_tensor(Y[:, 2], Y[:, 0], Y[:, 1], ALU.subtract))
                    nc.vector.scalar_tensor_tensor(Y[:, 3], Y[:, 0], SLOPE, Y[:, 1], ALU.mult, ALU.subtract)\
                        .then_inc(y_ready, 1)
                if keep is not None:
                    nc.vector.tensor_copy(keep[:], D)
                for k in range(len(sets)):
                    v.wait_ge(ex_ready, k + 1)
                    if k:
                        v.wait_ge(part_ready, 3 * k)
                    nc.vector.tensor_tensor(V[:, :, :, 0:hd], H4, bcast_last(EX[:, k].rearrange("p t h -> p (t h)"), hd)
                                            .rearrange("p (t h) c -> p t h c", t=T), ALU.mult)
                    link(nc.vector.tensor_copy(V[:, :, :, hd], EX[:, k]))
                    nc.vector.sem_inc(v_ready, 1)
                    for part in range(2):
                        v.wait_ge(part_ready, 3 * k + part + 1)
                        nc.vector.tensor_tensor(V, V, XS[k](part), ALU.subtract).then_inc(v_ready, 1)

            @block.scalar
            def _(act):
                act.wait_ge(dm_ready, 1)
                for k, slope in enumerate(sets):
                    nc.scalar.activation(EX[:, k], DM[:].rearrange("p h t -> p t h"), ACT.Exp, scale=slope)\
                        .then_inc(ex_ready, 1)
                if coef:
                    act.wait_ge(y_ready, 1)
                    nc.scalar.activation(coef[0], Y[:, 2].rearrange("p (a t) h -> p a t h", a=2), ACT.Exp)
                    nc.scalar.activation(coef[1], Y[:, 3].rearrange("p (a t) h -> p a t h", a=2), ACT.Exp)
                for k in range(len(sets)):
                    for part in range(3):
                        act.wait_ge(v_ready, 3 * k + part + 1)
                        nc.scalar.activation(XS[k](part), V, ACT.Copy).then_inc(part_ready, 1)


def edge_sum_stage(nc, K, name, moving, n, finish, links, bufs=None, adj=None, landing=None):
    ctx, sb, sem = open_stage(nc, name)
    with ctx:
        adj_in, edges_made = [sem("adj_in0"), sem("adj_in1")], sem("edges_made")
        ED = sb("edges", [P, 2, T, P], U8)
        TMP = bufs(sb) if bufs else None
        staged, summed, sum_free, dve = sem("staged"), sem("summed"), sem("sum_free"), sem("dve")
        passed = sem("passed")
        with nc.Block() as block:

            @block.sync
            def _(sp):
                if adj is not None:
                    with sp.Fori(0, T // 2) as t:
                        for q in range(2):
                            sp.wait_ge(edges_made, 2 * t + q + 1)
                            sp.dma_start(landing[q], adj[bass.ds(2 * t + q, 1), :, :]
                                         .rearrange("a p (b i) -> p (a b) i", i=P)).then_inc(adj_in[q], 16)

            @block.scalar
            def _(act):
                with act.Fori(0, T // 2) as t:
                    for q in range(2):
                        if adj is not None:
                            act.wait_ge(edges_made, 2 * t + q + 3)
                        act.wait_ge(summed, 2 * t + q + 1)
                        nc.scalar.activation(
                            ED[:, q].rearrange("p b i -> p (b i)").bitcast(U16),
                            K.EDGE[:, bass.ds(2 * t + q, 1)].rearrange("p a b i -> p (a b i)").bitcast(U16),
                            ACT.Copy).then_inc(staged, 1)

            @block.tensor
            def _(pe):
                with pe.Fori(0, T // 2) as t:
                    for q in range(2):
                        pe.wait_ge(staged, 2 * t + q + 1)
                        pe.wait_ge(sum_free, 2 * t + q + 1)
                        pe.sem_inc(passed, 1)
                        for j in range(T):
                            last = nc.tensor.matmul(K.PS[:, q, 0:n], ED[:, q, j, :].bitcast(FP8), moving(j),
                                                    start=(j == 0), stop=(j == T - 1))
                        last.then_inc(summed, 1)

            @block.vector
            def _(v):
                link = Link(v, dve)
                v.sem_inc(sum_free, 2)
                v.sem_inc(summed, 2)
                v.sem_inc(edges_made, 2)

                def make_edges(it, q, loads):
                    v.wait_ge(adj_in[q], loads)
                    nc.vector.tensor_scalar(K.EDGE[:, bass.ds(it, 1), :, :].rearrange("p a b i -> p (a b i)"),
                                            landing[q].rearrange("p b i -> p (b i)"),
                                            float(ONE8), None, ALU.mult).then_inc(edges_made, 1)

                if adj is not None:
                    make_edges(0, 0, 16)
                    with v.Fori(0, T // 2 - 1) as t:
                        for q in range(2):
                            make_edges(2 * t + q + 1, 1 - q, 16 * t + 16 * q + 16)
                            v.wait_ge(summed, 2 * t + q + 3)
                            v.wait_ge(sum_free, 2 * t + q + 2)
                            finish(v, link, 2 * t + q, K.PS[:, q, 0:n], 2 * links * t, sum_free, TMP)
                    make_edges(T - 1, 1, 8 * T)
                    for q in range(2):
                        v.wait_ge(summed, T - 2 + q + 3)
                        v.wait_ge(sum_free, T - 2 + q + 2)
                        finish(v, link, T - 2 + q, K.PS[:, q, 0:n], 0, sum_free, TMP)
                    return
                with v.Fori(0, T // 2) as t:
                    for q in range(2):
                        v.wait_ge(summed, 2 * t + q + 3)
                        v.wait_ge(sum_free, 2 * t + q + 2)
                        finish(v, link, 2 * t + q, K.PS[:, q, 0:n], 2 * links * t, sum_free, TMP)
                link.skip(2 * links * (T // 2 - 1))


def heads_out_stage(nc, K, XALL, XD):
    ctx, sb, sem = open_stage(nc, "heads_out")
    with ctx:
        stored = sem("stored")
        with nc.Block() as block:

            @block.sync
            def _(sp):
                for h in range(HEADS):
                    sp.dma_start(XD[h].rearrange("p (t c) -> p t c", c=6 * HC), XALL[:, :, h, :]).then_inc(stored, 16)
                sp.wait_ge(stored, 16 * HEADS)


def head_loop_stage(nc, K, XD, SD, XN0, D0, C1, C2, A0, RES):
    ctx, sb, sem = open_stage(nc, "head_loop")
    with ctx:
        RING = 4
        N_ACT = 14
        ON_ACT = [j for j in range(T) if (j * N_ACT) % T < N_ACT]
        EVAC_AT, COMB_AT, FIN_AT = 4, 9, 14
        C = 6 * HC
        SB = sb("scores", [P, 2, HN], F32)
        XH = sb("parts", [P, 2, T, C], BF16)
        ST = sb("step", [P, RING, HN], U8)
        ME = sb("masked", [P, RING, HN], U8)
        EV = sb("sums", [C, HN], F32)
        T1 = sb("t1", [P, HALF, HC], F32)
        T2 = sb("t2", [P, HALF, HC], F32)
        ND = sb("negd", [P, T, HEADS], F32)
        BD = sb("bigd", [P, T, HEADS], F32)
        BT = sb("turn_bigd", [P, 2, T], F32)
        in_x, in_s = [sem("in_x0"), sem("in_x1")], [sem("in_s0"), sem("in_s1")]
        consts, compared, masked, summed = sem("consts"), sem("compared"), sem("masked"), sem("summed")
        turn_done, evacuated, combined, finished, dve = (sem("turn_done"), sem("evacuated"), sem("combined"),
                                                         sem("finished"), sem("dve"))
        passed, sent, bias_ready = sem("passed"), sem("sent"), sem("bias_ready")
        go, back = sem("go"), sem("back")
        M0, S0 = 2 * T, 2 * N_ACT
        pieces = [(512 * b, min(512, HN - 512 * b)) for b in range(4)]

        def banks(q):
            return K.PS[:, 4 * q:4 * q + 4, :].rearrange("p b n -> p (b n)")

        def evacuate(act, q, n):
            act.wait_ge(turn_done, n + 2)
            act.wait_ge(combined, n + 1)
            nc.scalar.activation(EV[:], banks(q)[0:C, 0:HN], ACT.Copy).then_inc(evacuated, 1)

        def combine(pe, q, n):
            pe.wait_ge(evacuated, n + 1)
            for i in range(HALF):
                last = nc.tensor.matmul(K.PS[:, 4 * q + 3, i * 2 * HC:(i + 1) * 2 * HC], EV[:, i * P:(i + 1) * P],
                                        K.COMB[0:C, :], start=True, stop=True)
            last.then_inc(combined, 1)

        def finish(v, link, q, n, slot, base):
            v.wait_ge(combined, n + 2)
            sums = K.PS[:, 4 * q + 3, 0:HALF * 2 * HC].rearrange("p (t c) -> p t c", c=2 * HC)
            c1, c2 = (bcast_last(c[:, slot, :].rearrange("p a t -> p (a t)"), HC) for c in (C1, C2))
            a0, res = (a[:, slot, :, :].rearrange("p a t c -> p (a t) c") for a in (A0, RES))
            nc.vector.tensor_tensor(T1[:], sums[:, :, 0:HC], c1, ALU.mult)
            link(nc.vector.tensor_tensor(T2[:], a0, sums[:, :, HC:2 * HC], ALU.subtract), base)
            link(nc.vector.tensor_tensor(T2[:], T2[:], c2, ALU.mult), base)
            nc.vector.tensor_tensor(res, T1[:], T2[:], ALU.add).then_inc(finished, 1)

        with nc.Block() as block:

            @block.sync
            def _(sp):
                sp.dma_start(K.XN[:], XN0).then_inc(back, 16)
                sp.wait_ge(back, 16)
                with sp.Fori(0, 2) as half:
                    with sp.Fori(0, HEADS // 2) as pair:
                        for q in range(2):
                            n = 8 * half + 2 * pair + q
                            sp.wait_ge(compared, N_ACT * n + N_ACT)
                            sp.sem_inc(sent, 1)
                            sp.wait_ge(masked, T * n + T)
                            sp.sem_inc(sent, 1)
                            sp.wait_ge(turn_done, n + 1)
                            sp.sem_inc(sent, 1)
                            sp.dma_start(XH[:, q, :, :].rearrange("p t c -> p (t c)"),
                                         XD[bass.ds(2 * pair + q, 1), :, :].rearrange("a p c -> (a p) c")).then_inc(in_x[q], 16)
                            sp.dma_start(SB[:, q, :], SD[bass.ds(2 * pair + q, 1), bass.ds(HN * half, HN)]
                                         .rearrange("a n -> (a n)").partition_broadcast(P)).then_inc(in_s[q], 16)

            @block.scalar
            def _(act):
                act.wait_ge(consts, 2)
                with act.Fori(0, 2) as half:
                    with act.Fori(0, HEADS // 2) as pair:
                        w = 4 * half + pair
                        for q in range(2):
                            act.wait_ge(compared, N_ACT * (2 * w + q) + N_ACT)
                            nc.scalar.activation(BT[:, q, :], BD[:, :, bass.ds(2 * pair + q, 1)].rearrange("p t a -> p (t a)"),
                                                 ACT.Copy).then_inc(bias_ready, 1)
                            act.wait_ge(bias_ready, 2 * w + q + 1)
                            act.wait_ge(in_s[q], 16 * w + 16)
                            act.sem_inc(go, 1)
                            for j in range(T):
                                if j == EVAC_AT:
                                    evacuate(act, 1 - q, 2 * w + q)
                                if j in ON_ACT:
                                    slot = (T * q + j) % RING
                                    act.wait_ge(masked, 2 * T * w + (T * q + j + 1 + M0 - RING))
                                    act.sem_inc(go, 1)
                                    nc.scalar.activation(ST[:, slot, :].bitcast(FP8), SB[:, q, :], ACT.Sigmoid,
                                                         bias=BT[:, q, j:j + 1], scale=BIG,
                                                         saturate=False).then_inc(compared, 1)
                evacuate(act, 1, 2 * HEADS)

            @block.vector
            def _(v):
                link = Link(v, dve)
                for k, prime in ((S0, compared), (M0, masked), (RING, summed), (2, turn_done), (1, combined),
                                 (1, finished)):
                    v.sem_inc(prime, k)
                nc.vector.memset(K.PS[:, 4:8, :], 0.0).then_inc(consts, 1)
                nc.vector.tensor_scalar(BD[:], D0, BIG, None, ALU.mult).then_inc(consts, 1)
                link(nc.vector.tensor_scalar(ND[:], D0, -1.0, None, ALU.mult))
                links = 2 * (T - N_ACT + 2)

                with v.Fori(0, 2) as half:
                    with v.Fori(0, HEADS // 2) as pair:
                        w = 4 * half + pair
                        for q in range(2):
                            made = {}

                            def mask(j):
                                slot = (T * q + j) % RING
                                if j in ON_ACT:
                                    v.wait_ge(compared, 2 * N_ACT * w + (N_ACT * q + ON_ACT.index(j) + 1 + S0))
                                else:
                                    v.wait_ge(dve, links * w + made[j])
                                v.wait_ge(summed, 2 * T * w + (T * q + j + 1))
                                nc.vector.tensor_tensor(
                                    ME[:, slot, :].rearrange("p (t i) -> p t i", i=P).bitcast(U32),
                                    ST[:, slot, :].rearrange("p (t i) -> p t i", i=P).bitcast(U32),
                                    K.EDGE[:, bass.ds(HALF * half, HALF), j, :].bitcast(U32),
                                    ALU.bitwise_and).then_inc(masked, 1)

                            v.wait_ge(in_s[q], 16 * w + 16)
                            for j in range(T):
                                if j == FIN_AT:
                                    n = 2 * w + q
                                    finish(v, link, 1 - q, n, bass.ds(n, 1), links * w)
                                if j not in ON_ACT:
                                    v.wait_ge(masked, 2 * T * w + (T * q + j + 1 + M0 - RING))
                                    nc.vector.tensor_scalar(ST[:, (T * q + j) % RING, :], SB[:, q, :],
                                                            ND[:, j, bass.ds(2 * pair + q, 1)], float(ONE8),
                                                            ALU.is_ge, ALU.mult).then_inc(dve, 1)
                                    link.n += 1
                                    made[j] = link.n
                                if j >= 1:
                                    mask(j - 1)
                            mask(T - 1)
                link.skip(links * 7)
                finish(v, link, 1, 2 * HEADS, slice(2 * HEADS, 2 * HEADS + 1), 0)

            @block.tensor
            def _(pe):
                with pe.Fori(0, 2 * HEADS // 2) as w:
                    for q in range(2):
                        pe.wait_ge(in_x[q], 16 * w + 16)
                        pe.wait_ge(finished, 2 * w + q + 1)
                        for j in range(T):
                            if j == COMB_AT:
                                combine(pe, 1 - q, 2 * w + q)
                            slot = (T * q + j) % RING
                            pe.wait_ge(masked, 2 * T * w + (T * q + j + 1 + M0))
                            pe.sem_inc(passed, 1)
                            for b, (at, n) in enumerate(pieces):
                                last = nc.tensor.matmul(K.PS[0:C, 4 * q + b, 0:n], XH[:, q, j, :],
                                                        ME[:, slot, at:at + n].bitcast(FP8),
                                                        start=(j == 0), stop=(j == T - 1))
                            last.then_inc(summed, 1)
                        pe.wait_ge(summed, 2 * T * w + (T * q + T + RING))
                        nc.tensor.sem_inc(turn_done, 1)
                combine(pe, 1, 2 * HEADS)


def head_merge_stage(nc, K, RES):
    ctx, sb, sem = open_stage(nc, "head_merge")
    with ctx:
        RD = sb("rden", [P, 16, HALF], F32)
        H = sb("h", [P, T, P], F32)
        E = sb("e", [P, T, P], F32)
        dve, low, expd = sem("dve"), sem("low"), sem("expd")
        with nc.Block() as block:

            @block.vector
            def _(v):
                link = Link(v, dve)
                link(nc.vector.tensor_scalar(RD[:], RES[:, 1:17, :, HD], TINY, None, ALU.max))
                link(nc.vector.reciprocal(RD[:], RD[:]))
                for half in range(2):
                    ts = slice(HALF * half, HALF * (half + 1))
                    for h in range(HEADS):
                        n = 8 * half + h
                        last = nc.vector.tensor_tensor(H[:, ts, HD * h:HD * (h + 1)], RES[:, 1 + n, :, 0:HD],
                                                       bcast_last(RD[:, n, :], HD), ALU.mult)
                    link(last)
                    link(nc.vector.tensor_tensor(H[:, ts, :], H[:, ts, :], K.XN[:, ts, :], ALU.add))
                    nc.vector.tensor_scalar(E[:, ts, :], H[:, ts, :], 0.0, None, ALU.min).then_inc(low, 1)
                for half in range(2):
                    ts = slice(HALF * half, HALF * (half + 1))
                    v.wait_ge(expd, half + 1)
                    link(nc.vector.scalar_tensor_tensor(H[:, ts, :], H[:, ts, :], 0.0, E[:, ts, :], ALU.max, ALU.add))
                    link(nc.vector.scalar_tensor_tensor(K.X[:, ts, :], H[:, ts, :], 1.0, K.X[:, ts, :],
                                                        ALU.subtract, ALU.add))

            @block.scalar
            def _(act):
                for half in range(2):
                    ts = slice(HALF * half, HALF * (half + 1))
                    act.wait_ge(low, half + 1)
                    nc.scalar.activation(E[:, ts, :], E[:, ts, :], ACT.Exp).then_inc(expd, 1)


def layer0_gnn(nc, K, D):
    ctx = ExitStack()
    with ctx:
        sb = lambda n, shape, dt: ctx.enter_context(nc.sbuf_tensor(f"g0_{n}", shape, dt))
        A0 = sb("a0", [P, 17, HALF, HC], F32)
        C1 = sb("c1", [P, 17, HALF], F32)
        C2 = sb("c2", [P, 17, HALF], F32)
        D0 = sb("d0", [P, T, HEADS], F32)
        flat = A0[:].rearrange("p a t c -> p (a t c)")
        HP = flat[:, 0:T * 144].rearrange("p (t c) -> p t c", c=144)
        xt = K.XT[:]
        V = xt[:, 0:T * HEADS * HC].rearrange("p (t h c) -> p t h c", h=HEADS, c=HC)
        NAT = xt[:, 0:T * HEADS * HC].rearrange("p (t h c) -> p t h c", h=HEADS, c=HC)
        RES = xt[:, 0:17 * HALF * HC].rearrange("p (a t c) -> p a t c", t=HALF, c=HC)
        inner = ExitStack()
        with inner:
            XALL = inner.enter_context(nc.sbuf_tensor("g0_xall", [P, T, HEADS, 6 * HC], BF16))
            SROW = XALL[0:HEADS, :, :, :].rearrange("p t h c -> p (t h c)")[:, 0:2 * NP].bitcast(F32)
            norm_project_stage(nc, K, "p0", K.WP0[:], 144, 3, lambda t, k: HP[:, t:t + k, :], bias=K.BP0[:],
                               row=(K.WP0[:, P:P + HEADS], K.SB8[:], SROW, D["sd"]))

            def parts(k):
                return lambda s: XALL[:, :, :, (3 * k + s) * HC:(3 * k + s + 1) * HC]

            def natural(c):
                return c[:, 1:17, :].rearrange("p (a h) t -> p a t h", a=2)

            split_stage(nc, K, "x0", HP, HEADS, HD, P + HEADS, (1.0, SLOPE), (parts(0), parts(1)), V,
                        coef=(natural(C1), natural(C2)), keep=D0, store=(D["xn0"], K.XN[:]))
            heads_out_stage(nc, K, XALL, D["xd"])

            def sum_parts(v, link, it, ps, base, done, tmp):
                nc.vector.tensor_reduce(NAT[:, bass.ds(it, 1), :, :].rearrange("p a h c -> p (a h) c"),
                                        ps.rearrange("p (h s c) -> p h c s", h=HEADS, s=3), AX.X, ALU.add).then_inc(done, 1)

            edge_sum_stage(nc, K, "a0", lambda j: XALL[:, j, :, 3 * HC:6 * HC], 3 * HEADS * HC, sum_parts, 0,
                           adj=D["adj"], landing=[b.rearrange("p (b i) -> p b i", i=P).bitcast(I32) for b in
                                                  (K.XN[:].rearrange("p t d -> p (t d)"), flat[:, 0:NP])])
        reorder_stage(nc, K, NAT, A0, C1, C2)
        head_loop_stage(nc, K, D["xd"], D["sd"], D["xn0"], D0[:], C1, C2, A0, RES)
        head_merge_stage(nc, K, RES)


def reorder_stage(nc, K, NAT, A0, C1, C2):
    ctx, sb, sem = open_stage(nc, "reorder")
    with ctx:
        with nc.Block() as block:

            @block.vector
            def _(v):
                for half in range(2):
                    for h in range(HEADS):
                        nc.vector.tensor_copy(A0[:, 1 + 8 * half + h, :, :], NAT[:, HALF * half:HALF * (half + 1), h, :])
                for a in (A0[:, 0, :, :], C1[:, 0, :], C2[:, 0, :]):
                    nc.vector.memset(a, 0.0)


def cosine_prepare_stage(nc, K, QK, QT, KT):
    ctx, sb, sem = open_stage(nc, "cos_prep")
    with ctx:
        COS_EPS = 1e-4
        SS = sb("ss", [P, 2, 2 * T], F32)
        HALF_ = sb("half", [P, 2 * T], F32)
        SQ = sb("sq", [P, T, 2 * P], F32)
        squared, ss_ready, norm_ready, normed = sem("squared"), sem("ss_ready"), sem("norm_ready"), sem("normed")
        transposed, act_taken, dve_taken, dve = sem("transposed"), sem("act_taken"), sem("dve_taken"), sem("dve")
        consts = sem("consts")
        groups = [(m, t, min(4, T - t)) for t in range(0, T, 4) for m in range(2)]
        with nc.Block() as block:

            @block.scalar
            def _(act):
                for h in range(2):
                    ts = slice(HALF * h, HALF * (h + 1))
                    nc.scalar.activation(SQ[:, ts, :], QK[:, ts, :], ACT.Square).then_inc(squared, 1)
                for g, (m, t, k) in enumerate(groups):
                    if m == 0:
                        act.wait_ge(transposed, g + 1)
                        nc.scalar.activation(QT[:, t * P:(t + k) * P], K.PS[:, g % 8, 0:k * P], ACT.Copy)\
                            .then_inc(act_taken, 1)

            @block.gpsimd
            def _(pool):
                nc.gpsimd.memset(HALF_[:], 0.5).then_inc(consts, 1)
                pool.wait_ge(consts, 1)
                pool.wait_ge(ss_ready, 1)
                nc.gpsimd.tensor_tensor(SS[:, 1, :], SS[:, 0, :], HALF_[:], ALU.pow).then_inc(norm_ready, 1)

            @block.vector
            def _(v):
                link = Link(v, dve)
                ss = SS[:, 0, :].rearrange("p (t m) -> p t m", m=2)
                for h in range(2):
                    ts = slice(HALF * h, HALF * (h + 1))
                    v.wait_ge(squared, h + 1)
                    last = nc.vector.tensor_reduce(ss[:, ts, :], SQ[:, ts, :].rearrange("p t (m c) -> p t m c", m=2),
                                                   AX.X, ALU.add)
                last.then_inc(ss_ready, 1)
                v.wait_ge(norm_ready, 1)
                link(nc.vector.tensor_scalar(SS[:, 1, :], SS[:, 1, :], COS_EPS, None, ALU.max))
                link(nc.vector.reciprocal(SS[:, 1, :], SS[:, 1, :]))
                inv = SS[:, 1, :].rearrange("p (t m) -> p t m", m=2)
                for h in range(2):
                    ts = slice(HALF * h, HALF * (h + 1))
                    for m in range(2):
                        last = nc.vector.tensor_tensor(QK[:, ts, m * P:(m + 1) * P], QK[:, ts, m * P:(m + 1) * P],
                                                       bcast_last(inv[:, ts, m], P), ALU.mult)
                    last.then_inc(normed, 1)
                for g, (m, t, k) in enumerate(groups):
                    if m == 1:
                        v.wait_ge(transposed, g + 1)
                        nc.vector.tensor_copy(KT[:, t * P:(t + k) * P], K.PS[:, g % 8, 0:k * P]).then_inc(dve_taken, 1)

            @block.tensor
            def _(pe):
                for g, (m, t, k) in enumerate(groups):
                    pe.wait_ge(normed, 1 if t + k <= HALF else 2)
                    if g >= 8:
                        pe.wait_ge((act_taken, dve_taken)[m], (g - 8) // 2 + 1)
                    for j in range(k):
                        last = nc.tensor.transpose(K.PS[:, g % 8, j * P:(j + 1) * P], QK[:, t + j, m * P:(m + 1) * P],
                                                   K.IDENT[:])
                    last.then_inc(transposed, 1)


def ring_distance(g, steps, ring):
    if g >= ring:
        return ring
    return steps - ((steps - 1 - g) // ring) * ring


def cosine_stage(nc, K, QT, KT, X1):
    ctx, sb, sem = open_stage(nc, "cosine")
    with ctx:
        RING, STEPS, TURNS, LAG = 5, T // 2, T // 2, 2
        PB = sb("probs", [P, RING, 4 * P], F32)
        PA = sb("masked", [P, RING, 4 * P], F32)
        NUM = sb("num", [P, 2, P + 1], F32)
        S = sb("s", [P, 3, 2], F32)
        TM = sb("tm", [P, 2, P], F32)
        ready, scored, expd, masked, summed = sem("ready"), sem("scored"), sem("expd"), sem("masked"), sem("summed")
        taken, scales, added, dve, pool_own = sem("taken"), sem("scales"), sem("added"), sem("dve"), sem("pool_own")
        PRIME = STEPS
        back = [ring_distance(g, STEPS, RING) for g in range(STEPS)]
        with nc.Block() as block:

            @block.scalar
            def _(act):
                with act.Fori(0, TURNS) as c:
                    for g in range(STEPS):
                        act.wait_ge(scored, STEPS * c + g + 1)
                        act.wait_ge(masked, STEPS * c + (g + 1 - back[g] + PRIME))
                        nc.scalar.activation(PB[:, g % RING, :], K.PS[:, g % RING, :], ACT.Exp).then_inc(expd, 1)

            @block.vector
            def _(v):
                v.sem_inc(masked, PRIME)
                v.sem_inc(summed, PRIME)
                v.sem_inc(taken, 1)
                v.sem_inc(added, 1)
                link = Link(v, dve)
                nc.vector.tensor_copy(X1[:, :, 0:P], K.XN[:])
                nc.vector.memset(X1[:, :, P:P + 1], 1.0)
                nc.vector.memset(KT[:, NP:NP + 2 * P], 0.0).then_inc(ready, 1)
                v.wait_ge(ready, 1)
                v.sem_inc(ready, 1)
                with v.Fori(0, TURNS) as c:
                    for g in range(STEPS):
                        v.wait_ge(expd, STEPS * c + g + 1)
                        v.wait_ge(summed, STEPS * c + (g + 1 - back[g] + PRIME))
                        nc.vector.scalar_tensor_tensor(
                            PA[:, g % RING, :].rearrange("p (a n) -> p a n", a=2),
                            K.EDGE[:, bass.ds(2 * c, 2), 2 * g:2 * g + 2, :].rearrange("p a b i -> p a (b i)"), 1.0,
                            PB[:, g % RING, :].rearrange("p (a n) -> p a n", a=2), ALU.min, ALU.mult).then_inc(masked, 1)
                    v.wait_ge(summed, STEPS * c + STEPS + PRIME)
                    v.wait_ge(added, c + 1)
                    nc.vector.tensor_copy(NUM[:], K.PS[:, 5:7, 0:P + 1]).then_inc(taken, 1)
                    v.wait_ge(taken, c + 2)
                    link(nc.vector.tensor_scalar(S[:, 0, :], NUM[:, :, P], TINY, None, ALU.max), 3 * c)
                    link(nc.vector.reciprocal(S[:, 0, :], S[:, 0, :]), 3 * c)
                    link(nc.vector.tensor_scalar(S[:, 2, :], NUM[:, :, P], 0.0, -0.5, ALU.is_gt, ALU.mult), 3 * c)
                    nc.vector.tensor_scalar(S[:, 0, :], S[:, 0, :], 0.5, None, ALU.mult).then_inc(scales, 1)
                    nc.vector.tensor_scalar(S[:, 1, :], S[:, 2, :], 1.0, None, ALU.add).then_inc(scales, 1)

            @block.gpsimd
            def _(pool):
                link = Link(pool, pool_own)
                with pool.Fori(0, TURNS) as c:
                    pool.wait_ge(scales, 2 * c + 2)
                    link(nc.gpsimd.tensor_tensor(NUM[:, :, 0:P], NUM[:, :, 0:P], bcast_last(S[:, 0, :], P), ALU.mult), 3 * c)
                    link(nc.gpsimd.tensor_tensor(TM[:], K.XN[:, bass.ds(2 * c, 2), :], bcast_last(S[:, 1, :], P), ALU.mult), 3 * c)
                    link(nc.gpsimd.tensor_tensor(TM[:], TM[:], NUM[:, :, 0:P], ALU.add), 3 * c)
                    nc.gpsimd.tensor_tensor(K.X[:, bass.ds(2 * c, 2), :], K.X[:, bass.ds(2 * c, 2), :], TM[:], ALU.add)\
                        .then_inc(added, 1)

            @block.tensor
            def _(pe):
                pe.wait_ge(ready, 2)

                def score(g, nodes):
                    for b in range(2):
                        last = nc.tensor.matmul(
                            K.PS[:, g % RING, :].rearrange("p (a b i) -> p b a i", a=2, b=2)[:, b],
                            QT[:, (2 * g + b) * P:(2 * g + b + 1) * P],
                            KT[:, nodes].rearrange("p (a i) -> p a i", a=2), start=True, stop=True)
                    last.then_inc(scored, 1)

                for g in range(LAG):
                    score(g, bass.ds(0, 2 * P))
                with pe.Fori(0, TURNS) as c:
                    for g in range(STEPS):
                        ahead = g + LAG
                        score(ahead % STEPS, bass.ds(2 * P * c + 2 * P * (ahead // STEPS), 2 * P))
                        if g == 0:
                            pe.wait_ge(taken, c + 1)
                        pe.wait_ge(masked, STEPS * c + (g + 1 + PRIME))
                        for a in range(2):
                            for b in range(2):
                                last = nc.tensor.matmul(
                                    K.PS[:, 5 + a, 0:P + 1], PA[:, g % RING, (2 * a + b) * P:(2 * a + b + 1) * P],
                                    X1[:, 2 * g + b, :], start=(g == 0 and b == 0), stop=(g == STEPS - 1 and b == 1))
                        last.then_inc(summed, 1)


def layer1_gnn(nc, K):
    ctx = ExitStack()
    with ctx:
        sb = lambda n, shape, dt: ctx.enter_context(nc.sbuf_tensor(f"g1_{n}", shape, dt))
        QT = sb("qt", [P, NP], F32)
        inner = ExitStack()
        with inner:
            QK = inner.enter_context(nc.sbuf_tensor("g1_qk", [P, T, 2 * P], F32))
            norm_project_stage(nc, K, "p1", K.WP1[:], 2 * P, 2, lambda t, k: QK[:, t:t + k, :])
            cosine_prepare_stage(nc, K, QK, QT, K.XT)
        X1 = sb("x1", [P, T, P + 1], F32)
        cosine_stage(nc, K, QT, K.XT, X1)


def add_softmax(v, link, nc, K, it, num, S, base, done):
    link(nc.vector.tensor_scalar(S[:, 0:1], num[:, P:P + 1], TINY, None, ALU.max), base)
    link(nc.vector.reciprocal(S[:, 1:2], S[:, 0:1]), base)
    x = K.X[:, bass.ds(it, 1), :].rearrange("p a d -> p (a d)")
    nc.vector.scalar_tensor_tensor(x, num[:, 0:P], S[:, 1:2], x, ALU.mult, ALU.add).then_inc(done, 1)


def layer2_gnn(nc, K):
    ctx = ExitStack()
    C = P + 1
    with ctx:
        sb = lambda n, shape, dt: ctx.enter_context(nc.sbuf_tensor(f"g2_{n}", shape, dt))
        XS = sb("xs", [P, T, 3 * C], BF16)
        inner = ExitStack()
        with inner:
            HP = inner.enter_context(nc.sbuf_tensor("g2_hp", [P, T, C], F32))
            norm_project_stage(nc, K, "p2", K.WP2[:], C, 3, lambda t, k: HP[:, t:t + k, :], bias=K.BP2[:])
            V = K.XT[:, 0:T * C].rearrange("p (t a c) -> p t a c", t=T, a=1)
            split_stage(nc, K, "x2", HP, 1, P, P, (1.0,),
                        (lambda s: XS[:, :, s * C:(s + 1) * C].unsqueeze(2),), V)

        def finish(v, link, it, ps, base, done, tmp):
            link(nc.vector.tensor_reduce(tmp[0][:], ps.rearrange("p (s c) -> p c s", s=3), AX.X, ALU.add), base)
            add_softmax(v, link, nc, K, it, tmp[0], tmp[1], base, done)

        edge_sum_stage(nc, K, "a2", lambda j: XS[:, j, :], 3 * C, finish, 3,
                       bufs=lambda sb: (sb("sum", [P, C], F32), sb("s", [P, 2], F32)))


def layer3_gnn(nc, K, D):
    ctx = ExitStack()
    C = P + 1
    with ctx:
        sb = lambda n, shape, dt: ctx.enter_context(nc.sbuf_tensor(f"g3_{n}", shape, dt))
        XF = sb("xs", [P, T * 6 * C], BF16)
        XS = XF[:].rearrange("p (t a c) -> p t a c", a=2, c=3 * C)
        C1 = sb("c1", [P, T, 1], F32)
        C2 = sb("c2", [P, T, 1], F32)
        D0 = sb("d0", [P, T, 1], F32)
        inner = ExitStack()
        with inner:
            HP = inner.enter_context(nc.sbuf_tensor("g3_hp", [P, T, P + 2], F32))
            SROW = XF[0:1, 0:2 * NP].bitcast(F32)
            norm_project_stage(nc, K, "p3", K.WP3[:], P + 2, 3, lambda t, k: HP[:, t:t + k, :], bias=K.BP3[:],
                               row=(K.WP3[:, P:P + 1], K.BP3[0:1, P:P + 1], SROW, D["sd3"]))
            V = K.XT[:, 0:T * C].rearrange("p (t a c) -> p t a c", t=T, a=1)

            def parts(k):
                return lambda s: XS[:, :, k, s * C:(s + 1) * C].unsqueeze(2)

            def natural(c):
                return c[:].rearrange("p (a t) h -> p a t h", a=2)

            split_stage(nc, K, "x3", HP, 1, P, P + 1, (1.0, SLOPE), (parts(0), parts(1)), V,
                        coef=(natural(C1), natural(C2)), keep=D0)
        signed_sum_stage(nc, K, D["sd3"], XS, C1, C2, D0)


def signed_sum_stage(nc, K, SD, XS, C1, C2, D0):
    ctx, sb, sem = open_stage(nc, "signed")
    with ctx:
        C = P + 1
        SB = sb("scores", [P, NP], F32)
        SN = sb("tile_scores", [P, 2, P], F32)
        ST = sb("above", [P, 2, T, P], U8)
        ED = sb("below", [P, 2, T, P], U8)
        ND = sb("negd", [P, T], F32)
        U = sb("u", [P, 2, C], F32)
        S = sb("s", [P, 2], F32)
        in_s, negd, staged, scores_in, parted = sem("in_s"), sem("negd"), sem("staged"), sem("scores_in"), sem("parted")
        summed, finished, dve, passed = sem("summed"), sem("finished"), sem("dve"), sem("passed")
        with nc.Block() as block:

            @block.sync
            def _(sp):
                sp.dma_start(SB[:], SD.rearrange("a n -> (a n)").partition_broadcast(P)).then_inc(in_s, 16)

            @block.scalar
            def _(act):
                act.wait_ge(in_s, 16)
                with act.Fori(0, T // 2) as t:
                    for q in range(2):
                        act.wait_ge(summed, 2 * t + q + 1)
                        nc.scalar.activation(ED[:, q].rearrange("p b i -> p (b i)").bitcast(U16),
                                             K.EDGE[:, bass.ds(2 * t + q, 1)].rearrange("p a b i -> p (a b i)").bitcast(U16),
                                             ACT.Copy).then_inc(staged, 1)
                        nc.scalar.activation(SN[:, q, :], SB[:, bass.ds(P * (2 * t + q), P)], ACT.Copy).then_inc(staged, 1)

            @block.vector
            def _(v):
                link = Link(v, dve)
                v.sem_inc(summed, 2)
                v.sem_inc(finished, 2)
                link(nc.vector.tensor_scalar(ND[:], D0[:, :, 0], -1.0, None, ALU.mult))

                def part(it, q, base):
                    v.wait_ge(staged, 2 * it + 2)
                    v.sem_inc(passed, 1)
                    link(nc.vector.tensor_tensor(ST[:, q].bitcast(FP8), bcast_mid(SN[:, q, :], T),
                                                 bcast_last(ND[:], P), ALU.is_ge, saturate=False), base)
                    st, ed = (x[:, q].rearrange("p b i -> p (b i)").bitcast(U32) for x in (ST, ED))
                    link(nc.vector.tensor_tensor(st, st, ed, ALU.bitwise_and), base)
                    nc.vector.tensor_tensor(ed, ed, st, ALU.bitwise_xor).then_inc(parted, 1)

                def finish(it, q, base):
                    v.wait_ge(summed, it + 3)
                    v.wait_ge(finished, it + 2)
                    for k in range(2):
                        link(nc.vector.tensor_reduce(U[:, k, :], K.PS[:, 2 * q + k, 0:3 * C].rearrange("p (s c) -> p c s", s=3),
                                                     AX.X, ALU.add), base)
                    c1, c2 = (c[:, bass.ds(it, 1), :].rearrange("p a b -> p (a b)") for c in (C1, C2))
                    link(nc.vector.tensor_scalar(U[:, 1, :], U[:, 1, :], c2, None, ALU.mult), base)
                    link(nc.vector.scalar_tensor_tensor(U[:, 0, :], U[:, 0, :], c1, U[:, 1, :], ALU.mult, ALU.add), base)
                    add_softmax(v, link, nc, K, it, U[:, 0, :], S, base, finished)

                per = 2 * (2 + 6)
                for q in range(2):
                    part(q, q, 0)
                with v.Fori(0, T // 2 - 1) as t:
                    for q in range(2):
                        finish(2 * t + q, q, per * t)
                        part(2 * t + q + 2, q, per * t)
                link.skip(per * (T // 2 - 2))
                for q in range(2):
                    finish(T - 2 + q, q, 0)

            @block.tensor
            def _(pe):
                with pe.Fori(0, T // 2) as t:
                    for q in range(2):
                        pe.wait_ge(parted, 2 * t + q + 1)
                        pe.wait_ge(finished, 2 * t + q + 1)
                        pe.sem_inc(passed, 1)
                        for j in range(T):
                            for k, e in enumerate((ST, ED)):
                                last = nc.tensor.matmul(K.PS[:, 2 * q + k, 0:3 * C], e[:, q, j, :].bitcast(FP8),
                                                        XS[:, j, k, :], start=(j == 0), stop=(j == T - 1))
                        last.then_inc(summed, 1)


def moe_route_stage(nc, K, name, LG, E, W, mode, capacity=None, OHT=None):
    ctx, sb, sem = open_stage(nc, name)
    with ctx:
        M8 = sb("max", [P, T, 8], F32)
        I8 = sb("index", [P, T, 8], U32)
        IF = sb("index_f", [P, T, 2], F32)
        OH = sb("onehot", [P, 2, T, E], F32)
        S = sb("s", [P, 4, T], F32)
        dve, act_in, act_out, pe_in, pe_out = sem("dve"), sem("act_in"), sem("act_out"), sem("pe_in"), sem("pe_out")
        taken = sem("taken")
        top1 = mode == "top1"
        CUM = sb("cum", [P, 5, E * T], F32) if top1 else None
        groups = [(t, min(4, T - t)) for t in range(0, T, 4)]
        with nc.Block() as block:

            @block.vector
            def _(v):
                link = Link(v, dve)
                for t in range(T):
                    link(nc.vector.max(M8[:, t, :], LG[:, t, :]))
                    last = nc.vector.max_index(I8[:, t, :], M8[:, t, :], LG[:, t, :])
                link(last)
                link(nc.vector.tensor_copy(IF[:], I8[:, :, 0:2]))
                iota = bcast_mid(K.IOTA[:, 0:E], T)
                if mode == "top2":
                    nc.vector.tensor_tensor(S[:, 0, :], M8[:, :, 1], M8[:, :, 0], ALU.subtract).then_inc(act_in, 1)
                    for k in range(2):
                        last = nc.vector.tensor_tensor(OH[:, k], iota, bcast_last(IF[:, :, k], E), ALU.is_equal)
                    link(last)
                    v.wait_ge(act_out, 1)
                    link(nc.vector.tensor_scalar(S[:, 2, :], S[:, 1, :], 1.0, None, ALU.add))
                    link(nc.vector.reciprocal(S[:, 2, :], S[:, 2, :]))
                    link(nc.vector.tensor_tensor(S[:, 3, :], S[:, 1, :], S[:, 2, :], ALU.mult))
                    for k in range(2):
                        last = nc.vector.tensor_tensor(OH[:, k], OH[:, k], bcast_last(S[:, 2 + k, :], E), ALU.mult)
                    link(last)
                    link(nc.vector.tensor_tensor(W[:], OH[:, 0], OH[:, 1], ALU.add))
                elif mode == "argmax":
                    nc.vector.tensor_tensor(W[:], iota, bcast_last(IF[:, :, 0], E), ALU.is_equal).then_inc(pe_in, 1)
                else:
                    nc.vector.tensor_tensor(OH[:, 1], LG[:], bcast_last(M8[:, :, 0], E), ALU.subtract).then_inc(act_in, 1)
                    nc.vector.tensor_tensor(OH[:, 0], iota, bcast_last(IF[:, :, 0], E), ALU.is_equal).then_inc(pe_in, 1)
                    link(nc.vector.memset(CUM[:, 0, :], 1.0))
                    link(nc.vector.memset(CUM[:, 0, :].rearrange("p (e t) -> p e t", t=T)[:, :, 0:1], 0.0))
                    v.wait_ge(act_out, 1)
                    link(nc.vector.tensor_reduce(S[:, 0, :], OH[:, 1], AX.X, ALU.add))
                    link(nc.vector.reciprocal(S[:, 0, :], S[:, 0, :]))
                    v.wait_ge(pe_out, 1)
                    for k in range(2):
                        last = nc.vector.tensor_copy(CUM[:, 1 + k, :].rearrange("p (e t) -> p e t", t=T),
                                                     K.PS[:, k, 0:T * E].rearrange("p (t e) -> p e t", e=E))
                    link(last)
                    link(nc.vector.tensor_tensor_scan(CUM[:, 3, :], CUM[:, 0, :], CUM[:, 2, :], 0.0, ALU.mult, ALU.add))
                    link(nc.vector.tensor_tensor(CUM[:, 3, :], CUM[:, 3, :], CUM[:, 2, :], ALU.subtract))
                    link(nc.vector.tensor_tensor(CUM[:, 3, :], CUM[:, 3, :], CUM[:, 1, :], ALU.add))
                    link(nc.vector.tensor_scalar(CUM[:, 4, :], CUM[:, 3, :], float(capacity), None, ALU.is_le))
                    link(nc.vector.tensor_tensor(OH[:, 0], OH[:, 0], CUM[:, 4, :].rearrange("p (e t) -> p t e", t=T), ALU.mult))
                    link(nc.vector.tensor_tensor(W[:], OH[:, 0], bcast_last(S[:, 0, :], E), ALU.mult))

            @block.scalar
            def _(act):
                if mode == "top2":
                    act.wait_ge(act_in, 1)
                    nc.scalar.activation(S[:, 1, :], S[:, 0, :], ACT.Exp).then_inc(act_out, 1)
                if top1:
                    act.wait_ge(act_in, 1)
                    nc.scalar.activation(OH[:, 1], OH[:, 1], ACT.Exp).then_inc(act_out, 1)
                if mode == "argmax":
                    for g, (t, k) in enumerate(groups):
                        act.wait_ge(pe_out, g + 1)
                        nc.scalar.activation(OHT[:, t * P:(t + k) * P], K.PS[0:E, g, 0:k * P], ACT.Copy).then_inc(taken, 1)

            @block.tensor
            def _(pe):
                if top1:
                    pe.wait_ge(pe_in, 1)
                    oh = OH[:, 0].rearrange("p t e -> p (t e)")
                    nc.tensor.matmul(K.PS[:, 0, 0:T * E], K.LOWER[:], oh, start=True, stop=True)
                    nc.tensor.matmul(K.PS[:, 1, 0:T * E], K.ONES[:], oh, start=True, stop=True).then_inc(pe_out, 1)
                if mode == "argmax":
                    pe.wait_ge(pe_in, 1)
                    for g, (t, k) in enumerate(groups):
                        for j in range(k):
                            last = nc.tensor.transpose(K.PS[0:E, g, j * P:(j + 1) * P], W[:, t + j, :], K.IDENT[:])
                        last.then_inc(pe_out, 1)


def moe_bias_stage(nc, K, name, W, B2, E, dest, add):
    ctx, sb, sem = open_stage(nc, name)
    with ctx:
        WT = sb("wt", [E, NP], F32)
        transposed, wt_ready, biased, taken = sem("transposed"), sem("wt_ready"), sem("biased"), sem("taken")
        groups = [(t, min(4, T - t)) for t in range(0, T, 4)]
        with nc.Block() as block:

            @block.tensor
            def _(pe):
                for g, (t, k) in enumerate(groups):
                    if g >= 4:
                        pe.wait_ge(wt_ready, g - 3)
                    for j in range(k):
                        last = nc.tensor.transpose(K.PS[0:E, g % 4, j * P:(j + 1) * P], W[:, t + j, :], K.IDENT[:])
                    last.then_inc(transposed, 1)
                for g, (t, k) in enumerate(groups):
                    pe.wait_ge(wt_ready, g + 1)
                    if g >= 4:
                        pe.wait_ge(taken, g - 3)
                    for j in range(k):
                        last = nc.tensor.matmul(K.PS[:, 4 + g % 4, j * P:(j + 1) * P], WT[:, (t + j) * P:(t + j + 1) * P],
                                                B2[:], start=True, stop=True)
                    last.then_inc(biased, 1)

            @block.scalar
            def _(act):
                for g, (t, k) in enumerate(groups):
                    act.wait_ge(transposed, g + 1)
                    nc.scalar.activation(WT[:, t * P:(t + k) * P], K.PS[0:E, g % 4, 0:k * P], ACT.Copy).then_inc(wt_ready, 1)

            @block.vector
            def _(v):
                for g, (t, k) in enumerate(groups):
                    v.wait_ge(biased, g + 1)
                    ps = K.PS[:, 4 + g % 4, 0:k * P].rearrange("p (k d) -> p k d", d=P)
                    if add:
                        nc.vector.tensor_tensor(dest[:, t:t + k, :], dest[:, t:t + k, :], ps, ALU.add).then_inc(taken, 1)
                    else:
                        nc.vector.tensor_copy(dest[:, t:t + k, :], ps).then_inc(taken, 1)


def moe_stage(nc, K, name, W1, B1, W2, W, E, HT, func, acc, guard=None):
    ctx, sb, sem = open_stage(nc, name)
    with ctx:
        STEPS, TURNS, LAG, RING = E * HT, T // 2, 2, 4
        G = sb("hidden", [P, RING, 2 * P], F32)
        hidden, active, used, added, dve = sem("hidden"), sem("active"), sem("used"), sem("added"), sem("dve")
        held = sem("held")
        glinks = guard[1] if guard else 0
        with nc.Block() as block:

            @block.tensor
            def _(pe):
                def up(k, nodes):
                    nc.tensor.matmul(K.PS[:, k % RING, 0:2 * P], W1[:, k * P:(k + 1) * P], K.XT[:, nodes],
                                     start=True, stop=True).then_inc(hidden, 1)

                for k in range(LAG):
                    up(k, bass.ds(0, 2 * P))
                with pe.Fori(0, TURNS) as c:
                    for k in range(STEPS):
                        e, h = divmod(k, HT)
                        ahead = k + LAG
                        up(ahead % STEPS, bass.ds(2 * P * c + 2 * P * (ahead // STEPS), 2 * P))
                        pe.wait_ge(active, STEPS * c + k + 1)
                        if h == 0:
                            pe.wait_ge(added, E * c + e + 1)
                        for a in range(2):
                            last = nc.tensor.matmul(K.PS[:, 4 + 2 * (e % 2) + a, 0:P], G[:, k % RING, a * P:(a + 1) * P],
                                                    W2[:, k, :], start=(h == 0), stop=(h == HT - 1))
                        last.then_inc(used, 1)

            @block.scalar
            def _(act):
                with act.Fori(0, TURNS) as c:
                    for k in range(STEPS):
                        act.wait_ge(hidden, STEPS * c + k + 1)
                        act.wait_ge(used, STEPS * c + k + 1)
                        nc.scalar.activation(G[:, k % RING, :], K.PS[:, k % RING, 0:2 * P], func,
                                             bias=B1[:, k:k + 1]).then_inc(active, 1)

            @block.vector
            def _(v):
                v.sem_inc(used, RING)
                v.sem_inc(added, 2)
                link = Link(v, dve)
                with v.Fori(0, TURNS) as c:
                    for e in range(E):
                        v.wait_ge(used, STEPS * c + (HT * (e + 1) + RING))
                        v.wait_ge(added, E * c + e + 2)
                        for a in range(2):
                            x = acc[:, bass.ds(2 * c + a, 1), :].rearrange("p a d -> p (a d)")
                            last = nc.vector.scalar_tensor_tensor(x, K.PS[:, 4 + 2 * (e % 2) + a, 0:P],
                                                                  W[:, bass.ds(2 * c + a, 1), e], x, ALU.mult, ALU.add)
                        last.then_inc(added, 1)
                    if guard:
                        v.wait_ge(added, E * c + E + 2)
                        guard[0](v, link, c, glinks * c, held)


def moe_layer(nc, K, D, name, r0, E, HT, func, mode, twice=False, capacity=None, guard=False):
    ctx = ExitStack()
    with ctx:
        sb = lambda n, shape, dt: ctx.enter_context(nc.sbuf_tensor(f"{name}_{n}", shape, dt))
        W1 = sb("w1", [P, E * HT * P], F32)
        W2 = sb("w2", [P, E * HT, P], F32)
        B1 = sb("b1", [P, E * HT], F32)
        B2 = sb("b2", [E, P], F32)
        LG = sb("logits", [P, T, E], F32)
        W = sb("weights", [P, T, E], F32)
        loads = [(W1[:], D[f"{name}_w1"]), (W2[:], D[f"{name}_w2"]), (B1[:], D[f"{name}_b1"]), (B2[:], D[f"{name}_b2"])]
        norm_project_stage(nc, K, f"{name}p", K.R[:, r0:r0 + E], E, T, lambda t, k: LG[:, t:t + k, :],
                           bias=K.BR[:, r0:r0 + E], twice=twice, affine=twice, loads=loads)
        moe_route_stage(nc, K, f"{name}r", LG, E, W, mode, capacity)
        acc = K.XN if guard else K.X
        moe_bias_stage(nc, K, f"{name}b", W, B2, E, acc, add=not guard)
        MASK = sb("mask", [P, 2 * P], F32) if guard else None

        def nan_to_num(v, link, c, base, held):
            y = acc[:, bass.ds(2 * c, 2), :].rearrange("p a d -> p (a d)")
            x = K.X[:, bass.ds(2 * c, 2), :].rearrange("p a d -> p (a d)")
            fmax = float(np.finfo(np.float32).max)
            link(nc.vector.tensor_scalar(YT[:], y, 0.0, None, ALU.add), base)
            for op, bound, value in ((ALU.is_gt, fmax, 0), (ALU.is_lt, -fmax, 1), (ALU.not_equal, None, 2)):
                if bound is None:
                    link(nc.vector.tensor_tensor(MASK[:], YT[:], YT[:], op), base)
                else:
                    link(nc.vector.tensor_scalar(MASK[:], YT[:], bound, None, op), base)
                v.sem_inc(held, 1)
                link(nc.vector.copy_predicated(YT[:], MASK[:].bitcast(U32), VAL[:, value, :]), base)
            link(nc.vector.tensor_tensor(x, x, YT[:], ALU.add), base)

        if guard:
            YT = sb("y", [P, 2 * P], F32)
            VAL = sb("values", [P, 3, 2 * P], F32)
            with nc.Block() as block:

                @block.gpsimd
                def _(pool):
                    for k, value in enumerate((1e4, -1e4, 0.0)):
                        nc.gpsimd.memset(VAL[:, k, :], value)
        moe_stage(nc, K, f"{name}m", W1, B1, W2, W, E, HT, func, acc, guard=(nan_to_num, 8) if guard else None)


def moe32_layer(nc, K, D):
    ctx = ExitStack()
    with ctx:
        E, H, HT, RING, LAG = 32, 32, 8, 4, 2
        sb = lambda n, shape, dt: ctx.enter_context(nc.sbuf_tensor(f"f2_{n}", shape, dt))
        W1 = sb("w1", [P, HT * P], F32)
        W2 = sb("w2", [P, HT, P], F32)
        B1 = sb("b1", [P, HT], F32)
        B2 = sb("b2", [E, P], F32)
        BS = sb("b2_parts", [E, 3, P], BF16)
        SPREAD = sb("spread", [E, HT, P], F32)
        SP16 = sb("spread16", [E, HT, P], BF16)
        LG = sb("logits", [P, T, E], F32)
        W = sb("onehot", [P, T, E], F32)
        OHT = sb("oht", [E, NP + 2 * P], BF16)
        G0 = sb("relu", [P, RING, 2 * P], F32)
        G = sb("chosen", [P, RING, 2 * P], F32)
        loads = [(W1[:], D["f2_w1"]), (W2[:], D["f2_w2"]), (B1[:], D["f2_b1"]), (B2[:], D["f2_b2"]), (SPREAD[:], D["spread"])]
        norm_project_stage(nc, K, "f2p", K.R[:, 16:48], E, 16, lambda t, k: LG[:, t:t + k, :], bias=K.BR[:, 16:48], loads=loads)
        moe_route_stage(nc, K, "f2r", LG, E, W, "argmax", OHT=OHT)
        sems, _, sem = open_stage(nc, "f2m")
        with sems:
            ready, hidden, active, chosen, used, added, dve = (sem("ready"), sem("hidden"), sem("active"), sem("chosen"),
                                                               sem("used"), sem("added"), sem("dve"))
            biased = sem("biased")
            with nc.Block() as block:

                @block.tensor
                def _(pe):
                    pe.wait_ge(ready, 1)

                    def up(k, nodes):
                        nc.tensor.matmul(K.PS[:, k % RING, 0:2 * P], W1[:, k * P:(k + 1) * P], K.XT[:, nodes],
                                         start=True, stop=True)
                        nc.tensor.matmul(K.PS[:, k % RING, 2 * P:4 * P], SP16[:, k, :], OHT[:, nodes],
                                         start=True, stop=True).then_inc(hidden, 1)

                    for k in range(LAG):
                        up(k, bass.ds(0, 2 * P))
                    with pe.Fori(0, T // 2) as c:
                        for k in range(HT):
                            ahead = k + LAG
                            up(ahead % HT, bass.ds(2 * P * c + 2 * P * (ahead // HT), 2 * P))
                            if k == 0:
                                pe.wait_ge(added, c + 1)
                            pe.wait_ge(chosen, HT * c + (k + 1 + RING))
                            for a in range(2):
                                last = nc.tensor.matmul(K.PS[:, 4 + a, 0:P], G[:, k % RING, a * P:(a + 1) * P], W2[:, k, :],
                                                        start=(k == 0), stop=False)
                            last.then_inc(used, 1)
                        for a in range(2):
                            for s in range(3):
                                last = nc.tensor.matmul(K.PS[:, 4 + a, 0:P], OHT[:, bass.ds(2 * P * c + a * P, P)], BS[:, s, :],
                                                        start=False, stop=(s == 2))
                        last.then_inc(biased, 1)

                @block.scalar
                def _(act):
                    with act.Fori(0, T // 2) as c:
                        for k in range(HT):
                            act.wait_ge(hidden, HT * c + k + 1)
                            act.wait_ge(chosen, HT * c + k + 1)
                            nc.scalar.activation(G0[:, k % RING, :], K.PS[:, k % RING, 0:2 * P], ACT.Relu,
                                                 bias=B1[:, k:k + 1]).then_inc(active, 1)

                @block.vector
                def _(v):
                    link = Link(v, dve)
                    for part in range(3):
                        link(nc.vector.tensor_copy(BS[:, part, :], B2[:]))
                        if part < 2:
                            link(nc.vector.tensor_tensor(B2[:], B2[:], BS[:, part, :], ALU.subtract))
                    link(nc.vector.memset(OHT[:, NP:NP + 2 * P], 0.0))
                    nc.vector.tensor_copy(SP16[:], SPREAD[:]).then_inc(ready, 1)
                    v.sem_inc(chosen, RING)
                    v.sem_inc(used, RING)
                    v.sem_inc(added, 1)
                    with v.Fori(0, T // 2) as c:
                        for k in range(HT):
                            v.wait_ge(active, HT * c + k + 1)
                            v.wait_ge(used, HT * c + k + 1)
                            nc.vector.tensor_tensor(G[:, k % RING, :], G0[:, k % RING, :],
                                                    K.PS[:, k % RING, 2 * P:4 * P], ALU.mult).then_inc(chosen, 1)
                        v.wait_ge(biased, c + 1)
                        x = K.X[:, bass.ds(2 * c, 2), :]
                        nc.vector.scalar_tensor_tensor(x, K.PS[:, 4:6, 0:P], 0.0, x, ALU.max, ALU.add).then_inc(added, 1)


def program(nc, A, out, upto=99):
    D = {"xd": nc.dram_tensor("head_parts", [HEADS, P, T * 6 * HC], BF16).ap(),
         "sd": nc.dram_tensor("head_scores", [HEADS, NP], F32).ap(),
         "xn0": nc.dram_tensor("normed0", [P, T, P], F32).ap(),
         "sd3": nc.dram_tensor("scores3", [1, NP], F32).ap(), **A}
    K = Core()
    RETIRED.clear()
    ctx = ExitStack()
    with ctx:
        sb = lambda n, shape, dt: ctx.enter_context(nc.sbuf_tensor(n, shape, dt))
        K.EDGE = sb("edge", [P, T, T, P], U8)
        K.X = sb("nodes", [P, T, P], F32)
        K.XN = sb("normed", [P, T, P], F32)
        K.XT = sb("normed_t", [P, NP + 4 * P], F32)
        K.IDENT = sb("ident", [P, P], F32)
        K.ONES = sb("ones", [P, P], F32)
        K.LOWER = sb("lower", [P, P], F32)
        K.COMB = sb("comb", [P, 2 * HC], F32)
        K.IOTA = sb("iota", [P, 32], F32)
        K.NEG_HALF = sb("neg_half", [P, T], F32)
        K.WP0, K.BP0 = sb("wp0", [P, P + 16], F32), sb("bp0", [P, P + 16], F32)
        K.WP1 = sb("wp1", [P, 2 * P], F32)
        K.WP2, K.BP2 = sb("wp2", [P, P + 1], F32), sb("bp2", [P, P + 1], F32)
        K.WP3, K.BP3 = sb("wp3", [P, P + 2], F32), sb("bp3", [P, P + 2], F32)
        K.SB8 = sb("sb8", [HEADS, 1], F32)
        K.R, K.BR = sb("routers", [P, 56], F32), sb("router_b", [P, 56], F32)
        K.GB = sb("gamma_beta", [P, 2], F32)
        K.PS = ctx.enter_context(nc.psum_tensor("psum", [P, 8, 512], F32))
        stages = [
            lambda: setup_stage(nc, K, A),
            lambda: layer0_gnn(nc, K, D),
            lambda: moe_layer(nc, K, D, "f0", 0, 8, 2, ACT.Gelu, "top2", twice=True),
            lambda: layer1_gnn(nc, K),
            lambda: moe_layer(nc, K, D, "f1", 8, 8, 4, ACT.Gelu, "top2"),
            lambda: layer2_gnn(nc, K),
            lambda: moe32_layer(nc, K, D),
            lambda: layer3_gnn(nc, K, D),
            lambda: moe_layer(nc, K, D, "f3", 48, 8, 4, ACT.Relu, "top1", capacity=CAPACITY, guard=True),
        ]
        for s in stages[:upto]:
            s()
        out_stage(nc, K, out)


def out_stage(nc, K, out):
    ctx, sb, sem = open_stage(nc, "out")
    with ctx:
        stored = sem("stored")
        with nc.Block() as block:

            @block.sync
            def _(sp):
                sp.dma_start(out[0:(T - 1) * P, :].rearrange("(t p) d -> p t d", p=P), K.X[:, 0:T - 1, :]).then_inc(stored, 16)
                sp.dma_start(out[(T - 1) * P:N, :], K.X[0:N - (T - 1) * P, T - 1, :]).then_inc(stored, 16)
                sp.wait_ge(stored, 32)


def layouts(i):
    a = {k: np.asarray(v) for k, v in i.items()}
    x = np.zeros((NP, P), np.float32)
    x[:N] = a["x"]
    adj = np.zeros((NP, NP), np.int32)
    adj[:N, :N] = a["adj"]
    aw = a["L0_gnn_a_w"]
    sel = np.zeros((P, 2 * HEADS), np.float32)
    for h in range(HEADS):
        sel[HD * h:HD * (h + 1), h] = aw[0, :HD]
        sel[HD * h:HD * (h + 1), HEADS + h] = aw[0, HD:]
    c = np.ascontiguousarray
    experts = {}
    for name, w1, b1, w2, b2 in (("f0", "L0_ffn_W1", "L0_ffn_b1", "L0_ffn_W2", "L0_ffn_b2"),
                                 ("f1", "L1_ffn_W1", "L1_ffn_b1", "L1_ffn_W2", "L1_ffn_b2"),
                                 ("f2", "L2_ffn_W1", "L2_ffn_b1", "L2_ffn_W2", "L2_ffn_b2"),
                                 ("f3", "L3_ffn_w1", "L3_ffn_b1", "L3_ffn_w2", "L3_ffn_b2")):
        experts[f"{name}_w1"] = c(a[w1].transpose(1, 0, 2).reshape(P, -1))
        experts[f"{name}_w2"] = c(a[w2].reshape(-1, P, P).transpose(1, 0, 2))
        experts[f"{name}_b1"] = c(a[b1].reshape(-1, P).T)
        experts[f"{name}_b2"] = a[b2]
    spread = np.zeros((32, 8, P), np.float32)
    for e in range(32):
        spread[e, e // 4, 32 * (e % 4):32 * (e % 4 + 1)] = 1.0
    return {
        **experts, "spread": spread,
        "x": c(x.reshape(T, P, P).transpose(1, 0, 2)),
        "adj": c(adj.reshape(T, P, T, P).transpose(0, 3, 2, 1).reshape(T, P, NP)),
        "w0t": c(a["L0_gnn_W_w"].T), "w0": c(a["L0_gnn_W_w"]), "sel0": sel,
        "wqk": c(np.concatenate([a["L1_gnn_Wq"].T, a["L1_gnn_Wk"].T], 1)),
        "w2": c(a["L2_gnn_W_fc"]), "w2t": c(a["L2_gnn_W_fc"].T), "dst2": c(a["L2_gnn_w_att"][P:].reshape(P, 1)),
        "w3t": c(a["L3_gnn_W_w"].T), "w3": c(a["L3_gnn_W_w"]),
        "a3": c(np.stack([a["L3_gnn_a_src"], a["L3_gnn_a_dst"]], 1)),
        "bcols": c(np.stack([a["L0_gnn_W_b"], a["L2_gnn_b_fc"], a["L3_gnn_W_b"]], 1)),
        "b0": c(a["L0_gnn_W_b"]), "b2": c(a["L2_gnn_b_fc"]), "b3": c(a["L3_gnn_W_b"]),
        "ab": c(np.concatenate([a["L0_gnn_a_b"].reshape(1), a["L3_gnn_a_b"].reshape(1)])),
        "routers": c(np.concatenate([a["L0_ffn_Wr"], a["L1_ffn_Wg"], a["L2_ffn_router_w"].T, a["L3_ffn_gate_w"]], 1)),
        "router_b": c(np.concatenate([a["L0_ffn_br"], a["L1_ffn_bg"], a["L2_ffn_router_b"], a["L3_ffn_gate_b"]])),
        "gamma_beta": c(np.stack([a["L0_ffn_gamma"], a["L0_ffn_beta"]], 1)),
    }


def kernel(**inputs):
    import concourse.bacc as bacc
    from concourse.bass_utils import run_bass_kernel_spmd

    nc = bacc.Bacc("TRN2", target_bir_lowering=False, num_devices=1)
    arrays = layouts(inputs)
    args = {n: nc.dram_tensor(f"in_{n}", a.shape, mybir.dt.from_np(a.dtype), kind="ExternalInput").ap()
            for n, a in arrays.items()}
    out = nc.dram_tensor("out", (N, P), F32, kind="ExternalOutput").ap()
    program(nc, args, out)
    r = run_bass_kernel_spmd(nc, [{f"in_{n}": a for n, a in arrays.items()}], core_ids=[0])
    return r.results[0]["out"]
```

```python
import math
from contextlib import ExitStack

import numpy as np
import concourse.bass as bass
from concourse import mybir

F32 = mybir.dt.float32
BF16 = mybir.dt.bfloat16
FP8 = mybir.dt.float8e4
U8 = mybir.dt.uint8
U16 = mybir.dt.uint16
U32 = mybir.dt.uint32
I32 = mybir.dt.int32
ALU = mybir.AluOpType
ACT = mybir.ActivationFunctionType
AX = mybir.AxisListType

N = 3327
P = 128
T = 26
NP = T * P
HALF = T // 2
HN = HALF * P
LN_EPS = 1e-5
ONE8 = 56
TINY = 1e-30
HEADS, HD = 8, 16
HC = HD + 1
BIG = 2.0 ** 100
SLOPE = 0.2
CAPACITY = math.ceil(1.25 * N / 8)
PAIR_BLOCK = 2 * P
PAIR_BLOCKS = (2 * NP + 8 * (PAIR_BLOCK - 1)) // PAIR_BLOCK
SLOTS = max(PAIR_BLOCKS * PAIR_BLOCK + 1, 8 * CAPACITY + NP)


STAGE_SEMS = 24
RETIRED = []


class Link:

    def __init__(self, eng, sem):
        self.eng, self.sem, self.n = eng, sem, 0

    def __call__(self, ins, base=0):
        self.n += 1
        ins.then_inc(self.sem, 1)
        self.eng.wait_ge(self.sem, base + self.n)

    def skip(self, n):
        self.n += n


class Core:
    pass


def bcast_mid(ap, n):
    return ap.unsqueeze(1).to_broadcast([ap.shape[0], n, ap.shape[1]])


def bcast_last(ap, n):
    return ap.unsqueeze(2).to_broadcast([ap.shape[0], ap.shape[1], n])


def open_stage(nc, name):
    ctx = ExitStack()
    if len(nc.free_semaphores) < STAGE_SEMS:
        nc.clear_and_free_semaphores(RETIRED)
        RETIRED.clear()
        nc.all_engine_barrier()

    def sb(n, shape, dt):
        return ctx.enter_context(nc.sbuf_tensor(f"{name}_{n}", shape, dt))

    def sem(n):
        RETIRED.append(nc.alloc_semaphore(f"{name}_{n}"))
        return RETIRED[-1]

    return ctx, sb, sem


def setup_stage(nc, K, A):
    ctx, sb, sem = open_stage(nc, "setup")
    with ctx:
        SEL0 = sb("sel0", [P, 16], F32)
        W0 = sb("w0", [P, P], F32)
        WT2 = sb("wt2", [P, P], F32)
        DST2 = sb("dst2", [P, 1], F32)
        W3 = sb("w3", [P, P], F32)
        A3 = sb("a3", [P, 2], F32)
        BC = sb("bc", [P, 3], F32)
        BW = sb("bw", [P, 3, P], F32)
        AB = sb("ab", [P, 2], F32)
        loaded, cols, consts, products = sem("loaded"), sem("cols"), sem("consts"), sem("products")
        loads = [
            (K.X[:], A["x"]),
            (K.WP0[:, 0:P], A["w0t"]), (W0[:], A["w0"]), (SEL0[:], A["sel0"]),
            (K.WP1[:], A["wqk"]),
            (K.WP2[:, 0:P], A["w2"]), (WT2[:], A["w2t"]), (DST2[:], A["dst2"]),
            (K.WP3[:, 0:P], A["w3t"]), (W3[:], A["w3"]), (A3[:], A["a3"]),
            (BC[:], A["bcols"]),
            (K.BP0[:, 0:P], A["b0"].partition_broadcast(P)),
            (K.BP2[:, 0:P], A["b2"].partition_broadcast(P)),
            (K.BP3[:, 0:P], A["b3"].partition_broadcast(P)),
            (AB[:], A["ab"].partition_broadcast(P)),
            (K.R[:], A["routers"]),
            (K.BR[:], A["router_b"].partition_broadcast(P)),
            (K.GB[:], A["gamma_beta"]),
        ]
        n_loads = 16 * len(loads)
        with nc.Block() as block:

            @block.scalar
            def _(act):
                for dst, src in loads:
                    act.dma_start(dst, src).then_inc(loaded, 16)
                act.wait_ge(loaded, n_loads)
                for k in range(3):
                    nc.scalar.activation(BW[:, k, :], BC[:, k:k + 1].to_broadcast([P, P]), ACT.Copy)\
                        .then_inc(cols, 1)

            @block.gpsimd
            def _(pool):
                nc.gpsimd.memset(K.ONES[:], 1.0).then_inc(consts, 1)
                nc.gpsimd.memset(K.IDENT[:], 0.0).then_inc(consts, 1)
                nc.gpsimd.memset(K.XT[:, NP:NP + 2 * P], 0.0).then_inc(consts, 1)
                nc.gpsimd.memset(K.NEG_HALF[:], -0.5).then_inc(consts, 1)
                nc.gpsimd.iota(K.IOTA[:], pattern=[[1, 32]], base=-32, channel_multiplier=0,
                               allow_small_or_imprecise_dtypes=True).then_inc(consts, 1)
                nc.gpsimd.iota(K.OVERFLOW[:], pattern=[[P, T]], base=8 * CAPACITY, channel_multiplier=1,
                               allow_small_or_imprecise_dtypes=True).then_inc(consts, 1)
                nc.gpsimd.memset(K.ZERO[:], 0.0).then_inc(consts, 1)
                pool.wait_ge(consts, 7)
                nc.gpsimd.affine_select(out=K.IDENT[:], in_=K.IDENT[:], compare_op=ALU.not_equal, fill=1.0,
                                        base=0, pattern=[[-1, P]], channel_multiplier=1).then_inc(consts, 1)
                nc.gpsimd.affine_select(out=K.LOWER[:], in_=K.ONES[:], compare_op=ALU.is_ge, fill=0.0,
                                        base=0, pattern=[[1, P]], channel_multiplier=-1).then_inc(consts, 1)
                nc.gpsimd.memset(K.COMB[:], 0.0).then_inc(consts, 1)
                pool.wait_ge(consts, 10)
                for k in range(2):
                    for s in range(3):
                        nc.gpsimd.affine_select(
                            out=K.COMB[:, k * HC:(k + 1) * HC], in_=K.COMB[:, k * HC:(k + 1) * HC],
                            compare_op=ALU.not_equal, fill=1.0, base=-(3 * HC * k + HC * s),
                            pattern=[[-1, HC]], channel_multiplier=1).then_inc(consts, 1)
                        pool.wait_ge(consts, 11 + 3 * k + s)

            @block.tensor
            def _(pe):
                pe.wait_ge(loaded, n_loads)
                nc.tensor.matmul(K.PS[:, 0, 0:16], W0[:], SEL0[:], start=True, stop=True)
                nc.tensor.matmul(K.PS[:, 1, 0:1], WT2[:], DST2[:], start=True, stop=True)
                nc.tensor.matmul(K.PS[:, 2, 0:2], W3[:], A3[:], start=True, stop=True)
                pe.wait_ge(cols, 3)
                nc.tensor.matmul(K.PS[:, 3, 0:16], BW[:, 0, :], SEL0[:], start=True, stop=True)
                nc.tensor.matmul(K.PS[:, 4, 0:1], BW[:, 1, :], DST2[:], start=True, stop=True)
                nc.tensor.matmul(K.PS[:, 5, 0:2], BW[:, 2, :], A3[:], start=True, stop=True)
                nc.tensor.matmul(K.PS[0:HEADS, 6, 0:1], SEL0[:, 0:HEADS], BC[:, 0:1], start=True, stop=True)\
                    .then_inc(products, 1)

            @block.vector
            def _(v):
                v.wait_ge(loaded, n_loads)
                v.wait_ge(products, 1)
                nc.vector.tensor_copy(K.WP0[:, P:P + 16], K.PS[:, 0, 0:16])
                nc.vector.tensor_copy(K.WP2[:, P:P + 1], K.PS[:, 1, 0:1])
                nc.vector.tensor_copy(K.WP3[:, P:P + 2], K.PS[:, 2, 0:2])
                nc.vector.tensor_scalar(K.BP0[:, P:P + 8], K.PS[:, 3, 0:8], AB[:, 0:1], None, ALU.add)
                nc.vector.tensor_copy(K.BP0[:, P + 8:P + 16], K.PS[:, 3, 8:16])
                nc.vector.tensor_copy(K.BP2[:, P:P + 1], K.PS[:, 4, 0:1])
                nc.vector.tensor_scalar(K.BP3[:, P:P + 1], K.PS[:, 5, 0:1], AB[:, 1:2], None, ALU.add)
                nc.vector.tensor_copy(K.BP3[:, P + 1:P + 2], K.PS[:, 5, 1:2])
                nc.vector.tensor_scalar(K.SB8[:], K.PS[0:HEADS, 6, 0:1], AB[0:HEADS, 0:1], None, ALU.add)


def norm_project_stage(nc, K, name, W, n, per, dest, bias=None, twice=False, affine=False, row=None,
                       loads=()):
    ctx, sb, sem = open_stage(nc, name)
    with ctx:
        ST = sb("stats", [P, T, 6], F32)
        M = sb("moments", [P, 6, T], F32)
        var_ready, rstd_ready, normed = sem("var_ready"), sem("rstd_ready"), sem("normed")
        transposed, xt_ready = sem("transposed"), sem("xt_ready")
        projected, taken, dve = sem("projected"), sem("taken"), sem("dve")
        loaded = sem("loaded")
        row_done, row_taken, row_stored = sem("row_done"), sem("row_taken"), sem("row_stored")
        passes = 2 if twice else 1
        chunks = [(0, 4), (4, 8), (12, 8), (20, 6)]
        items = [(rnd, c) for rnd in range(passes) for c in range(len(chunks))]
        tgroups = [(t, min(4, T - t)) for t in range(0, T, 4)]
        pgroups = [(t, min(per, T - t)) for t in range(0, T, per)]

        def ending_in(groups, c):
            t0, k = chunks[c]
            return [(g, t, m) for g, (t, m) in enumerate(groups) if t0 < t + m <= t0 + k]

        with nc.Block() as block:

            @block.vector
            def _(v):
                link = Link(v, dve)

                def variance(rnd, c):
                    t0, k = chunks[c]
                    src, ts = (K.XN if rnd else K.X), slice(t0, t0 + k)
                    for t in range(t0, t0 + k):
                        last = nc.vector.bn_stats(ST[:, t, :], src[:, t, :])
                    link(last)
                    nc.vector.tensor_tensor(M[:, 0, ts], ST[:, ts, 1], ST[:, ts, 4], ALU.add)
                    nc.vector.tensor_tensor(M[:, 1, ts], ST[:, ts, 1], ST[:, ts, 4], ALU.subtract)
                    link(nc.vector.tensor_tensor(M[:, 2, ts], ST[:, ts, 2], ST[:, ts, 5], ALU.add))
                    nc.vector.tensor_scalar(M[:, 0, ts], M[:, 0, ts], 0.5, None, ALU.mult)
                    link(nc.vector.tensor_tensor(M[:, 3, ts], M[:, 1, ts], M[:, 1, ts], ALU.mult))
                    link(nc.vector.scalar_tensor_tensor(M[:, 2, ts], M[:, 3, ts], P / 4.0, M[:, 2, ts], ALU.mult, ALU.add))
                    nc.vector.tensor_scalar(M[:, 4, ts], M[:, 2, ts], 1.0 / P, LN_EPS, ALU.mult, ALU.add)\
                        .then_inc(var_ready, 1)

                def norm(i):
                    rnd, c = items[i]
                    t0, k = chunks[c]
                    src, ts = (K.XN if rnd else K.X), slice(t0, t0 + k)
                    link(nc.vector.tensor_tensor(K.XN[:, ts, :], src[:, ts, :], bcast_last(M[:, 0, ts], P), ALU.subtract))
                    v.wait_ge(rstd_ready, i + 1)
                    last = nc.vector.tensor_tensor(K.XN[:, ts, :], K.XN[:, ts, :], bcast_last(M[:, 5, ts], P), ALU.mult)
                    if rnd == passes - 1:
                        last.then_inc(normed, 1)
                    else:
                        link(last)

                def take(c):
                    for g, t, k in ending_in(pgroups, c):
                        v.wait_ge(projected, g + 1)
                        ps = K.PS[:, 4 + g % 4, 0:k * n].rearrange("p (k n) -> p k n", n=n)
                        if bias is None:
                            nc.vector.tensor_copy(dest(t, k), ps).then_inc(taken, 1)
                        else:
                            nc.vector.tensor_tensor(dest(t, k), ps, bcast_mid(bias, k), ALU.add).then_inc(taken, 1)

                variance(*items[0])
                for i, (rnd, c) in enumerate(items):
                    if i + 1 < len(items):
                        variance(*items[i + 1])
                    norm(i)
                    if rnd == passes - 1 and c:
                        take(c - 1)
                take(len(chunks) - 1)

            @block.sync
            def _(sp):
                for dst, src in loads:
                    sp.dma_start(dst, src).then_inc(loaded, 16)
                if loads:
                    sp.wait_ge(loaded, 16 * len(loads))
                if row is not None:
                    sp.wait_ge(row_taken, len(tgroups))
                    sp.dma_start(row[3], row[2]).then_inc(row_stored, 16)
                    sp.wait_ge(row_stored, 16)

            @block.gpsimd
            def _(pool):
                for i, (rnd, c) in enumerate(items):
                    t0, k = chunks[c]
                    pool.wait_ge(var_ready, i + 1)
                    nc.gpsimd.tensor_tensor(M[:, 5, t0:t0 + k], M[:, 4, t0:t0 + k], K.NEG_HALF[:, 0:k], ALU.pow)\
                        .then_inc(rstd_ready, 1)

            @block.tensor
            def _(pe):
                for c in range(len(chunks)):
                    pe.wait_ge(normed, c + 1)
                    for g, t, k in ending_in(tgroups, c):
                        if g >= 3:
                            pe.wait_ge(xt_ready, g - 2)
                        for j in range(k):
                            last = nc.tensor.transpose(K.PS[:, g % 3, j * P:(j + 1) * P], K.XN[:, t + j, :], K.IDENT[:])
                        last.then_inc(transposed, 1)
                    for g, t, k in ending_in(pgroups, c):
                        pe.wait_ge(xt_ready, (t + k - 1) // 4 + 1)
                        if g >= 4:
                            pe.wait_ge(taken, g - 3)
                        for j in range(k):
                            last = nc.tensor.matmul(K.PS[:, 4 + g % 4, j * n:(j + 1) * n],
                                                    K.XT[:, (t + j) * P:(t + j + 1) * P], W, start=True, stop=True)
                        last.then_inc(projected, 1)
                    if row is not None:
                        m = row[0].shape[1]
                        for g, t, k in ending_in(tgroups, c):
                            pe.wait_ge(xt_ready, g + 1)
                            if g:
                                pe.wait_ge(row_taken, g)
                            nc.tensor.matmul(K.PS[0:m, 3, 0:k * P], row[0], K.XT[:, t * P:(t + k) * P],
                                             start=True, stop=True).then_inc(row_done, 1)

            @block.scalar
            def _(act):
                for c in range(len(chunks)):
                    for g, t, k in ending_in(tgroups, c):
                        act.wait_ge(transposed, g + 1)
                        out, ps = K.XT[:, t * P:(t + k) * P], K.PS[:, g % 3, 0:k * P]
                        if affine:
                            nc.scalar.activation(out, ps, ACT.Identity, bias=K.GB[:, 1:2], scale=K.GB[:, 0:1])\
                                .then_inc(xt_ready, 1)
                        else:
                            nc.scalar.activation(out, ps, ACT.Copy).then_inc(xt_ready, 1)
                    if row is not None:
                        m = row[0].shape[1]
                        for g, t, k in ending_in(tgroups, c):
                            act.wait_ge(row_done, g + 1)
                            nc.scalar.activation(row[2][0:m, t * P:(t + k) * P], K.PS[0:m, 3, 0:k * P], ACT.Identity,
                                                 bias=row[1], scale=1.0).then_inc(row_taken, 1)


def global_max(nc, eng_link, v, pe_done, ready, d, n, K, tmp):
    link = eng_link
    nc.vector.tensor_reduce(tmp.PM[:, 0:n], d, AX.X, ALU.max).then_inc(ready, 1)
    v.wait_ge(pe_done, 1)
    link(nc.vector.tensor_reduce(tmp.G8[0:n, :], K.PS[0:n, 0, 0:P], AX.X, ALU.max))
    nc.vector.tensor_scalar(tmp.DG[0:n, 0:n], K.IDENT[0:n, 0:n], tmp.G8[0:n, 0:1], None, ALU.mult).then_inc(ready, 1)
    v.wait_ge(pe_done, 2)
    link(nc.vector.tensor_copy(tmp.GB[:, 0:n], K.PS[:, 1, 0:n]))


def global_max_products(nc, pe, pe_done, ready, n, K, tmp):
    pe.wait_ge(ready, 1)
    nc.tensor.transpose(K.PS[0:n, 0, 0:P], tmp.PM[:, 0:n], K.IDENT[:]).then_inc(pe_done, 1)
    pe.wait_ge(ready, 2)
    nc.tensor.matmul(K.PS[:, 1, 0:n], K.ONES[0:n, :], tmp.DG[0:n, 0:n], start=True, stop=True).then_inc(pe_done, 1)


def max_buffers(sb, n):
    tmp = Core()
    tmp.PM, tmp.G8 = sb("pm", [P, n], F32), sb("g8", [n, 1], F32)
    tmp.DG, tmp.GB = sb("dg", [n, n], F32), sb("gb", [P, n], F32)
    return tmp


def split_stage(nc, K, name, HP, heads, hd, score_col, sets, XS, V, coef=None, keep=None, store=None):
    ctx, sb, sem = open_stage(nc, name)
    with ctx:
        tmp = max_buffers(sb, heads)
        DM = sb("dm", [P, heads, T], F32)
        EX = sb("ex", [P, len(sets), T, heads], F32)
        Y = sb("y", [P, 4, T, heads], F32) if coef else None
        ready, pe_done, dve = sem("ready"), sem("pe_done"), sem("dve")
        dm_ready, ex_ready, y_ready, coef_ready = sem("dm_ready"), sem("ex_ready"), sem("y_ready"), sem("coef_ready")
        v_ready, part_ready, stored = sem("v_ready"), sem("part_ready"), sem("stored")
        H4 = HP[:, :, 0:heads * hd].rearrange("p t (h c) -> p t h c", c=hd)
        D = HP[:, :, score_col:score_col + heads]
        halves = (slice(0, HALF), slice(HALF, T))
        with nc.Block() as block:

            @block.sync
            def _(sp):
                if store is not None:
                    sp.dma_start(*store).then_inc(stored, 16)
                    sp.wait_ge(stored, 16)

            @block.tensor
            def _(pe):
                global_max_products(nc, pe, pe_done, ready, heads, K, tmp)

            @block.vector
            def _(v):
                link = Link(v, dve)
                global_max(nc, link, v, pe_done, ready, D.rearrange("p t h -> p h t"), heads, K, tmp)
                nc.vector.tensor_tensor(DM[:].rearrange("p h t -> p t h"), D, bcast_mid(tmp.GB[:, 0:heads], T),
                                        ALU.subtract).then_inc(dm_ready, 1)
                if coef:
                    S = HP[:, :, score_col - heads:score_col]
                    link(nc.vector.tensor_tensor(Y[:, 0], S, bcast_mid(tmp.GB[:, 0:heads], T), ALU.add))
                    link(nc.vector.scalar_tensor_tensor(Y[:, 1], Y[:, 0], SLOPE, Y[:, 0], ALU.mult, ALU.max))
                    link(nc.vector.tensor_tensor(Y[:, 2], Y[:, 0], Y[:, 1], ALU.subtract))
                    nc.vector.scalar_tensor_tensor(Y[:, 3], Y[:, 0], SLOPE, Y[:, 1], ALU.mult, ALU.subtract)\
                        .then_inc(y_ready, 1)
                if keep is not None:
                    nc.vector.tensor_copy(keep[:], D)
                for k in range(len(sets)):
                    v.wait_ge(ex_ready, k + 1)
                    for half, ts in enumerate(halves):
                        if k:
                            v.wait_ge(part_ready, 6 * k - 1 + half)
                        nc.vector.tensor_copy(V[:, ts, :, hd], EX[:, k, ts])
                        nc.vector.tensor_tensor(V[:, ts, :, 0:hd], H4[:, ts],
                                                bcast_last(EX[:, k, ts].rearrange("p t h -> p (t h)"), hd)
                                                .rearrange("p (t h) c -> p t h c", t=HALF), ALU.mult).then_inc(v_ready, 1)
                    for part in range(2):
                        for half, ts in enumerate(halves):
                            v.wait_ge(part_ready, 6 * k + 2 * part + half + 1)
                            nc.vector.tensor_tensor(V[:, ts], V[:, ts], XS[k](part)[:, ts], ALU.subtract).then_inc(v_ready, 1)

            @block.scalar
            def _(act):
                act.wait_ge(dm_ready, 1)
                for k, slope in enumerate(sets):
                    nc.scalar.activation(EX[:, k], DM[:].rearrange("p h t -> p t h"), ACT.Exp, scale=slope)\
                        .then_inc(ex_ready, 1)
                if coef:
                    act.wait_ge(y_ready, 1)
                    nc.scalar.activation(coef[0], Y[:, 2].rearrange("p (a t) h -> p a t h", a=2), ACT.Exp)
                    nc.scalar.activation(coef[1], Y[:, 3].rearrange("p (a t) h -> p a t h", a=2), ACT.Exp)
                for k in range(len(sets)):
                    for part in range(3):
                        for half, ts in enumerate(halves):
                            act.wait_ge(v_ready, 6 * k + 2 * part + half + 1)
                            nc.scalar.activation(XS[k](part)[:, ts], V[:, ts], ACT.Copy).then_inc(part_ready, 1)


def edge_sum_stage(nc, K, name, moving, n, finish, links, bufs=None, adj=None, landing=None, store=None):
    ctx, sb, sem = open_stage(nc, name)
    with ctx:
        adj_in, edges_made = [sem("adj_in0"), sem("adj_in1")], sem("edges_made")
        ED = sb("edges", [P, 2, T, P], U8)
        TMP = bufs(sb) if bufs else None
        staged, summed, sum_free, dve = sem("staged"), sem("summed"), sem("sum_free"), sem("dve")
        passed, stored = sem("passed"), sem("stored")
        with nc.Block() as block:

            @block.sync
            def _(sp):
                if adj is not None:
                    sp.dma_start(*store).then_inc(stored, 16)
                    with sp.Fori(0, T // 2) as t:
                        for q in range(2):
                            sp.wait_ge(edges_made, 2 * t + q + 1)
                            sp.dma_start(landing[q], adj[bass.ds(2 * t + q, 1), :, :]
                                         .rearrange("a p (b i) -> p (a b) i", i=P)).then_inc(adj_in[q], 16)
                    sp.wait_ge(stored, 16)

            @block.scalar
            def _(act):
                with act.Fori(0, T // 2) as t:
                    for q in range(2):
                        if adj is not None:
                            act.wait_ge(edges_made, 2 * t + q + 3)
                        act.wait_ge(summed, 2 * t + q + 1)
                        nc.scalar.activation(
                            ED[:, q].rearrange("p b i -> p (b i)").bitcast(U16),
                            K.EDGE[:, bass.ds(2 * t + q, 1)].rearrange("p a b i -> p (a b i)").bitcast(U16),
                            ACT.Copy).then_inc(staged, 1)

            @block.tensor
            def _(pe):
                with pe.Fori(0, T // 2) as t:
                    for q in range(2):
                        pe.wait_ge(staged, 2 * t + q + 1)
                        pe.wait_ge(sum_free, 2 * t + q + 1)
                        pe.sem_inc(passed, 1)
                        for j in range(T):
                            last = nc.tensor.matmul(K.PS[:, q, 0:n], ED[:, q, j, :].bitcast(FP8), moving(j),
                                                    start=(j == 0), stop=(j == T - 1))
                        last.then_inc(summed, 1)

            @block.vector
            def _(v):
                link = Link(v, dve)
                v.sem_inc(sum_free, 2)
                v.sem_inc(summed, 2)
                v.sem_inc(edges_made, 2)

                def make_edges(it, q, loads):
                    v.wait_ge(adj_in[q], loads)
                    nc.vector.tensor_scalar(K.EDGE[:, bass.ds(it, 1), :, :].rearrange("p a b i -> p (a b i)"),
                                            landing[q].rearrange("p b i -> p (b i)"),
                                            float(ONE8), None, ALU.mult).then_inc(edges_made, 1)

                if adj is not None:
                    make_edges(0, 0, 16)
                    with v.Fori(0, T // 2 - 1) as t:
                        for q in range(2):
                            make_edges(2 * t + q + 1, 1 - q, 16 * t + 16 * q + 16)
                            v.wait_ge(summed, 2 * t + q + 3)
                            v.wait_ge(sum_free, 2 * t + q + 2)
                            finish(v, link, 2 * t + q, K.PS[:, q, 0:n], 2 * links * t, sum_free, TMP)
                    make_edges(T - 1, 1, 8 * T)
                    for q in range(2):
                        v.wait_ge(summed, T - 2 + q + 3)
                        v.wait_ge(sum_free, T - 2 + q + 2)
                        finish(v, link, T - 2 + q, K.PS[:, q, 0:n], 0, sum_free, TMP)
                    return
                with v.Fori(0, T // 2) as t:
                    for q in range(2):
                        v.wait_ge(summed, 2 * t + q + 3)
                        v.wait_ge(sum_free, 2 * t + q + 2)
                        finish(v, link, 2 * t + q, K.PS[:, q, 0:n], 2 * links * t, sum_free, TMP)
                link.skip(2 * links * (T // 2 - 1))


def head_loop_stage(nc, K, XD, SD, XN0, D0, C1, C2, A0, RES):
    ctx, sb, sem = open_stage(nc, "head_loop")
    with ctx:
        RING, MRING = 8, 6
        back, mback = ([ring_distance(g, 2 * T, ring) for g in range(2 * T)] for ring in (RING, MRING))
        N_ACT = 15
        ON_ACT = [j for j in range(T) if (j * N_ACT) % T < N_ACT]
        EVAC_AT, COMB_AT, FIN_AT = 10, 12, 18
        BIAS_AT = 6
        C = 6 * HC
        SB = sb("scores", [P, 2, HN], F32)
        XH = sb("parts", [P, 2, T, C], BF16)
        ST = sb("step", [P, RING, HN], U8)
        ME = sb("masked", [P, MRING, HN], U8)
        EV = sb("sums", [C, HN], F32)
        T1 = sb("t1", [P, HALF, HC], F32)
        T2 = sb("t2", [P, HALF, HC], F32)
        ND = sb("negd", [P, T, HEADS], F32)
        BD = sb("bigd", [P, T, HEADS + 1], F32)
        BT = sb("turn_bigd", [P, 2, T], F32)
        in_x, in_s = [sem("in_x0"), sem("in_x1")], [sem("in_s0"), sem("in_s1")]
        consts, compared, masked, summed = sem("consts"), sem("compared"), sem("masked"), sem("summed")
        turn_done, evacuated, combined, finished, dve = (sem("turn_done"), sem("evacuated"), sem("combined"),
                                                         sem("finished"), sem("dve"))
        passed, sent, bias_ready = sem("passed"), sem("sent"), sem("bias_ready")
        go, reloaded = sem("go"), sem("reloaded")
        M0, S0 = 2 * T, 2 * N_ACT
        U0 = M0
        pieces = [(512 * b, min(512, HN - 512 * b)) for b in range(4)]

        def banks(q):
            return K.PS[:, 4 * q:4 * q + 4, :].rearrange("p b n -> p (b n)")

        def evacuate(act, q, n):
            act.wait_ge(turn_done, n + 2)
            act.wait_ge(combined, n + 1)
            nc.scalar.activation(EV[:], banks(q)[0:C, 0:HN], ACT.Copy).then_inc(evacuated, 1)

        def combine(pe, q, n):
            pe.wait_ge(evacuated, n + 1)
            for i in range(HALF):
                last = nc.tensor.matmul(K.PS[:, 4 * q + 3, i * 2 * HC:(i + 1) * 2 * HC], EV[:, i * P:(i + 1) * P],
                                        K.COMB[0:C, :], start=True, stop=True)
            last.then_inc(combined, 1)

        def finish(v, link, q, n, slot, base):
            v.wait_ge(combined, n + 2)
            sums = K.PS[:, 4 * q + 3, 0:HALF * 2 * HC].rearrange("p (t c) -> p t c", c=2 * HC)
            c1, c2 = (bcast_last(c[:, slot, :].rearrange("p a t -> p (a t)"), HC) for c in (C1, C2))
            a0, res = (a[:, slot, :, :].rearrange("p a t c -> p (a t) c") for a in (A0, RES))
            nc.vector.tensor_tensor(T1[:], sums[:, :, 0:HC], c1, ALU.mult)
            link(nc.vector.tensor_tensor(T2[:], a0, sums[:, :, HC:2 * HC], ALU.subtract), base)
            link(nc.vector.tensor_tensor(T2[:], T2[:], c2, ALU.mult), base)
            nc.vector.tensor_tensor(res, T1[:], T2[:], ALU.add).then_inc(finished, 1)

        with nc.Block() as block:

            @block.sync
            def _(sp):
                sp.dma_start(K.XN[:], XN0).then_inc(reloaded, 16)
                sp.wait_ge(reloaded, 16)
                with sp.Fori(0, 2) as half:
                    with sp.Fori(0, HEADS // 2) as pair:
                        for q in range(2):
                            n = 8 * half + 2 * pair + q
                            sp.wait_ge(compared, N_ACT * n + N_ACT)
                            sp.sem_inc(sent, 1)
                            sp.wait_ge(masked, T * n + T)
                            sp.sem_inc(sent, 1)
                            sp.wait_ge(turn_done, n + 1)
                            sp.sem_inc(sent, 1)
                            sp.dma_start(XH[:, q, :, :],
                                         XD[:, :, bass.ds(2 * pair + q, 1), :].rearrange("p t a c -> p t (a c)")).then_inc(in_x[q], 16)
                            sp.dma_start(SB[:, q, :], SD[bass.ds(2 * pair + q, 1), bass.ds(HN * half, HN)]
                                         .rearrange("a n -> (a n)").partition_broadcast(P)).then_inc(in_s[q], 16)

            @block.scalar
            def _(act):
                act.wait_ge(consts, 2)
                with act.Fori(0, 2) as half:
                    with act.Fori(0, HEADS // 2) as pair:
                        w = 4 * half + pair
                        for q in range(2):
                            act.wait_ge(bias_ready, 2 * w + q + 1)
                            act.wait_ge(in_s[q], 16 * w + 16)
                            act.sem_inc(go, 1)
                            for j in range(T):
                                if j == EVAC_AT:
                                    evacuate(act, 1 - q, 2 * w + q)
                                if j in ON_ACT:
                                    slot = (T * q + j) % RING
                                    act.wait_ge(masked, 2 * T * w + (T * q + j + 1 + M0 - back[T * q + j]))
                                    act.sem_inc(go, 1)
                                    nc.scalar.activation(ST[:, slot, :].bitcast(FP8), SB[:, q, :], ACT.Sigmoid,
                                                         bias=BT[:, q, j:j + 1], scale=BIG,
                                                         saturate=False).then_inc(compared, 1)
                evacuate(act, 1, 2 * HEADS)

            @block.vector
            def _(v):
                link = Link(v, dve)
                for k, prime in ((S0, compared), (M0, masked), (U0, summed), (2, turn_done), (1, combined),
                                 (1, finished)):
                    v.sem_inc(prime, k)
                nc.vector.memset(K.PS[:, 4:8, :], 0.0).then_inc(consts, 1)
                nc.vector.tensor_scalar(BD[:, :, 0:HEADS], D0, BIG, None, ALU.mult)
                nc.vector.tensor_scalar(BD[:, :, HEADS], D0[:, :, 0], BIG, None, ALU.mult).then_inc(consts, 1)
                nc.vector.tensor_scalar(BT[:, 0, :], D0[:, :, 0], BIG, None, ALU.mult).then_inc(bias_ready, 1)
                v.wait_ge(consts, 2)
                link(nc.vector.tensor_scalar(ND[:], D0, -1.0, None, ALU.mult))
                links = 2 * (T - N_ACT + 2)

                with v.Fori(0, 2) as half:
                    with v.Fori(0, HEADS // 2) as pair:
                        w = 4 * half + pair
                        for q in range(2):
                            made = {}

                            def mask(j):
                                slot = (T * q + j) % RING
                                if j in ON_ACT:
                                    v.wait_ge(compared, 2 * N_ACT * w + (N_ACT * q + ON_ACT.index(j) + 1 + S0))
                                else:
                                    v.wait_ge(dve, links * w + made[j])
                                v.wait_ge(summed, 2 * T * w + (T * q + j + 1 + U0 - mback[T * q + j]))
                                nc.vector.tensor_tensor(
                                    ME[:, (T * q + j) % MRING, :].rearrange("p (t i) -> p t i", i=P).bitcast(U32),
                                    ST[:, slot, :].rearrange("p (t i) -> p t i", i=P).bitcast(U32),
                                    K.EDGE[:, bass.ds(HALF * half, HALF), j, :].bitcast(U32),
                                    ALU.bitwise_and).then_inc(masked, 1)

                            v.wait_ge(in_s[q], 16 * w + 16)
                            for j in range(T):
                                if j == BIAS_AT:
                                    nc.vector.tensor_scalar(BT[:, 1 - q, :], BD[:, :, bass.ds(2 * pair + q + 1, 1)]
                                                            .rearrange("p t a -> p (t a)"), 1.0, None, ALU.mult)\
                                        .then_inc(bias_ready, 1)
                                if j == FIN_AT:
                                    n = 2 * w + q
                                    finish(v, link, 1 - q, n, bass.ds(n, 1), links * w)
                                if j not in ON_ACT:
                                    v.wait_ge(masked, 2 * T * w + (T * q + j + 1 + M0 - back[T * q + j]))
                                    nc.vector.tensor_scalar(ST[:, (T * q + j) % RING, :], SB[:, q, :],
                                                            ND[:, j, bass.ds(2 * pair + q, 1)], float(ONE8),
                                                            ALU.is_ge, ALU.mult).then_inc(dve, 1)
                                    link.n += 1
                                    made[j] = link.n
                                if j >= 1:
                                    mask(j - 1)
                            mask(T - 1)
                link.skip(links * 7)
                finish(v, link, 1, 2 * HEADS, slice(2 * HEADS, 2 * HEADS + 1), 0)

            @block.tensor
            def _(pe):
                with pe.Fori(0, 2 * HEADS // 2) as w:
                    for q in range(2):
                        pe.wait_ge(in_x[q], 16 * w + 16)
                        pe.wait_ge(finished, 2 * w + q + 1)
                        for j in range(T):
                            if j == COMB_AT:
                                combine(pe, 1 - q, 2 * w + q)
                            slot = (T * q + j) % MRING
                            pe.wait_ge(masked, 2 * T * w + (T * q + j + 1 + M0))
                            pe.sem_inc(passed, 1)
                            for b, (at, n) in enumerate(pieces):
                                last = nc.tensor.matmul(K.PS[0:C, 4 * q + b, 0:n], XH[:, q, j, :],
                                                        ME[:, slot, at:at + n].bitcast(FP8),
                                                        start=(j == 0), stop=(j == T - 1))
                            last.then_inc(summed, 1)
                        pe.wait_ge(summed, 2 * T * w + (T * q + T + U0))
                        nc.tensor.sem_inc(turn_done, 1)
                combine(pe, 1, 2 * HEADS)


def head_merge_stage(nc, K, RES):
    ctx, sb, sem = open_stage(nc, "head_merge")
    with ctx:
        RD = sb("rden", [P, 16, HALF], F32)
        H = sb("h", [P, T, P], F32)
        E = sb("e", [P, T, P], F32)
        dve, low, expd = sem("dve"), sem("low"), sem("expd")
        with nc.Block() as block:

            @block.vector
            def _(v):
                link = Link(v, dve)
                link(nc.vector.tensor_scalar(RD[:], RES[:, 1:17, :, HD], TINY, None, ALU.max))
                link(nc.vector.reciprocal(RD[:], RD[:]))
                for half in range(2):
                    ts = slice(HALF * half, HALF * (half + 1))
                    for h in range(HEADS):
                        n = 8 * half + h
                        last = nc.vector.tensor_tensor(H[:, ts, HD * h:HD * (h + 1)], RES[:, 1 + n, :, 0:HD],
                                                       bcast_last(RD[:, n, :], HD), ALU.mult)
                    link(last)
                    link(nc.vector.tensor_tensor(H[:, ts, :], H[:, ts, :], K.XN[:, ts, :], ALU.add))
                    nc.vector.tensor_scalar(E[:, ts, :], H[:, ts, :], 0.0, None, ALU.min).then_inc(low, 1)
                for half in range(2):
                    ts = slice(HALF * half, HALF * (half + 1))
                    v.wait_ge(expd, half + 1)
                    link(nc.vector.scalar_tensor_tensor(H[:, ts, :], H[:, ts, :], 0.0, E[:, ts, :], ALU.max, ALU.add))
                    link(nc.vector.scalar_tensor_tensor(K.X[:, ts, :], H[:, ts, :], 1.0, K.X[:, ts, :],
                                                        ALU.subtract, ALU.add))

            @block.scalar
            def _(act):
                for half in range(2):
                    ts = slice(HALF * half, HALF * (half + 1))
                    act.wait_ge(low, half + 1)
                    nc.scalar.activation(E[:, ts, :], E[:, ts, :], ACT.Exp).then_inc(expd, 1)


def layer0_gnn(nc, K, D):
    ctx = ExitStack()
    with ctx:
        sb = lambda n, shape, dt: ctx.enter_context(nc.sbuf_tensor(f"g0_{n}", shape, dt))
        A0 = sb("a0", [P, 17, HALF, HC], F32)
        C1 = sb("c1", [P, 17, HALF], F32)
        C2 = sb("c2", [P, 17, HALF], F32)
        D0 = sb("d0", [P, T, HEADS], F32)
        flat = A0[:].rearrange("p a t c -> p (a t c)")
        HP = flat[:, 0:T * 144].rearrange("p (t c) -> p t c", c=144)
        xt = K.XT[:]
        V = xt[:, 0:T * HEADS * HC].rearrange("p (t h c) -> p t h c", h=HEADS, c=HC)
        NAT = xt[:, 0:T * HEADS * HC].rearrange("p (t h c) -> p t h c", h=HEADS, c=HC)
        RES = xt[:, 0:17 * HALF * HC].rearrange("p (a t c) -> p a t c", t=HALF, c=HC)
        inner = ExitStack()
        with inner:
            XALL = inner.enter_context(nc.sbuf_tensor("g0_xall", [P, T, HEADS, 6 * HC], BF16))
            SROW = XALL[0:HEADS, :, :, :].rearrange("p t h c -> p (t h c)")[:, 0:2 * NP].bitcast(F32)
            norm_project_stage(nc, K, "p0", K.WP0[:], 144, 3, lambda t, k: HP[:, t:t + k, :], bias=K.BP0[:],
                               row=(K.WP0[:, P:P + HEADS], K.SB8[:], SROW, D["sd"]))

            def parts(k):
                return lambda s: XALL[:, :, :, (3 * k + s) * HC:(3 * k + s + 1) * HC]

            def natural(c):
                return c[:, 1:17, :].rearrange("p (a h) t -> p a t h", a=2)

            split_stage(nc, K, "x0", HP, HEADS, HD, P + HEADS, (1.0, SLOPE), (parts(0), parts(1)), V,
                        coef=(natural(C1), natural(C2)), keep=D0, store=(D["xn0"], K.XN[:]))

            def sum_parts(v, link, it, ps, base, done, tmp):
                nc.vector.tensor_reduce(NAT[:, bass.ds(it, 1), :, :].rearrange("p a h c -> p (a h) c"),
                                        ps.rearrange("p (h s c) -> p h c s", h=HEADS, s=3), AX.X, ALU.add).then_inc(done, 1)

            edge_sum_stage(nc, K, "a0", lambda j: XALL[:, j, :, 3 * HC:6 * HC], 3 * HEADS * HC, sum_parts, 0,
                           adj=D["adj"], store=(D["xd"], XALL[:]), landing=[b.rearrange("p (b i) -> p b i", i=P).bitcast(I32) for b in
                                                  (K.XN[:].rearrange("p t d -> p (t d)"), flat[:, 0:NP])])
        reorder_stage(nc, K, NAT, A0, C1, C2)
        head_loop_stage(nc, K, D["xd"], D["sd"], D["xn0"], D0[:], C1, C2, A0, RES)
        head_merge_stage(nc, K, RES)


def reorder_stage(nc, K, NAT, A0, C1, C2):
    ctx, sb, sem = open_stage(nc, "reorder")
    with ctx:
        with nc.Block() as block:

            @block.vector
            def _(v):
                for half in range(2):
                    for h in range(HEADS):
                        nc.vector.tensor_copy(A0[:, 1 + 8 * half + h, :, :], NAT[:, HALF * half:HALF * (half + 1), h, :])
                for a in (A0[:, 0, :, :], C1[:, 0, :], C2[:, 0, :]):
                    nc.vector.memset(a, 0.0)


def cosine_prepare_stage(nc, K, QK, QT, KT):
    ctx, sb, sem = open_stage(nc, "cos_prep")
    with ctx:
        COS_EPS = 1e-4
        SS = sb("ss", [P, 2, 2 * T], F32)
        HALF_ = sb("half", [P, 2 * T], F32)
        SQ = sb("sq", [P, T, 2 * P], F32)
        squared, ss_ready, norm_ready, normed = sem("squared"), sem("ss_ready"), sem("norm_ready"), sem("normed")
        transposed, act_taken, dve_taken, dve = sem("transposed"), sem("act_taken"), sem("dve_taken"), sem("dve")
        consts = sem("consts")
        groups = [(m, t, min(4, T - t)) for t in range(0, T, 4) for m in range(2)]
        with nc.Block() as block:

            @block.scalar
            def _(act):
                for h in range(2):
                    ts = slice(HALF * h, HALF * (h + 1))
                    nc.scalar.activation(SQ[:, ts, :], QK[:, ts, :], ACT.Square).then_inc(squared, 1)
                for g, (m, t, k) in enumerate(groups):
                    if m == 0:
                        act.wait_ge(transposed, g + 1)
                        nc.scalar.activation(QT[:, t * P:(t + k) * P], K.PS[:, g % 8, 0:k * P], ACT.Copy)\
                            .then_inc(act_taken, 1)

            @block.gpsimd
            def _(pool):
                nc.gpsimd.memset(HALF_[:], 0.5).then_inc(consts, 1)
                pool.wait_ge(consts, 1)
                pool.wait_ge(ss_ready, 1)
                nc.gpsimd.tensor_tensor(SS[:, 1, :], SS[:, 0, :], HALF_[:], ALU.pow).then_inc(norm_ready, 1)

            @block.vector
            def _(v):
                link = Link(v, dve)
                ss = SS[:, 0, :].rearrange("p (t m) -> p t m", m=2)
                for h in range(2):
                    ts = slice(HALF * h, HALF * (h + 1))
                    v.wait_ge(squared, h + 1)
                    last = nc.vector.tensor_reduce(ss[:, ts, :], SQ[:, ts, :].rearrange("p t (m c) -> p t m c", m=2),
                                                   AX.X, ALU.add)
                last.then_inc(ss_ready, 1)
                v.wait_ge(norm_ready, 1)
                link(nc.vector.tensor_scalar(SS[:, 1, :], SS[:, 1, :], COS_EPS, None, ALU.max))
                link(nc.vector.reciprocal(SS[:, 1, :], SS[:, 1, :]))
                inv = SS[:, 1, :].rearrange("p (t m) -> p t m", m=2)
                for h in range(2):
                    ts = slice(HALF * h, HALF * (h + 1))
                    for m in range(2):
                        last = nc.vector.tensor_tensor(QK[:, ts, m * P:(m + 1) * P], QK[:, ts, m * P:(m + 1) * P],
                                                       bcast_last(inv[:, ts, m], P), ALU.mult)
                    last.then_inc(normed, 1)
                for g, (m, t, k) in enumerate(groups):
                    if m == 1:
                        v.wait_ge(transposed, g + 1)
                        nc.vector.tensor_copy(KT[:, t * P:(t + k) * P], K.PS[:, g % 8, 0:k * P]).then_inc(dve_taken, 1)

            @block.tensor
            def _(pe):
                for g, (m, t, k) in enumerate(groups):
                    pe.wait_ge(normed, 1 if t + k <= HALF else 2)
                    if g >= 8:
                        pe.wait_ge((act_taken, dve_taken)[m], (g - 8) // 2 + 1)
                    for j in range(k):
                        last = nc.tensor.transpose(K.PS[:, g % 8, j * P:(j + 1) * P], QK[:, t + j, m * P:(m + 1) * P],
                                                   K.IDENT[:])
                    last.then_inc(transposed, 1)


def ring_distance(g, steps, ring):
    if g >= ring:
        return ring
    return steps - ((steps - 1 - g) // ring) * ring


def cosine_stage(nc, K, QT, KT, X1):
    ctx, sb, sem = open_stage(nc, "cosine")
    with ctx:
        RING, STEPS, TURNS, LAG = 5, T // 2, T // 2, 2
        PB = sb("probs", [P, RING, 4 * P], F32)
        PA = sb("masked", [P, RING, 4 * P], F32)
        NUM = sb("num", [P, 2, P + 1], F32)
        S = sb("s", [P, 3, 2], F32)
        TM = sb("tm", [P, 2, P], F32)
        ready, scored, expd, masked, summed = sem("ready"), sem("scored"), sem("expd"), sem("masked"), sem("summed")
        taken, scales, added, dve, pool_own = sem("taken"), sem("scales"), sem("added"), sem("dve"), sem("pool_own")
        PRIME = STEPS
        back = [ring_distance(g, STEPS, RING) for g in range(STEPS)]
        with nc.Block() as block:

            @block.scalar
            def _(act):
                with act.Fori(0, TURNS) as c:
                    for g in range(STEPS):
                        act.wait_ge(scored, STEPS * c + g + 1)
                        act.wait_ge(masked, STEPS * c + (g + 1 - back[g] + PRIME))
                        nc.scalar.activation(PB[:, g % RING, :], K.PS[:, g % RING, :], ACT.Exp).then_inc(expd, 1)

            @block.vector
            def _(v):
                v.sem_inc(masked, PRIME)
                v.sem_inc(summed, PRIME)
                v.sem_inc(taken, 1)
                v.sem_inc(added, 1)
                link = Link(v, dve)
                nc.vector.tensor_copy(X1[:, :, 0:P], K.XN[:])
                nc.vector.memset(X1[:, :, P:P + 1], 1.0)
                nc.vector.memset(KT[:, NP:NP + 2 * P], 0.0).then_inc(ready, 1)
                v.wait_ge(ready, 1)
                v.sem_inc(ready, 1)

                def mask(c, g):
                    v.wait_ge(expd, STEPS * c + g + 1)
                    v.wait_ge(summed, STEPS * c + (g + 1 - back[g] + PRIME))
                    nc.vector.scalar_tensor_tensor(
                        PA[:, g % RING, :].rearrange("p (a n) -> p a n", a=2),
                        K.EDGE[:, bass.ds(2 * c, 2), 2 * g:2 * g + 2, :].rearrange("p a b i -> p a (b i)"), 1.0,
                        PB[:, g % RING, :].rearrange("p (a n) -> p a n", a=2), ALU.min, ALU.mult).then_inc(masked, 1)

                def take(c):
                    v.wait_ge(summed, STEPS * c + STEPS + PRIME)
                    v.wait_ge(added, c + 1)
                    nc.vector.tensor_copy(NUM[:], K.PS[:, 5:7, 0:P + 1]).then_inc(taken, 1)

                def scale(c, base):
                    v.wait_ge(taken, c + 2)
                    link(nc.vector.tensor_scalar(S[:, 0, :], NUM[:, :, P], TINY, None, ALU.max), base)
                    link(nc.vector.reciprocal(S[:, 0, :], S[:, 0, :]), base)
                    link(nc.vector.tensor_scalar(S[:, 2, :], NUM[:, :, P], 0.0, -0.5, ALU.is_gt, ALU.mult), base)
                    nc.vector.tensor_scalar(S[:, 0, :], S[:, 0, :], 0.5, None, ALU.mult).then_inc(scales, 1)
                    nc.vector.tensor_scalar(S[:, 1, :], S[:, 2, :], 1.0, None, ALU.add).then_inc(scales, 1)

                for g in range(2):
                    mask(0, g)
                with v.Fori(0, TURNS - 1) as c:
                    for g in range(2, STEPS):
                        mask(c, g)
                    mask(c + 1, 0)
                    take(c)
                    mask(c + 1, 1)
                    scale(c, 3 * c)
                link.skip(3 * (TURNS - 2))
                for g in range(2, STEPS):
                    mask(TURNS - 1, g)
                take(TURNS - 1)
                scale(TURNS - 1, 0)

            @block.gpsimd
            def _(pool):
                link = Link(pool, pool_own)
                with pool.Fori(0, TURNS) as c:
                    pool.wait_ge(scales, 2 * c + 2)
                    link(nc.gpsimd.tensor_tensor(NUM[:, :, 0:P], NUM[:, :, 0:P], bcast_last(S[:, 0, :], P), ALU.mult), 3 * c)
                    link(nc.gpsimd.tensor_tensor(TM[:], K.XN[:, bass.ds(2 * c, 2), :], bcast_last(S[:, 1, :], P), ALU.mult), 3 * c)
                    link(nc.gpsimd.tensor_tensor(TM[:], TM[:], NUM[:, :, 0:P], ALU.add), 3 * c)
                    nc.gpsimd.tensor_tensor(K.X[:, bass.ds(2 * c, 2), :], K.X[:, bass.ds(2 * c, 2), :], TM[:], ALU.add)\
                        .then_inc(added, 1)

            @block.tensor
            def _(pe):
                pe.wait_ge(ready, 2)

                def score(g, nodes):
                    for b in range(2):
                        last = nc.tensor.matmul(
                            K.PS[:, g % RING, :].rearrange("p (a b i) -> p b a i", a=2, b=2)[:, b],
                            QT[:, (2 * g + b) * P:(2 * g + b + 1) * P],
                            KT[:, nodes].rearrange("p (a i) -> p a i", a=2), start=True, stop=True)
                    last.then_inc(scored, 1)

                for g in range(LAG):
                    score(g, bass.ds(0, 2 * P))
                with pe.Fori(0, TURNS) as c:
                    for g in range(STEPS):
                        ahead = g + LAG
                        score(ahead % STEPS, bass.ds(2 * P * c + 2 * P * (ahead // STEPS), 2 * P))
                        if g == 0:
                            pe.wait_ge(taken, c + 1)
                        pe.wait_ge(masked, STEPS * c + (g + 1 + PRIME))
                        for a in range(2):
                            for b in range(2):
                                last = nc.tensor.matmul(
                                    K.PS[:, 5 + a, 0:P + 1], PA[:, g % RING, (2 * a + b) * P:(2 * a + b + 1) * P],
                                    X1[:, 2 * g + b, :], start=(g == 0 and b == 0), stop=(g == STEPS - 1 and b == 1))
                        last.then_inc(summed, 1)


def layer1_gnn(nc, K):
    ctx = ExitStack()
    with ctx:
        sb = lambda n, shape, dt: ctx.enter_context(nc.sbuf_tensor(f"g1_{n}", shape, dt))
        QT = sb("qt", [P, NP], F32)
        inner = ExitStack()
        with inner:
            QK = inner.enter_context(nc.sbuf_tensor("g1_qk", [P, T, 2 * P], F32))
            norm_project_stage(nc, K, "p1", K.WP1[:], 2 * P, 2, lambda t, k: QK[:, t:t + k, :])
            cosine_prepare_stage(nc, K, QK, QT, K.XT)
        X1 = sb("x1", [P, T, P + 1], F32)
        cosine_stage(nc, K, QT, K.XT, X1)


def add_softmax(v, link, nc, K, it, num, S, base, done):
    link(nc.vector.tensor_scalar(S[:, 0:1], num[:, P:P + 1], TINY, None, ALU.max), base)
    link(nc.vector.reciprocal(S[:, 1:2], S[:, 0:1]), base)
    x = K.X[:, bass.ds(it, 1), :].rearrange("p a d -> p (a d)")
    nc.vector.scalar_tensor_tensor(x, num[:, 0:P], S[:, 1:2], x, ALU.mult, ALU.add).then_inc(done, 1)


def layer2_gnn(nc, K):
    ctx = ExitStack()
    C = P + 1
    with ctx:
        sb = lambda n, shape, dt: ctx.enter_context(nc.sbuf_tensor(f"g2_{n}", shape, dt))
        XS = sb("xs", [P, T, 3 * C], BF16)
        inner = ExitStack()
        with inner:
            HP = inner.enter_context(nc.sbuf_tensor("g2_hp", [P, T, C], F32))
            norm_project_stage(nc, K, "p2", K.WP2[:], C, 3, lambda t, k: HP[:, t:t + k, :], bias=K.BP2[:])
            V = K.XT[:, 0:T * C].rearrange("p (t a c) -> p t a c", t=T, a=1)
            split_stage(nc, K, "x2", HP, 1, P, P, (1.0,),
                        (lambda s: XS[:, :, s * C:(s + 1) * C].unsqueeze(2),), V)

        def finish(v, link, it, ps, base, done, tmp):
            link(nc.vector.tensor_reduce(tmp[0][:], ps.rearrange("p (s c) -> p c s", s=3), AX.X, ALU.add), base)
            add_softmax(v, link, nc, K, it, tmp[0], tmp[1], base, done)

        edge_sum_stage(nc, K, "a2", lambda j: XS[:, j, :], 3 * C, finish, 3,
                       bufs=lambda sb: (sb("sum", [P, C], F32), sb("s", [P, 2], F32)))


def layer3_gnn(nc, K, D):
    ctx = ExitStack()
    C = P + 1
    with ctx:
        sb = lambda n, shape, dt: ctx.enter_context(nc.sbuf_tensor(f"g3_{n}", shape, dt))
        XF = sb("xs", [P, T * 6 * C], BF16)
        XS = XF[:].rearrange("p (t a c) -> p t a c", a=2, c=3 * C)
        C1 = sb("c1", [P, T, 1], F32)
        C2 = sb("c2", [P, T, 1], F32)
        D0 = sb("d0", [P, T, 1], F32)
        inner = ExitStack()
        with inner:
            HP = inner.enter_context(nc.sbuf_tensor("g3_hp", [P, T, P + 2], F32))
            SROW = XF[0:1, 0:2 * NP].bitcast(F32)
            norm_project_stage(nc, K, "p3", K.WP3[:], P + 2, 3, lambda t, k: HP[:, t:t + k, :], bias=K.BP3[:],
                               row=(K.WP3[:, P:P + 1], K.BP3[0:1, P:P + 1], SROW, D["sd3"]))
            V = K.XT[:, 0:T * C].rearrange("p (t a c) -> p t a c", t=T, a=1)

            def parts(k):
                return lambda s: XS[:, :, k, s * C:(s + 1) * C].unsqueeze(2)

            def natural(c):
                return c[:].rearrange("p (a t) h -> p a t h", a=2)

            split_stage(nc, K, "x3", HP, 1, P, P + 1, (1.0, SLOPE), (parts(0), parts(1)), V,
                        coef=(natural(C1), natural(C2)), keep=D0)
        signed_sum_stage(nc, K, D["sd3"], XS, C1, C2, D0)


def signed_sum_stage(nc, K, SD, XS, C1, C2, D0):
    ctx, sb, sem = open_stage(nc, "signed")
    with ctx:
        C = P + 1
        SB = sb("scores", [P, NP], F32)
        SN = sb("tile_scores", [P, 2, P], F32)
        ST = sb("above", [P, 2, T, P], U8)
        ED = sb("below", [P, 2, T, P], U8)
        ND = sb("negd", [P, T], F32)
        U = sb("u", [P, 2, C], F32)
        S = sb("s", [P, 2], F32)
        in_s, negd, staged, scores_in, parted = sem("in_s"), sem("negd"), sem("staged"), sem("scores_in"), sem("parted")
        summed, finished, dve, passed = sem("summed"), sem("finished"), sem("dve"), sem("passed")
        with nc.Block() as block:

            @block.sync
            def _(sp):
                sp.dma_start(SB[:], SD.rearrange("a n -> (a n)").partition_broadcast(P)).then_inc(in_s, 16)

            @block.scalar
            def _(act):
                act.wait_ge(in_s, 16)
                with act.Fori(0, T // 2) as t:
                    for q in range(2):
                        act.wait_ge(summed, 2 * t + q + 1)
                        nc.scalar.activation(ED[:, q].rearrange("p b i -> p (b i)").bitcast(U16),
                                             K.EDGE[:, bass.ds(2 * t + q, 1)].rearrange("p a b i -> p (a b i)").bitcast(U16),
                                             ACT.Copy).then_inc(staged, 1)
                        nc.scalar.activation(SN[:, q, :], SB[:, bass.ds(P * (2 * t + q), P)], ACT.Copy).then_inc(staged, 1)

            @block.vector
            def _(v):
                link = Link(v, dve)
                v.sem_inc(summed, 2)
                v.sem_inc(finished, 2)
                link(nc.vector.tensor_scalar(ND[:], D0[:, :, 0], -1.0, None, ALU.mult))

                def part(it, q, base):
                    v.wait_ge(staged, 2 * it + 2)
                    v.sem_inc(passed, 1)
                    link(nc.vector.tensor_tensor(ST[:, q].bitcast(FP8), bcast_mid(SN[:, q, :], T),
                                                 bcast_last(ND[:], P), ALU.is_ge, saturate=False), base)
                    st, ed = (x[:, q].rearrange("p b i -> p (b i)").bitcast(U32) for x in (ST, ED))
                    link(nc.vector.tensor_tensor(st, st, ed, ALU.bitwise_and), base)
                    nc.vector.tensor_tensor(ed, ed, st, ALU.bitwise_xor).then_inc(parted, 1)

                def finish(it, q, base):
                    v.wait_ge(summed, it + 3)
                    v.wait_ge(finished, it + 2)
                    for k in range(2):
                        link(nc.vector.tensor_reduce(U[:, k, :], K.PS[:, 2 * q + k, 0:3 * C].rearrange("p (s c) -> p c s", s=3),
                                                     AX.X, ALU.add), base)
                    c1, c2 = (c[:, bass.ds(it, 1), :].rearrange("p a b -> p (a b)") for c in (C1, C2))
                    link(nc.vector.tensor_scalar(U[:, 1, :], U[:, 1, :], c2, None, ALU.mult), base)
                    link(nc.vector.scalar_tensor_tensor(U[:, 0, :], U[:, 0, :], c1, U[:, 1, :], ALU.mult, ALU.add), base)
                    add_softmax(v, link, nc, K, it, U[:, 0, :], S, base, finished)

                per = 2 * (2 + 6)
                for q in range(2):
                    part(q, q, 0)
                with v.Fori(0, T // 2 - 1) as t:
                    for q in range(2):
                        finish(2 * t + q, q, per * t)
                        part(2 * t + q + 2, q, per * t)
                link.skip(per * (T // 2 - 2))
                for q in range(2):
                    finish(T - 2 + q, q, 0)

            @block.tensor
            def _(pe):
                with pe.Fori(0, T // 2) as t:
                    for q in range(2):
                        pe.wait_ge(parted, 2 * t + q + 1)
                        pe.wait_ge(finished, 2 * t + q + 1)
                        pe.sem_inc(passed, 1)
                        for j in range(T):
                            for k, e in enumerate((ST, ED)):
                                last = nc.tensor.matmul(K.PS[:, 2 * q + k, 0:3 * C], e[:, q, j, :].bitcast(FP8),
                                                        XS[:, j, k, :], start=(j == 0), stop=(j == T - 1))
                        last.then_inc(summed, 1)


def choose(nc, K, link, LG, E, best, onehot, first):
    iota = bcast_mid(K.IOTA[:, 0:E], T)
    link(nc.vector.tensor_reduce(best, LG, AX.X, ALU.max))
    link(nc.vector.tensor_tensor(onehot, LG, bcast_last(best, E), ALU.is_equal))
    link(nc.vector.tensor_tensor(onehot, onehot, iota, ALU.mult))
    link(nc.vector.tensor_reduce(first, onehot, AX.X, ALU.min))
    link(nc.vector.tensor_tensor(onehot, iota, bcast_last(first, E), ALU.is_equal))


def moe_route_stage(nc, K, name, LG, E, W, mode, OHT=None):
    ctx, sb, sem = open_stage(nc, name)
    with ctx:
        OH = sb("onehot", [P, 2, T, E], F32)
        REST = sb("rest", [P, T, E], F32)
        S = sb("s", [P, 7, T], F32)
        dve, act_in, act_out, pe_in, pe_out = sem("dve"), sem("act_in"), sem("act_out"), sem("pe_in"), sem("pe_out")
        taken = sem("taken")
        groups = [(t, min(4, T - t)) for t in range(0, T, 4)]
        with nc.Block() as block:

            @block.vector
            def _(v):
                link = Link(v, dve)
                if mode == "argmax":
                    choose(nc, K, link, LG[:], E, S[:, 4, :], W[:], S[:, 5, :])
                    nc.vector.sem_inc(pe_in, 1)
                    return
                choose(nc, K, link, LG[:], E, S[:, 4, :], OH[:, 0], S[:, 5, :])
                link(nc.vector.scalar_tensor_tensor(REST[:], OH[:, 0], -3e38, LG[:], ALU.mult, ALU.add))
                choose(nc, K, link, REST[:], E, S[:, 6, :], OH[:, 1], S[:, 5, :])
                nc.vector.tensor_tensor(S[:, 0, :], S[:, 6, :], S[:, 4, :], ALU.subtract).then_inc(act_in, 1)
                v.wait_ge(act_out, 1)
                link(nc.vector.tensor_scalar(S[:, 2, :], S[:, 1, :], 1.0, None, ALU.add))
                link(nc.vector.reciprocal(S[:, 2, :], S[:, 2, :]))
                link(nc.vector.tensor_tensor(S[:, 3, :], S[:, 1, :], S[:, 2, :], ALU.mult))
                for k in range(2):
                    last = nc.vector.tensor_tensor(OH[:, k], OH[:, k], bcast_last(S[:, 2 + k, :], E), ALU.mult)
                link(last)
                link(nc.vector.tensor_tensor(W[:], OH[:, 0], OH[:, 1], ALU.add))

            @block.scalar
            def _(act):
                if mode == "top2":
                    act.wait_ge(act_in, 1)
                    nc.scalar.activation(S[:, 1, :], S[:, 0, :], ACT.Exp).then_inc(act_out, 1)
                else:
                    for g, (t, k) in enumerate(groups):
                        act.wait_ge(pe_out, g + 1)
                        nc.scalar.activation(OHT[:, t * P:(t + k) * P], K.PS[0:E, g, 0:k * P], ACT.Copy).then_inc(taken, 1)

            @block.tensor
            def _(pe):
                if mode == "argmax":
                    pe.wait_ge(pe_in, 1)
                    for g, (t, k) in enumerate(groups):
                        for j in range(k):
                            last = nc.tensor.transpose(K.PS[0:E, g, j * P:(j + 1) * P], W[:, t + j, :], K.IDENT[:])
                        last.then_inc(pe_out, 1)


def moe_stage(nc, K, name, W1, B1, W2, B2, W, E, HT, func):
    ctx, sb, sem = open_stage(nc, name)
    with ctx:
        STEPS, TURNS, LAG, RING = E * HT, T // 2, 2, 4
        G = sb("hidden", [P, RING, 2 * P], F32)
        hidden, active, used, added = sem("hidden"), sem("active"), sem("used"), sem("added")
        bias = Bias(nc, K, sb, sem, W, B2, E)
        with nc.Block() as block:

            @block.tensor
            def _(pe):
                bias.tensor(pe)

                def up(k, nodes):
                    nc.tensor.matmul(K.PS[:, k % RING, 0:2 * P], W1[:, k * P:(k + 1) * P], K.XT[:, nodes],
                                     start=True, stop=True).then_inc(hidden, 1)

                for k in range(LAG):
                    up(k, bass.ds(0, 2 * P))
                with pe.Fori(0, TURNS) as c:
                    for k in range(STEPS):
                        e, h = divmod(k, HT)
                        ahead = k + LAG
                        up(ahead % STEPS, bass.ds(2 * P * c + 2 * P * (ahead // STEPS), 2 * P))
                        pe.wait_ge(active, STEPS * c + k + 1)
                        if h == 0:
                            pe.wait_ge(added, E * c + e + 1)
                        for a in range(2):
                            last = nc.tensor.matmul(K.PS[:, 4 + 2 * (e % 2) + a, 0:P], G[:, k % RING, a * P:(a + 1) * P],
                                                    W2[:, k, :], start=(h == 0), stop=(h == HT - 1))
                        last.then_inc(used, 1)

            @block.scalar
            def _(act):
                bias.scalar(act)
                with act.Fori(0, TURNS) as c:
                    for k in range(STEPS):
                        act.wait_ge(hidden, STEPS * c + k + 1)
                        act.wait_ge(used, STEPS * c + k + 1)
                        nc.scalar.activation(G[:, k % RING, :], K.PS[:, k % RING, 0:2 * P], func,
                                             bias=B1[:, k:k + 1]).then_inc(active, 1)

            @block.vector
            def _(v):
                v.sem_inc(used, RING)
                v.sem_inc(added, 2)
                bias.vector(v)
                v.wait_ge(bias.taken, len(bias.groups))
                with v.Fori(0, TURNS) as c:
                    for e in range(E):
                        v.wait_ge(used, STEPS * c + (HT * (e + 1) + RING))
                        v.wait_ge(added, E * c + e + 2)
                        for a in range(2):
                            x = K.X[:, bass.ds(2 * c + a, 1), :].rearrange("p a d -> p (a d)")
                            last = nc.vector.scalar_tensor_tensor(x, K.PS[:, 4 + 2 * (e % 2) + a, 0:P],
                                                                  W[:, bass.ds(2 * c + a, 1), e], x, ALU.mult, ALU.add)
                        last.then_inc(added, 1)


def moe_layer(nc, K, D, name, r0, E, HT, func, twice=False):
    ctx = ExitStack()
    with ctx:
        sb = lambda n, shape, dt: ctx.enter_context(nc.sbuf_tensor(f"{name}_{n}", shape, dt))
        W1 = sb("w1", [P, E * HT * P], F32)
        W2 = sb("w2", [P, E * HT, P], F32)
        B1 = sb("b1", [P, E * HT], F32)
        B2 = sb("b2", [E, P], F32)
        LG = sb("logits", [P, T, E], F32)
        W = sb("weights", [P, T, E], F32)
        loads = [(W1[:], D[f"{name}_w1"]), (W2[:], D[f"{name}_w2"]), (B1[:], D[f"{name}_b1"]), (B2[:], D[f"{name}_b2"])]
        norm_project_stage(nc, K, f"{name}p", K.R[:, r0:r0 + E], E, T, lambda t, k: LG[:, t:t + k, :],
                           bias=K.BR[:, r0:r0 + E], twice=twice, affine=twice, loads=loads)
        moe_route_stage(nc, K, f"{name}r", LG, E, W, "top2")
        moe_stage(nc, K, f"{name}m", W1, B1, W2, B2, W, E, HT, func)


def moe32_layer(nc, K, D):
    ctx = ExitStack()
    with ctx:
        E, H, HT, RING, LAG = 32, 32, 8, 4, 2
        sb = lambda n, shape, dt: ctx.enter_context(nc.sbuf_tensor(f"f2_{n}", shape, dt))
        W1 = sb("w1", [P, HT * P], F32)
        W2 = sb("w2", [P, HT, P], F32)
        B1 = sb("b1", [P, HT], F32)
        B2 = sb("b2", [E, P], F32)
        BS = sb("b2_parts", [E, 3, P], BF16)
        SPREAD = sb("spread", [E, HT, P], F32)
        SP16 = sb("spread16", [E, HT, P], BF16)
        LG = sb("logits", [P, T, E], F32)
        W = sb("onehot", [P, T, E], F32)
        OHT = sb("oht", [E, NP + 2 * P], BF16)
        G0 = sb("relu", [P, RING, 2 * P], F32)
        G = sb("chosen", [P, RING, 2 * P], F32)
        loads = [(W1[:], D["f2_w1"]), (W2[:], D["f2_w2"]), (B1[:], D["f2_b1"]), (B2[:], D["f2_b2"]), (SPREAD[:], D["spread"])]
        norm_project_stage(nc, K, "f2p", K.R[:, 16:48], E, 16, lambda t, k: LG[:, t:t + k, :], bias=K.BR[:, 16:48], loads=loads)
        moe_route_stage(nc, K, "f2r", LG, E, W, "argmax", OHT=OHT)
        sems, _, sem = open_stage(nc, "f2m")
        with sems:
            ready, hidden, active, chosen, used, added, dve = (sem("ready"), sem("hidden"), sem("active"), sem("chosen"),
                                                               sem("used"), sem("added"), sem("dve"))
            biased = sem("biased")
            with nc.Block() as block:

                @block.tensor
                def _(pe):
                    pe.wait_ge(ready, 1)

                    def up(k, nodes):
                        nc.tensor.matmul(K.PS[:, k % RING, 0:2 * P], W1[:, k * P:(k + 1) * P], K.XT[:, nodes],
                                         start=True, stop=True)
                        nc.tensor.matmul(K.PS[:, k % RING, 2 * P:4 * P], SP16[:, k, :], OHT[:, nodes],
                                         start=True, stop=True).then_inc(hidden, 1)

                    for k in range(LAG):
                        up(k, bass.ds(0, 2 * P))
                    with pe.Fori(0, T // 2) as c:
                        for k in range(HT):
                            ahead = k + LAG
                            up(ahead % HT, bass.ds(2 * P * c + 2 * P * (ahead // HT), 2 * P))
                            if k == 0:
                                pe.wait_ge(added, c + 1)
                            pe.wait_ge(chosen, HT * c + (k + 1 + RING))
                            for a in range(2):
                                last = nc.tensor.matmul(K.PS[:, 4 + a, 0:P], G[:, k % RING, a * P:(a + 1) * P], W2[:, k, :],
                                                        start=(k == 0), stop=False)
                            last.then_inc(used, 1)
                        for a in range(2):
                            for s in range(3):
                                last = nc.tensor.matmul(K.PS[:, 4 + a, 0:P], OHT[:, bass.ds(2 * P * c + a * P, P)], BS[:, s, :],
                                                        start=False, stop=(s == 2))
                        last.then_inc(biased, 1)

                @block.scalar
                def _(act):
                    with act.Fori(0, T // 2) as c:
                        for k in range(HT):
                            act.wait_ge(hidden, HT * c + k + 1)
                            act.wait_ge(chosen, HT * c + k + 1)
                            nc.scalar.activation(G0[:, k % RING, :], K.PS[:, k % RING, 0:2 * P], ACT.Relu,
                                                 bias=B1[:, k:k + 1]).then_inc(active, 1)

                @block.vector
                def _(v):
                    link = Link(v, dve)
                    for part in range(3):
                        link(nc.vector.tensor_copy(BS[:, part, :], B2[:]))
                        if part < 2:
                            link(nc.vector.tensor_tensor(B2[:], B2[:], BS[:, part, :], ALU.subtract))
                    link(nc.vector.memset(OHT[:, NP:NP + 2 * P], 0.0))
                    nc.vector.tensor_copy(SP16[:], SPREAD[:]).then_inc(ready, 1)
                    v.sem_inc(chosen, RING)
                    v.sem_inc(used, RING)
                    v.sem_inc(added, 1)
                    with v.Fori(0, T // 2) as c:
                        for k in range(HT):
                            v.wait_ge(active, HT * c + k + 1)
                            v.wait_ge(used, HT * c + k + 1)
                            nc.vector.tensor_tensor(G[:, k % RING, :], G0[:, k % RING, :],
                                                    K.PS[:, k % RING, 2 * P:4 * P], ALU.mult).then_inc(chosen, 1)
                        v.wait_ge(biased, c + 1)
                        x = K.X[:, bass.ds(2 * c, 2), :]
                        nc.vector.scalar_tensor_tensor(x, K.PS[:, 4:6, 0:P], 0.0, x, ALU.max, ALU.add).then_inc(added, 1)


def pair_route_stage(nc, K, name, LG, E, BLOCK, NB, W, SHARE, SEND, FETCH, WROW):
    ctx, sb, sem = open_stage(nc, name)
    with ctx:
        OH = sb("onehot", [P, 3, T, E], F32)
        REST = sb("rest", [P, T, E], F32)
        CUM = sb("cum", [P, 4, E * T], F32)
        S = sb("s", [P, 6, T], F32)
        KMAX = NP // BLOCK
        STEP = sb("steps", [P, KMAX], F32)
        MANY = sb("many", [P, E, KMAX], F32)
        BI = sb("block", [P, NB], F32)
        PAST = sb("past", [P, NB, E], F32)
        WR = sb("weight_row", [P, NB], F32)
        PART = sb("partition", [P, 1], F32)
        N8 = sb("blocks", [P, 3, E], F32)
        ROW = sb("row", [P, 2, T], F32)
        NONE = sb("none", [P, 2, T], F32)
        dve, act_in, act_out, pe_in, pe_out = sem("dve"), sem("act_in"), sem("act_out"), sem("pe_in"), sem("pe_out")
        consts = sem("consts")
        with nc.Block() as block:

            @block.gpsimd
            def _(pool):
                for dst, step, p in ((STEP, BLOCK, 0), (BI, 1, 0), (PART, 1, 1)):
                    nc.gpsimd.iota(dst[:], pattern=[[step, dst.shape[1]]], base=0, channel_multiplier=p,
                                   allow_small_or_imprecise_dtypes=True).then_inc(consts, 1)

            @block.vector
            def _(v):
                link = Link(v, dve)
                choose(nc, K, link, LG[:], E, S[:, 4, :], OH[:, 0], S[:, 5, :])
                link(nc.vector.scalar_tensor_tensor(REST[:], OH[:, 0], -3e38, LG[:], ALU.mult, ALU.add))
                choose(nc, K, link, REST[:], E, S[:, 3, :], OH[:, 1], S[:, 5, :])
                nc.vector.tensor_tensor(S[:, 0, :], S[:, 3, :], S[:, 4, :], ALU.subtract).then_inc(act_in, 1)
                nc.vector.tensor_tensor(OH[:, 2], OH[:, 0], OH[:, 1], ALU.add).then_inc(pe_in, 1)
                link(nc.vector.memset(CUM[:, 0, :], 1.0))
                link(nc.vector.memset(CUM[:, 0, :].rearrange("p (e t) -> p e t", t=T)[:, :, 0:1], 0.0))
                v.wait_ge(act_out, 1)
                link(nc.vector.tensor_scalar(S[:, 2, :], S[:, 1, :], 1.0, None, ALU.add))
                link(nc.vector.reciprocal(SHARE[:, 0, :], S[:, 2, :]))
                link(nc.vector.tensor_tensor(SHARE[:, 1, :], S[:, 1, :], SHARE[:, 0, :], ALU.mult))
                nc.vector.tensor_tensor(W[:], OH[:, 0], bcast_last(SHARE[:, 0, :], E), ALU.mult)
                link(nc.vector.tensor_tensor(REST[:], OH[:, 1], bcast_last(SHARE[:, 1, :], E), ALU.mult))
                link(nc.vector.tensor_tensor(W[:], W[:], REST[:], ALU.add))
                v.wait_ge(pe_out, 1)
                for k in range(2):
                    last = nc.vector.tensor_copy(CUM[:, 1 + k, :].rearrange("p (e t) -> p e t", t=T),
                                                 K.PS[:, k, 0:T * E].rearrange("p (t e) -> p e t", e=E))
                link(last)
                link(nc.vector.tensor_tensor_scan(CUM[:, 3, :], CUM[:, 0, :], CUM[:, 2, :], 0.0, ALU.mult, ALU.add))
                v.wait_ge(consts, 3)
                total = CUM[:, 3, :].rearrange("p (e t) -> p e t", t=T)[:, :, T - 1]
                link(nc.vector.tensor_tensor(MANY[:], bcast_last(total, KMAX), bcast_mid(STEP[:], E), ALU.is_gt))
                link(nc.vector.tensor_reduce(N8[:, 0, :], MANY[:], AX.X, ALU.add))
                link(nc.vector.tensor_tensor_scan(N8[:, 1, :], K.ONES[:, 0:E], N8[:, 0, :], 0.0, ALU.mult, ALU.add))
                link(nc.vector.tensor_tensor(N8[:, 2, :], N8[:, 1, :], N8[:, 0, :], ALU.subtract))
                link(nc.vector.tensor_scalar(N8[:, 2, :], N8[:, 2, :], float(BLOCK), None, ALU.mult))
                link(nc.vector.tensor_tensor(CUM[:, 3, :], CUM[:, 3, :], CUM[:, 2, :], ALU.subtract))
                link(nc.vector.tensor_tensor(CUM[:, 3, :], CUM[:, 3, :], CUM[:, 1, :], ALU.add))
                e3 = CUM[:, 3, :].rearrange("p (e t) -> p e t", t=T)
                link(nc.vector.tensor_tensor(e3, e3, bcast_last(N8[:, 2, :], T), ALU.add))
                for k in range(2):
                    last = nc.vector.tensor_tensor(OH[:, k], OH[:, k], CUM[:, 3, :].rearrange("p (e t) -> p t e", t=T),
                                                   ALU.mult)
                link(last)
                link(nc.vector.tensor_reduce(ROW[:], OH[:, 0:2], AX.X, ALU.add))
                link(nc.vector.tensor_scalar(NONE[:], ROW[:], 0.5, NB * BLOCK + 1.0, ALU.is_lt, ALU.mult))
                link(nc.vector.tensor_scalar(ROW[:], ROW[:], 1.0, None, ALU.subtract))
                link(nc.vector.tensor_tensor(ROW[:], ROW[:], NONE[:], ALU.add))
                link(nc.vector.tensor_copy(SEND[:], ROW[:]))
                link(nc.vector.tensor_scalar(ROW[:], ROW[:], NB * BLOCK - 1.0, None, ALU.min))
                link(nc.vector.tensor_copy(FETCH[:], ROW[:]))
                link(nc.vector.tensor_tensor(PAST[:], bcast_mid(N8[:, 1, :], NB), bcast_last(BI[:], E), ALU.is_le))
                link(nc.vector.tensor_reduce(WR[:], PAST[:], AX.X, ALU.add))
                link(nc.vector.tensor_scalar(WR[:], WR[:], E - 1.0, float(P), ALU.min, ALU.mult))
                link(nc.vector.tensor_scalar(WR[:], WR[:], PART[:, 0:1], None, ALU.add))
                nc.vector.tensor_copy(WROW[:], WR[:])

            @block.scalar
            def _(act):
                act.wait_ge(act_in, 1)
                nc.scalar.activation(S[:, 1, :], S[:, 0, :], ACT.Exp).then_inc(act_out, 1)

            @block.tensor
            def _(pe):
                pe.wait_ge(pe_in, 1)
                oh = OH[:, 2].rearrange("p t e -> p (t e)")
                nc.tensor.matmul(K.PS[:, 0, 0:T * E], K.LOWER[:], oh, start=True, stop=True)
                nc.tensor.matmul(K.PS[:, 1, 0:T * E], K.ONES[:], oh, start=True, stop=True).then_inc(pe_out, 1)


class Bias:

    def __init__(self, nc, K, sb, sem, W, B2, E):
        self.nc, self.K, self.W, self.B2, self.E = nc, K, W, B2, E
        self.WT = sb("wt", [E, NP], F32)
        self.transposed, self.wt_ready = sem("transposed_w"), sem("wt_ready")
        self.biased, self.taken = sem("biased"), sem("bias_taken")
        self.groups = [(t, min(4, T - t)) for t in range(0, T, 4)]

    def tensor(self, pe):
        nc, K, E = self.nc, self.K, self.E
        for g, (t, k) in enumerate(self.groups):
            if g >= 4:
                pe.wait_ge(self.wt_ready, g - 3)
            for j in range(k):
                last = nc.tensor.transpose(K.PS[0:E, g % 4, j * P:(j + 1) * P], self.W[:, t + j, :], K.IDENT[:])
            last.then_inc(self.transposed, 1)
        for g, (t, k) in enumerate(self.groups):
            pe.wait_ge(self.wt_ready, g + 1)
            if g >= 4:
                pe.wait_ge(self.taken, g - 3)
            for j in range(k):
                last = nc.tensor.matmul(K.PS[:, 4 + g % 4, j * P:(j + 1) * P], self.WT[:, (t + j) * P:(t + j + 1) * P],
                                        self.B2[:], start=True, stop=True)
            last.then_inc(self.biased, 1)
        pe.wait_ge(self.taken, len(self.groups))

    def scalar(self, act):
        for g, (t, k) in enumerate(self.groups):
            act.wait_ge(self.transposed, g + 1)
            self.nc.scalar.activation(self.WT[:, t * P:(t + k) * P], self.K.PS[0:self.E, g % 4, 0:k * P], ACT.Copy)\
                .then_inc(self.wt_ready, 1)

    def vector(self, v):
        for g, (t, k) in enumerate(self.groups):
            v.wait_ge(self.biased, g + 1)
            ps, x = self.K.PS[:, 4 + g % 4, 0:k * P].rearrange("p (k d) -> p k d", d=P), self.K.X[:, t:t + k, :]
            self.nc.vector.tensor_tensor(x, x, ps, ALU.add).then_inc(self.taken, 1)


def pair_experts_stage(nc, K, D, name, E, HT, BLOCK, NB, W, B2, SHARE, SEND, FETCH, WROW):
    ctx, sb, sem = open_stage(nc, name)
    with ctx:
        RING, A = 3, BLOCK // P
        H = HT * P
        XE = sb("rows", [P, RING, A, P], F32)
        XET = sb("rows_t", [P, RING, BLOCK], F32)
        WB = sb("w", [P, RING, 2 * H + HT], F32)
        G = sb("hidden", [P, RING, HT, BLOCK], F32)
        Y = sb("results", [P, RING, A, P], F32)
        sent, in_x, in_w = sem("sent"), [sem(f"in_x{q}") for q in range(RING)], [sem(f"in_w{q}") for q in range(RING)]
        transposed, xt_ready, hidden, active = sem("transposed"), sem("xt_ready"), sem("hidden"), sem("active")
        summed, y_ready, stored = sem("summed"), sem("y_ready"), [sem(f"stored{q}") for q in range(RING)]
        groups = [(t, min(7, T - t)) for t in range(0, T, 7)]
        fetched, held, added = [sem(f"fetched{g}") for g in range(len(groups))], sem("held"), sem("added")
        bias = Bias(nc, K, sb, sem, W, B2, E)
        slots, results = D["slots"], D["results1"]
        FETCHED = [K.XN[:], K.XT[:, 0:NP].rearrange("p (t d) -> p t d", d=P)]
        TURNS = NB // RING
        with nc.Block() as block:

            @block.gpsimd
            def _(pool):
                def weights(b):
                    nc.gpsimd.indirect_dma_start(out=WB[:, b % RING, :], out_offset=None, in_=D["f1_w"],
                                                 in_offset=bass.IndirectOffsetOnAxis(ap=WROW[:, b:b + 1], axis=0))\
                        .then_inc(in_w[b % RING], 16)

                for b in range(RING):
                    weights(b)
                for t in range(T):
                    for k in range(2):
                        nc.gpsimd.indirect_dma_start(
                            out=slots, out_offset=bass.IndirectOffsetOnAxis(ap=SEND[:, k, t:t + 1], axis=0),
                            in_=K.XN[:, t, :], in_offset=None).then_inc(sent, 16)
                for b in range(RING, NB):
                    pool.wait_ge(summed, b + 1)
                    weights(b)
                pool.wait_ge(sent, 16 * 2 * T)
                for q in range(RING):
                    pool.wait_ge(stored[q], 16 * TURNS + 16)
                for g, (t0, m) in enumerate(groups):
                    for t in range(t0, t0 + m):
                        for k in range(2):
                            nc.gpsimd.indirect_dma_start(
                                out=FETCHED[k][:, t, :], out_offset=None, in_=results,
                                in_offset=bass.IndirectOffsetOnAxis(ap=FETCH[:, k, t:t + 1], axis=0))\
                                .then_inc(fetched[g], 16)

            @block.sync
            def _(sp):
                def load(b, q):
                    sp.dma_start(XE[:, q, :, :].rearrange("p a d -> p (a d)"),
                                 slots[bass.ds(BLOCK * b, BLOCK), :].rearrange("(p a) d -> p (a d)", a=A))\
                        .then_inc(in_x[q], 16)

                def store(b, q):
                    sp.dma_start(results[bass.ds(BLOCK * b, BLOCK), :].rearrange("(p a) d -> p (a d)", a=A),
                                 Y[:, q, :, :].rearrange("p a d -> p (a d)")).then_inc(stored[q], 16)

                sp.wait_ge(sent, 16 * 2 * T)
                for q in range(RING):
                    load(q, q)
                with sp.Fori(0, TURNS - 1) as t:
                    for q in range(RING):
                        sp.wait_ge(y_ready, RING * t + q + 2)
                        sp.sem_inc(held, 1)
                        store(RING * t + q, q)
                        load(RING * t + q + RING, q)
                for q in range(RING):
                    sp.wait_ge(y_ready, NB - RING + q + 2)
                    store(NB - RING + q, q)

            @block.tensor
            def _(pe):
                bias.tensor(pe)

                def turn(b, q, loads):
                    pe.wait_ge(in_x[q], loads)
                    pe.wait_ge(xt_ready, b + 1)
                    for a in range(A):
                        last = nc.tensor.transpose(K.PS[:, 0, a * P:(a + 1) * P], XE[:, q, a, :], K.IDENT[:])
                    last.then_inc(transposed, 1)

                def up(b, q, loads):
                    pe.wait_ge(in_w[q], loads)
                    pe.wait_ge(xt_ready, b + 2)
                    for h in range(HT):
                        nc.tensor.matmul(K.PS[:, 2 + h, 0:BLOCK], WB[:, q, h * P:(h + 1) * P], XET[:, q, :],
                                         start=True, stop=True).then_inc(hidden, 1)

                def down(b, q):
                    pe.wait_ge(active, HT * b + HT)
                    pe.wait_ge(y_ready, b + 1)
                    for a in range(A):
                        for h in range(HT):
                            last = nc.tensor.matmul(K.PS[:, 1, a * P:(a + 1) * P], G[:, q, h, a * P:(a + 1) * P],
                                                    WB[:, q, H + h * P:H + (h + 1) * P], start=(h == 0), stop=(h == HT - 1))
                    last.then_inc(summed, 1)

                turn(0, 0, 16)
                up(0, 0, 16)
                with pe.Fori(0, TURNS - 1) as t:
                    for q in range(RING):
                        b, nq = RING * t + q, (q + 1) % RING
                        loads = 16 * t + (32 if q == RING - 1 else 16)
                        turn(b + 1, nq, loads)
                        down(b, q)
                        up(b + 1, nq, loads)
                for q in range(RING):
                    b = NB - RING + q
                    if q < RING - 1:
                        turn(b + 1, q + 1, 16 * TURNS)
                    down(b, q)
                    if q < RING - 1:
                        up(b + 1, q + 1, 16 * TURNS)

            @block.scalar
            def _(act):
                bias.scalar(act)
                with act.Fori(0, TURNS) as t:
                    for q in range(RING):
                        b = RING * t + q
                        act.wait_ge(summed, b + 1)
                        for h in range(HT):
                            act.wait_ge(hidden, HT * b + (h + 1 + 2 * HT))
                            nc.scalar.activation(G[:, q, h, :], K.PS[:, 2 + h, 0:BLOCK], ACT.Gelu,
                                                 bias=WB[:, q, 2 * H + h:2 * H + h + 1]).then_inc(active, 1)

            @block.vector
            def _(v):
                v.sem_inc(xt_ready, 1)
                v.sem_inc(y_ready, 1)
                v.sem_inc(summed, RING)
                v.sem_inc(hidden, 2 * HT)
                for q in range(RING):
                    v.sem_inc(stored[q], 16)
                bias.vector(v)

                def columns(b, q):
                    v.wait_ge(transposed, b + 1)
                    v.wait_ge(hidden, HT * b)
                    nc.vector.tensor_copy(XET[:, q, :], K.PS[:, 0, 0:BLOCK]).then_inc(xt_ready, 1)

                def result(b, q, stores):
                    v.wait_ge(summed, b + 1 + RING)
                    v.wait_ge(stored[q], stores)
                    nc.vector.tensor_copy(Y[:, q, :, :].rearrange("p a d -> p (a d)"), K.PS[:, 1, 0:BLOCK])\
                        .then_inc(y_ready, 1)

                columns(0, 0)
                with v.Fori(0, TURNS - 1) as t:
                    for q in range(RING):
                        b = RING * t + q
                        columns(b + 1, (q + 1) % RING)
                        result(b, q, 16 * t + 16)
                for q in range(RING):
                    b = NB - RING + q
                    if q < RING - 1:
                        columns(b + 1, q + 1)
                    result(b, q, 16 * TURNS)
                for g, (t0, m) in enumerate(groups):
                    v.wait_ge(fetched[g], 16 * 2 * m)
                    for k in range(2):
                        for t in range(t0, t0 + m):
                            last = nc.vector.scalar_tensor_tensor(K.X[:, t, :], FETCHED[k][:, t, :], SHARE[:, k, t:t + 1],
                                                                  K.X[:, t, :], ALU.mult, ALU.add)
                        last.then_inc(added, 1)
                        v.wait_ge(added, 2 * g + k + 1)


def pair_layer(nc, K, D):
    E, HT, BLOCK, NB = 8, 4, PAIR_BLOCK, PAIR_BLOCKS
    assert NB % 3 == 0
    ctx = ExitStack()
    with ctx:
        sb = lambda n, shape, dt: ctx.enter_context(nc.sbuf_tensor(f"f1_{n}", shape, dt))
        LG = sb("logits", [P, T, E], F32)
        W = sb("weights", [P, T, E], F32)
        B2 = sb("b2", [E, P], F32)
        SHARE = sb("share", [P, 2, T], F32)
        SEND, FETCH = sb("send", [P, 2, T], I32), sb("fetch", [P, 2, T], I32)
        WROW = sb("weight_rows", [P, NB], I32)
        empty = D["slots"][0:NB * BLOCK, :].rearrange("(p k) d -> p k d", p=P)
        zeros = K.ZERO[:].unsqueeze(1).to_broadcast([P, NB * BLOCK // P, P])
        norm_project_stage(nc, K, "f1p", K.R[:, 8:8 + E], E, T, lambda t, k: LG[:, t:t + k, :],
                           bias=K.BR[:, 8:8 + E], loads=[(B2[:], D["f1_b2"]), (empty, zeros)])
        pair_route_stage(nc, K, "f1r", LG, E, BLOCK, NB, W, SHARE, SEND, FETCH, WROW)
        pair_experts_stage(nc, K, D, "f1m", E, HT, BLOCK, NB, W, B2, SHARE, SEND, FETCH, WROW)


def capacity_route_stage(nc, K, name, LG, E, capacity, SEND, FETCH, SHARE):
    ctx, sb, sem = open_stage(nc, name)
    with ctx:
        best, first = sb("best", [P, T], F32), sb("first", [P, T], F32)
        OH = sb("onehot", [P, T, E], F32)
        EX = sb("exp", [P, T, E], F32)
        CUM = sb("cum", [P, 4, E * T], F32)
        S = sb("s", [P, 6, T], F32)
        dve, act_in, act_out, pe_in, pe_out = sem("dve"), sem("act_in"), sem("act_out"), sem("pe_in"), sem("pe_out")
        with nc.Block() as block:

            @block.vector
            def _(v):
                link = Link(v, dve)
                choose(nc, K, link, LG[:], E, best[:], OH[:], first[:])
                nc.vector.tensor_tensor(EX[:], LG[:], bcast_last(best[:], E), ALU.subtract).then_inc(act_in, 1)
                nc.vector.sem_inc(pe_in, 1)
                link(nc.vector.memset(CUM[:, 0, :], 1.0))
                link(nc.vector.memset(CUM[:, 0, :].rearrange("p (e t) -> p e t", t=T)[:, :, 0:1], 0.0))
                v.wait_ge(pe_out, 1)
                for k in range(2):
                    last = nc.vector.tensor_copy(CUM[:, 1 + k, :].rearrange("p (e t) -> p e t", t=T),
                                                 K.PS[:, k, 0:T * E].rearrange("p (t e) -> p e t", e=E))
                link(last)
                link(nc.vector.tensor_tensor_scan(CUM[:, 3, :], CUM[:, 0, :], CUM[:, 2, :], 0.0, ALU.mult, ALU.add))
                link(nc.vector.tensor_tensor(CUM[:, 3, :], CUM[:, 3, :], CUM[:, 2, :], ALU.subtract))
                link(nc.vector.tensor_tensor(CUM[:, 3, :], CUM[:, 3, :], CUM[:, 1, :], ALU.add))
                link(nc.vector.tensor_tensor(OH[:], OH[:], CUM[:, 3, :].rearrange("p (e t) -> p t e", t=T), ALU.mult))
                place, kept, base, row, prob, send = (S[:, k, :] for k in range(6))
                link(nc.vector.tensor_reduce(place, OH[:], AX.X, ALU.add))
                link(nc.vector.tensor_scalar(kept, place, 1.0, None, ALU.is_ge))
                link(nc.vector.tensor_scalar(row, place, float(capacity), None, ALU.is_le))
                link(nc.vector.tensor_tensor(kept, kept, row, ALU.mult))
                link(nc.vector.tensor_scalar(base, first[:], float(capacity), 32.0 * capacity - 1, ALU.mult, ALU.add))
                link(nc.vector.tensor_scalar(row, place, float(capacity), None, ALU.min))
                link(nc.vector.tensor_tensor(row, row, base, ALU.add))
                link(nc.vector.tensor_scalar(row, row, E * capacity - 1.0, None, ALU.min))
                link(nc.vector.tensor_copy(FETCH[:], row))
                link(nc.vector.tensor_tensor(send, row, K.OVERFLOW[:], ALU.subtract))
                link(nc.vector.tensor_tensor(send, send, kept, ALU.mult))
                link(nc.vector.tensor_tensor(send, send, K.OVERFLOW[:], ALU.add))
                link(nc.vector.tensor_copy(SEND[:], send))
                v.wait_ge(act_out, 1)
                link(nc.vector.tensor_reduce(prob, EX[:], AX.X, ALU.add))
                link(nc.vector.reciprocal(prob, prob))
                link(nc.vector.tensor_tensor(SHARE[:], prob, kept, ALU.mult))

            @block.scalar
            def _(act):
                act.wait_ge(act_in, 1)
                nc.scalar.activation(EX[:], EX[:], ACT.Exp).then_inc(act_out, 1)

            @block.tensor
            def _(pe):
                pe.wait_ge(pe_in, 1)
                oh = OH[:].rearrange("p t e -> p (t e)")
                nc.tensor.matmul(K.PS[:, 0, 0:T * E], K.LOWER[:], oh, start=True, stop=True)
                nc.tensor.matmul(K.PS[:, 1, 0:T * E], K.ONES[:], oh, start=True, stop=True).then_inc(pe_out, 1)


def capacity_experts_stage(nc, K, D, name, E, HT, capacity, SEND, FETCH, SHARE):
    ctx, sb, sem = open_stage(nc, name)
    with ctx:
        B = 5
        R = capacity // B
        C2 = capacity // 2
        XE = sb("rows", [R, 2, B, P], F32)
        XET = sb("rows_t", [P, 2, B * R], F32)
        W1 = sb("w1", [P, 2, HT * P], F32)
        W2 = sb("w2", [P, 2, HT, P], F32)
        B1 = sb("b1", [P, 2, HT], F32)
        B2 = sb("b2", [R, 2, P], F32)
        G = sb("hidden", [P, 2, HT, B * R], F32)
        Y = sb("results", [R, 2, B, P], F32)
        groups = [(t, min(7, T - t)) for t in range(0, T, 7)]
        MASK = sb("mask", [P, 7 * P], F32)
        VAL = sb("values", [P, 3, 7 * P], F32)
        sent, in_x, in_w = sem("sent"), [sem("in_x0"), sem("in_x1")], [sem("in_w0"), sem("in_w1")]
        transposed, xt_ready, hidden, active = sem("transposed"), sem("xt_ready"), sem("hidden"), sem("active")
        summed, y_ready, stored, dve = sem("summed"), sem("y_ready"), sem("stored"), sem("dve")
        fetched = [sem(f"fetched{g}") for g in range(len(groups))]
        values, held, taken = sem("values"), sem("held"), sem("taken")
        slots, results = D["slots"], D["results3"]
        with nc.Block() as block:

            @block.gpsimd
            def _(pool):
                for t in range(T):
                    nc.gpsimd.indirect_dma_start(out=slots, out_offset=bass.IndirectOffsetOnAxis(ap=SEND[:, t:t + 1], axis=0),
                                                 in_=K.XN[:, t, :], in_offset=None).then_inc(sent, 16)
                for k, value in enumerate((1e4, -1e4, 0.0)):
                    nc.gpsimd.memset(VAL[:, k, :], value).then_inc(values, 1)
                pool.wait_ge(sent, 16 * T)
                pool.wait_ge(stored, 16 * E)
                for g, (t0, k) in enumerate(groups):
                    for t in range(t0, t0 + k):
                        nc.gpsimd.indirect_dma_start(out=K.XN[:, t, :], out_offset=None, in_=results,
                                                     in_offset=bass.IndirectOffsetOnAxis(ap=FETCH[:, t:t + 1], axis=0))\
                            .then_inc(fetched[g], 16)

            @block.sync
            def _(sp):
                def load(e, q):
                    sp.dma_start(W1[:, q, :], D["f3_w1"][:, bass.ds(HT * P * e, HT * P)]).then_inc(in_w[q], 16)
                    sp.dma_start(W2[:, q, :, :], D["f3_w2"][:, bass.ds(HT * e, HT), :]).then_inc(in_w[q], 16)
                    sp.dma_start(B1[:, q, :], D["f3_b1"][:, bass.ds(HT * e, HT)]).then_inc(in_w[q], 16)
                    sp.dma_start(B2[:, q, :], D["f3_b2"][bass.ds(e, 1), :].rearrange("a d -> (a d)")
                                 .partition_broadcast(R)).then_inc(in_w[q], 16)
                    sp.wait_ge(sent, 16 * T)
                    sp.dma_start(XE[:, q, :, :].rearrange("p b d -> p (b d)"),
                                 slots[bass.ds(capacity * e, capacity), :].rearrange("(p b) d -> p (b d)", b=B))\
                        .then_inc(in_x[q], 16)

                def store(e, q):
                    sp.dma_start(results[bass.ds(capacity * e, capacity), :].rearrange("(p b) d -> p (b d)", b=B),
                                 Y[:, q, :, :].rearrange("p b d -> p (b d)")).then_inc(stored, 16)

                for q in range(2):
                    load(q, q)
                with sp.Fori(0, E // 2 - 1) as t:
                    for q in range(2):
                        sp.wait_ge(y_ready, 2 * t + q + 1)
                        sp.sem_inc(taken, 1)
                        store(2 * t + q, q)
                        load(2 * t + q + 2, q)
                for q in range(2):
                    sp.wait_ge(y_ready, E - 2 + q + 1)
                    store(E - 2 + q, q)
                sp.wait_ge(stored, 16 * E)

            @block.tensor
            def _(pe):
                def turn(e, q, loads):
                    pe.wait_ge(in_x[q], loads)
                    pe.wait_ge(xt_ready, e + 1)
                    for b in range(B):
                        last = nc.tensor.transpose(K.PS[:, b // 4, (b % 4) * P:(b % 4) * P + R], XE[:, q, b, :],
                                                   K.IDENT[0:R, 0:R])
                    last.then_inc(transposed, 1)

                def up(e, q, loads):
                    pe.wait_ge(in_w[q], loads)
                    pe.wait_ge(xt_ready, e + 2)
                    for h in range(HT):
                        pe.wait_ge(active, HT * e + h + 1)
                        for a in range(2):
                            last = nc.tensor.matmul(K.PS[:, 2 + 2 * (h % 2) + a, 0:C2], W1[:, q, h * P:(h + 1) * P],
                                                    XET[:, q, a * C2:(a + 1) * C2], start=True, stop=True)
                        last.then_inc(hidden, 1)

                def down(e, q):
                    pe.wait_ge(active, HT * e + HT + 2)
                    pe.wait_ge(y_ready, e)
                    for b in range(B):
                        for h in range(HT):
                            last = nc.tensor.matmul(K.PS[0:R, 6 + b // 4, (b % 4) * P:(b % 4 + 1) * P],
                                                    G[:, q, h, b * R:(b + 1) * R], W2[:, q, h, :],
                                                    start=(h == 0), stop=(h == HT - 1))
                    last.then_inc(summed, 1)

                turn(0, 0, 16)
                up(0, 0, 64)
                with pe.Fori(0, E // 2 - 1) as t:
                    for q in range(2):
                        e = 2 * t + q
                        turn(e + 1, 1 - q, 16 * t + 16 * q + 16)
                        down(e, q)
                        up(e + 1, 1 - q, 64 * t + 64 * q + 64)
                turn(E - 1, 1, 8 * E)
                down(E - 2, 0)
                up(E - 1, 1, 32 * E)
                down(E - 1, 1)

            @block.scalar
            def _(act):
                with act.Fori(0, E // 2) as t:
                    for q in range(2):
                        e = 2 * t + q
                        act.wait_ge(in_w[q], 64 * t + 64)
                        act.wait_ge(summed, e + 1)
                        for h in range(HT):
                            act.wait_ge(hidden, HT * e + (h + 1 + HT))
                            nc.scalar.activation(G[:, q, h, :].rearrange("p (a n) -> p a n", a=2),
                                                 K.PS[:, 2 + 2 * (h % 2):4 + 2 * (h % 2), 0:C2], ACT.Relu,
                                                 bias=B1[:, q, h:h + 1]).then_inc(active, 1)

            @block.vector
            def _(v):
                v.sem_inc(xt_ready, 1)
                v.sem_inc(active, 2)
                v.sem_inc(summed, 2)
                v.sem_inc(hidden, HT)
                link = Link(v, dve)

                def columns(e, q):
                    v.wait_ge(transposed, e + 1)
                    v.wait_ge(hidden, HT * e)
                    nc.vector.tensor_copy(XET[:, q, :].rearrange("p (b r) -> p b r", b=B),
                                          K.PS[:, 0:2, :].rearrange("p a n -> p (a n)")[:, 0:B * P]
                                          .rearrange("p (b r) -> p b r", b=B)[:, :, 0:R]).then_inc(xt_ready, 1)

                def result(e, q):
                    v.wait_ge(summed, e + 3)
                    v.wait_ge(stored, 16 * e)
                    nc.vector.tensor_tensor(Y[:, q, :, :], K.PS[0:R, 6:8, :].rearrange("p a n -> p (a n)")[:, 0:B * P]
                                            .rearrange("p (b d) -> p b d", b=B), bcast_mid(B2[:, q, :], B), ALU.add)\
                        .then_inc(y_ready, 1)

                columns(0, 0)
                with v.Fori(0, E // 2 - 1) as t:
                    for q in range(2):
                        columns(2 * t + q + 1, 1 - q)
                        result(2 * t + q, q)
                columns(E - 1, 1)
                for q in range(2):
                    result(E - 2 + q, q)

                v.wait_ge(values, 3)
                fmax = float(np.finfo(np.float32).max)
                for g, (t0, k) in enumerate(groups):
                    v.wait_ge(fetched[g], 16 * k)
                    y3, mask = K.XN[:, t0:t0 + k, :], MASK[:, 0:k * P]
                    y = y3.rearrange("p t d -> p (t d)")
                    link(nc.vector.tensor_tensor(y3, y3, bcast_last(SHARE[:, t0:t0 + k], P), ALU.mult))
                    for op, bound, value in ((ALU.is_gt, fmax, 0), (ALU.is_lt, -fmax, 1), (ALU.not_equal, None, 2)):
                        if bound is None:
                            link(nc.vector.tensor_tensor(mask, y, y, op))
                        else:
                            link(nc.vector.tensor_scalar(mask, y, bound, None, op))
                        link(nc.vector.copy_predicated(y, mask.bitcast(U32), VAL[:, value, 0:k * P]))
                    x = K.X[:, t0:t0 + k, :]
                    nc.vector.tensor_tensor(x, x, y3, ALU.add)


def capacity_layer(nc, K, D):
    E, HT = 8, 4
    ctx = ExitStack()
    with ctx:
        sb = lambda n, shape, dt: ctx.enter_context(nc.sbuf_tensor(f"f3_{n}", shape, dt))
        LG = sb("logits", [P, T, E], F32)
        SEND, FETCH = sb("send", [P, T], I32), sb("fetch", [P, T], I32)
        SHARE = sb("share", [P, T], F32)
        empty = D["slots"][0:E * CAPACITY, :].rearrange("(p k) d -> p k d", p=CAPACITY // 5)
        zeros = K.ZERO[0:CAPACITY // 5, :].unsqueeze(1).to_broadcast([CAPACITY // 5, 5 * E, P])
        norm_project_stage(nc, K, "f3p", K.R[:, 48:48 + E], E, T, lambda t, k: LG[:, t:t + k, :],
                           bias=K.BR[:, 48:48 + E], loads=[(empty, zeros)])
        capacity_route_stage(nc, K, "f3r", LG, E, CAPACITY, SEND, FETCH, SHARE)
        capacity_experts_stage(nc, K, D, "f3m", E, HT, CAPACITY, SEND, FETCH, SHARE)


def program(nc, A, out, upto=99):
    D = {"xd": nc.dram_tensor("head_parts", [P, T, HEADS, 6 * HC], BF16).ap(),
         "sd": nc.dram_tensor("head_scores", [HEADS, NP], F32).ap(),
         "slots": nc.dram_tensor("expert_slots", [SLOTS, P], F32).ap(),
         "results1": nc.dram_tensor("block_results", [PAIR_BLOCKS * PAIR_BLOCK, P], F32).ap(),
         "results3": nc.dram_tensor("slot_results", [8 * CAPACITY, P], F32).ap(),
         "xn0": nc.dram_tensor("normed0", [P, T, P], F32).ap(),
         "sd3": nc.dram_tensor("scores3", [1, NP], F32).ap(), **A}
    K = Core()
    RETIRED.clear()
    ctx = ExitStack()
    with ctx:
        sb = lambda n, shape, dt: ctx.enter_context(nc.sbuf_tensor(n, shape, dt))
        K.EDGE = sb("edge", [P, T, T, P], U8)
        K.X = sb("nodes", [P, T, P], F32)
        K.XN = sb("normed", [P, T, P], F32)
        K.XT = sb("normed_t", [P, NP + 4 * P], F32)
        K.IDENT = sb("ident", [P, P], F32)
        K.ONES = sb("ones", [P, P], F32)
        K.LOWER = sb("lower", [P, P], F32)
        K.COMB = sb("comb", [P, 2 * HC], F32)
        K.IOTA = sb("iota", [P, 32], F32)
        K.OVERFLOW = sb("overflow", [P, T], F32)
        K.ZERO = sb("zero", [P, P], F32)
        K.NEG_HALF = sb("neg_half", [P, T], F32)
        K.WP0, K.BP0 = sb("wp0", [P, P + 16], F32), sb("bp0", [P, P + 16], F32)
        K.WP1 = sb("wp1", [P, 2 * P], F32)
        K.WP2, K.BP2 = sb("wp2", [P, P + 1], F32), sb("bp2", [P, P + 1], F32)
        K.WP3, K.BP3 = sb("wp3", [P, P + 2], F32), sb("bp3", [P, P + 2], F32)
        K.SB8 = sb("sb8", [HEADS, 1], F32)
        K.R, K.BR = sb("routers", [P, 56], F32), sb("router_b", [P, 56], F32)
        K.GB = sb("gamma_beta", [P, 2], F32)
        K.PS = ctx.enter_context(nc.psum_tensor("psum", [P, 8, 512], F32))
        stages = [
            lambda: setup_stage(nc, K, A),
            lambda: layer0_gnn(nc, K, D),
            lambda: moe_layer(nc, K, D, "f0", 0, 8, 2, ACT.Gelu, twice=True),
            lambda: layer1_gnn(nc, K),
            lambda: pair_layer(nc, K, D),
            lambda: layer2_gnn(nc, K),
            lambda: moe32_layer(nc, K, D),
            lambda: layer3_gnn(nc, K, D),
            lambda: capacity_layer(nc, K, D),
        ]
        for s in stages[:upto]:
            s()
        out_stage(nc, K, out)


def out_stage(nc, K, out):
    ctx, sb, sem = open_stage(nc, "out")
    with ctx:
        stored = sem("stored")
        with nc.Block() as block:

            @block.sync
            def _(sp):
                sp.dma_start(out[0:(T - 1) * P, :].rearrange("(t p) d -> p t d", p=P), K.X[:, 0:T - 1, :]).then_inc(stored, 16)
                sp.dma_start(out[(T - 1) * P:N, :], K.X[0:N - (T - 1) * P, T - 1, :]).then_inc(stored, 16)
                sp.wait_ge(stored, 32)


def layouts(i):
    a = {k: np.asarray(v) for k, v in i.items()}
    x = np.zeros((NP, P), np.float32)
    x[:N] = a["x"]
    adj = np.zeros((NP, NP), np.int32)
    adj[:N, :N] = a["adj"]
    aw = a["L0_gnn_a_w"]
    sel = np.zeros((P, 2 * HEADS), np.float32)
    for h in range(HEADS):
        sel[HD * h:HD * (h + 1), h] = aw[0, :HD]
        sel[HD * h:HD * (h + 1), HEADS + h] = aw[0, HD:]
    c = np.ascontiguousarray
    experts = {}
    for name, w1, b1, w2, b2 in (("f0", "L0_ffn_W1", "L0_ffn_b1", "L0_ffn_W2", "L0_ffn_b2"),
                                 ("f1", "L1_ffn_W1", "L1_ffn_b1", "L1_ffn_W2", "L1_ffn_b2"),
                                 ("f2", "L2_ffn_W1", "L2_ffn_b1", "L2_ffn_W2", "L2_ffn_b2"),
                                 ("f3", "L3_ffn_w1", "L3_ffn_b1", "L3_ffn_w2", "L3_ffn_b2")):
        if name == "f1":
            experts["f1_w"] = c(np.concatenate([a[w1].reshape(8 * P, -1),
                                                a[w2].reshape(8, -1, P, P).transpose(0, 2, 1, 3).reshape(8 * P, -1),
                                                a[b1].reshape(8, -1, P).transpose(0, 2, 1).reshape(8 * P, -1)], 1))
            experts["f1_b2"] = a[b2]
            continue
        experts[f"{name}_w1"] = c(a[w1].transpose(1, 0, 2).reshape(P, -1))
        experts[f"{name}_w2"] = c(a[w2].reshape(-1, P, P).transpose(1, 0, 2))
        experts[f"{name}_b1"] = c(a[b1].reshape(-1, P).T)
        experts[f"{name}_b2"] = a[b2]
    spread = np.zeros((32, 8, P), np.float32)
    for e in range(32):
        spread[e, e // 4, 32 * (e % 4):32 * (e % 4 + 1)] = 1.0
    return {
        **experts, "spread": spread,
        "x": c(x.reshape(T, P, P).transpose(1, 0, 2)),
        "adj": c(adj.reshape(T, P, T, P).transpose(0, 3, 2, 1).reshape(T, P, NP)),
        "w0t": c(a["L0_gnn_W_w"].T), "w0": c(a["L0_gnn_W_w"]), "sel0": sel,
        "wqk": c(np.concatenate([a["L1_gnn_Wq"].T, a["L1_gnn_Wk"].T], 1)),
        "w2": c(a["L2_gnn_W_fc"]), "w2t": c(a["L2_gnn_W_fc"].T), "dst2": c(a["L2_gnn_w_att"][P:].reshape(P, 1)),
        "w3t": c(a["L3_gnn_W_w"].T), "w3": c(a["L3_gnn_W_w"]),
        "a3": c(np.stack([a["L3_gnn_a_src"], a["L3_gnn_a_dst"]], 1)),
        "bcols": c(np.stack([a["L0_gnn_W_b"], a["L2_gnn_b_fc"], a["L3_gnn_W_b"]], 1)),
        "b0": c(a["L0_gnn_W_b"]), "b2": c(a["L2_gnn_b_fc"]), "b3": c(a["L3_gnn_W_b"]),
        "ab": c(np.concatenate([a["L0_gnn_a_b"].reshape(1), a["L3_gnn_a_b"].reshape(1)])),
        "routers": c(np.concatenate([a["L0_ffn_Wr"], a["L1_ffn_Wg"], a["L2_ffn_router_w"].T, a["L3_ffn_gate_w"]], 1)),
        "router_b": c(np.concatenate([a["L0_ffn_br"], a["L1_ffn_bg"], a["L2_ffn_router_b"], a["L3_ffn_gate_b"]])),
        "gamma_beta": c(np.stack([a["L0_ffn_gamma"], a["L0_ffn_beta"]], 1)),
    }


def kernel(**inputs):
    import concourse.bacc as bacc
    from concourse.bass_utils import run_bass_kernel_spmd

    nc = bacc.Bacc("TRN2", target_bir_lowering=False, num_devices=1)
    arrays = layouts(inputs)
    args = {n: nc.dram_tensor(f"in_{n}", a.shape, mybir.dt.from_np(a.dtype), kind="ExternalInput").ap()
            for n, a in arrays.items()}
    out = nc.dram_tensor("out", (N, P), F32, kind="ExternalOutput").ap()
    program(nc, args, out)
    r = run_bass_kernel_spmd(nc, [{f"in_{n}": a for n, a in arrays.items()}], core_ids=[0])
    return r.results[0]["out"]
```

```python
import math
from contextlib import ExitStack

import numpy as np
import concourse.bass as bass
from concourse import mybir

F32 = mybir.dt.float32
BF16 = mybir.dt.bfloat16
FP8 = mybir.dt.float8e4
U8 = mybir.dt.uint8
U16 = mybir.dt.uint16
U32 = mybir.dt.uint32
I32 = mybir.dt.int32
ALU = mybir.AluOpType
ACT = mybir.ActivationFunctionType
AX = mybir.AxisListType

N = 3327
P = 128
T = 26
NP = T * P
HALF = T // 2
HN = HALF * P
LN_EPS = 1e-5
ONE8 = 56
CHUNKS = [(0, 4), (4, 8), (12, 8), (20, 6)]
ARRIVING = [(0, 8), (8, 8), (16, 4), (20, 4), (24, 2)]
TINY = 1e-30
HEADS, HD = 8, 16
HC = HD + 1
BIG = 2.0 ** 100
SLOPE = 0.2
CAPACITY = math.ceil(1.25 * N / 8)
PAIR_BLOCK = 2 * P
ROUTED0 = 16
SLOTS = max((2 * NP // PAIR_BLOCK + 8) * PAIR_BLOCK, 8 * CAPACITY + NP)


STAGE_SEMS = 42
RETIRED = []


class Link:

    def __init__(self, eng, sem):
        self.eng, self.sem, self.n = eng, sem, 0

    def __call__(self, ins, base=0):
        self.n += 1
        ins.then_inc(self.sem, 1)
        self.eng.wait_ge(self.sem, base + self.n)

    def skip(self, n):
        self.n += n


WEIGHT_COLS = {"layer 0": P + 2 * HEADS, "layer 1": 2 * P, "layer 2": P + 1, "layer 3": P + 2, "routers": 56,
               "gamma, beta": 2}
BIAS_COLS = {"layer 0": P + 2 * HEADS, "layer 2": P + 1, "layer 3": P + 2, "routers": 56, "a_b": 2}
SETUP_COLS = {"layer 0": P, "layer 2 transposed": P, "layer 3": P, "a of layer 0": 2 * HEADS, "a of layer 2": 1,
              "a of layer 3": 2, "biases": 3}


def columns(buffer, widths):
    at = np.cumsum([0, *widths.values()])
    return [buffer[:, int(a):int(b)] for a, b in zip(at[:-1], at[1:])]


def pair_blocks(R):
    return -(-((2 * R * P + 8 * (PAIR_BLOCK - 1)) // PAIR_BLOCK) // 3) * 3


class Core:
    pass


def bcast_mid(ap, n):
    return ap.unsqueeze(1).to_broadcast([ap.shape[0], n, ap.shape[1]])


def bcast_last(ap, n):
    return ap.unsqueeze(2).to_broadcast([ap.shape[0], ap.shape[1], n])


def open_stage(nc, name):
    ctx = ExitStack()
    if len(nc.free_semaphores) < STAGE_SEMS:
        nc.clear_and_free_semaphores(RETIRED)
        RETIRED.clear()
        nc.all_engine_barrier()

    def sb(n, shape, dt):
        return ctx.enter_context(nc.sbuf_tensor(f"{name}_{n}", shape, dt))

    def sem(n):
        RETIRED.append(nc.alloc_semaphore(f"{name}_{n}"))
        return RETIRED[-1]

    return ctx, sb, sem


def setup_stage(nc, K, A):
    ctx, sb, sem = open_stage(nc, "setup")
    with ctx:
        W = sb("weights", [P, sum(SETUP_COLS.values())], F32)
        W0, WT2, W3, SEL0, DST2, A3, BC = columns(W, SETUP_COLS)
        BW = sb("bw", [P, 3, P], F32)
        loaded, cols, consts, products = sem("loaded"), sem("cols"), sem("consts"), sem("products")
        AB = K.AB
        loads = [(K.WEIGHTS[:], A["weights"]), (W[:], A["setup"]), (K.X[:], A["x"]),
                 (K.BIASES[:], A["biases"].partition_broadcast(P))]
        n_loads = 16 * len(loads)
        with nc.Block() as block:

            @block.scalar
            def _(act):
                for dst, src in loads:
                    act.dma_start(dst, src).then_inc(loaded, 16)
                act.wait_ge(loaded, n_loads)
                for k in range(3):
                    nc.scalar.activation(BW[:, k, :], BC[:, k:k + 1].to_broadcast([P, P]), ACT.Copy)\
                        .then_inc(cols, 1)

            @block.gpsimd
            def _(pool):
                nc.gpsimd.memset(K.ONES[:], 1.0).then_inc(consts, 1)
                nc.gpsimd.memset(K.IDENT[:], 0.0).then_inc(consts, 1)
                nc.gpsimd.memset(K.XT[:, NP:NP + 2 * P], 0.0).then_inc(consts, 1)
                nc.gpsimd.memset(K.NEG_HALF[:], -0.5).then_inc(consts, 1)
                nc.gpsimd.iota(K.IOTA[:], pattern=[[1, 32]], base=-32, channel_multiplier=0,
                               allow_small_or_imprecise_dtypes=True).then_inc(consts, 1)
                nc.gpsimd.iota(K.OVERFLOW[:], pattern=[[P, T]], base=8 * CAPACITY, channel_multiplier=1,
                               allow_small_or_imprecise_dtypes=True).then_inc(consts, 1)
                nc.gpsimd.memset(K.ZERO[:], 0.0).then_inc(consts, 1)
                pool.wait_ge(consts, 7)
                nc.gpsimd.affine_select(out=K.IDENT[:], in_=K.IDENT[:], compare_op=ALU.not_equal, fill=1.0,
                                        base=0, pattern=[[-1, P]], channel_multiplier=1).then_inc(consts, 1)
                nc.gpsimd.affine_select(out=K.LOWER[:], in_=K.ONES[:], compare_op=ALU.is_ge, fill=0.0,
                                        base=0, pattern=[[1, P]], channel_multiplier=-1).then_inc(consts, 1)
                nc.gpsimd.memset(K.COMB[:], 0.0).then_inc(consts, 1)
                pool.wait_ge(consts, 10)
                for k in range(2):
                    for s in range(3):
                        nc.gpsimd.affine_select(
                            out=K.COMB[:, k * HC:(k + 1) * HC], in_=K.COMB[:, k * HC:(k + 1) * HC],
                            compare_op=ALU.not_equal, fill=1.0, base=-(3 * HC * k + HC * s),
                            pattern=[[-1, HC]], channel_multiplier=1).then_inc(consts, 1)
                        pool.wait_ge(consts, 11 + 3 * k + s)

            @block.tensor
            def _(pe):
                pe.wait_ge(loaded, n_loads)
                nc.tensor.matmul(K.PS[:, 0, 0:16], W0[:], SEL0[:], start=True, stop=True)
                nc.tensor.matmul(K.PS[:, 1, 0:1], WT2[:], DST2[:], start=True, stop=True)
                nc.tensor.matmul(K.PS[:, 2, 0:2], W3[:], A3[:], start=True, stop=True)
                pe.wait_ge(cols, 3)
                nc.tensor.matmul(K.PS[:, 3, 0:16], BW[:, 0, :], SEL0[:], start=True, stop=True)
                nc.tensor.matmul(K.PS[:, 4, 0:1], BW[:, 1, :], DST2[:], start=True, stop=True)
                nc.tensor.matmul(K.PS[:, 5, 0:2], BW[:, 2, :], A3[:], start=True, stop=True)
                nc.tensor.matmul(K.PS[0:HEADS, 6, 0:1], SEL0[:, 0:HEADS], BC[:, 0:1], start=True, stop=True)\
                    .then_inc(products, 1)

            @block.vector
            def _(v):
                v.wait_ge(loaded, n_loads)
                v.wait_ge(products, 1)
                nc.vector.tensor_copy(K.WP0[:, P:P + 16], K.PS[:, 0, 0:16])
                nc.vector.tensor_copy(K.WP2[:, P:P + 1], K.PS[:, 1, 0:1])
                nc.vector.tensor_copy(K.WP3[:, P:P + 2], K.PS[:, 2, 0:2])
                nc.vector.tensor_scalar(K.BP0[:, P:P + 8], K.PS[:, 3, 0:8], AB[:, 0:1], None, ALU.add)
                nc.vector.tensor_copy(K.BP0[:, P + 8:P + 16], K.PS[:, 3, 8:16])
                nc.vector.tensor_copy(K.BP2[:, P:P + 1], K.PS[:, 4, 0:1])
                nc.vector.tensor_scalar(K.BP3[:, P:P + 1], K.PS[:, 5, 0:1], AB[:, 1:2], None, ALU.add)
                nc.vector.tensor_copy(K.BP3[:, P + 1:P + 2], K.PS[:, 5, 1:2])
                nc.vector.tensor_scalar(K.SB8[:], K.PS[0:HEADS, 6, 0:1], AB[0:HEADS, 0:1], None, ALU.add)


def norm_project_stage(nc, K, name, W, n, per, dest, bias=None, twice=False, affine=False, row=None,
                       loads=(), arrival=None):
    ctx, sb, sem = open_stage(nc, name)
    with ctx:
        ST = sb("stats", [P, T, 6], F32)
        M = sb("moments", [P, 6, T], F32)
        var_ready, rstd_ready, normed = sem("var_ready"), sem("rstd_ready"), sem("normed")
        transposed, xt_ready = sem("transposed"), sem("xt_ready")
        projected, taken, dve = sem("projected"), sem("taken"), sem("dve")
        loaded, powered, powered_mean, normed_once = sem("loaded"), sem("powered"), sem("powered_mean"), sem("normed_once")
        row_done, row_taken, row_stored = sem("row_done"), sem("row_taken"), sem("row_stored")
        passes = 2 if twice else 1
        chunks = ARRIVING if arrival else CHUNKS
        if arrival:
            arrival.open(sem)
        items = [(rnd, c) for rnd in range(passes) for c in range(len(chunks))]
        tgroups = [(t, min(4, T - t)) for t in range(0, T, 4)]
        pgroups = [(t, min(per, T - t)) for t in range(0, T, per)]

        def ending_in(groups, c):
            t0, k = chunks[c]
            return [(g, t, m) for g, (t, m) in enumerate(groups) if t0 < t + m <= t0 + k]

        def bank(g, k):
            return K.PS[:, 4 + g % 4, 0:k * n].rearrange("p (k n) -> p k n", n=n)

        with nc.Block() as block:

            @block.vector
            def _(v):
                link = Link(v, dve)

                def variance(rnd, c):
                    t0, k = chunks[c]
                    src, ts = (K.XN if rnd else K.X), slice(t0, t0 + k)
                    if arrival:
                        arrival.add(v, c)
                    if rnd:
                        v.wait_ge(normed_once, c + 1)
                    for t in range(t0, t0 + k):
                        last = nc.vector.bn_stats(ST[:, t, :], src[:, t, :])
                    link(last)
                    nc.vector.tensor_tensor(M[:, 0, ts], ST[:, ts, 1], ST[:, ts, 4], ALU.add)
                    nc.vector.tensor_tensor(M[:, 1, ts], ST[:, ts, 1], ST[:, ts, 4], ALU.subtract)
                    link(nc.vector.tensor_tensor(M[:, 2, ts], ST[:, ts, 2], ST[:, ts, 5], ALU.add))
                    nc.vector.tensor_scalar(M[:, 0, ts], M[:, 0, ts], 0.5, None, ALU.mult)
                    link(nc.vector.tensor_tensor(M[:, 3, ts], M[:, 1, ts], M[:, 1, ts], ALU.mult))
                    link(nc.vector.scalar_tensor_tensor(M[:, 2, ts], M[:, 3, ts], P / 4.0, M[:, 2, ts], ALU.mult, ALU.add))
                    nc.vector.tensor_scalar(M[:, 4, ts], M[:, 2, ts], 1.0 / P, LN_EPS, ALU.mult, ALU.add)\
                        .then_inc(var_ready, 1)

                def norm(i):
                    rnd, c = items[i]
                    if rnd < passes - 1:
                        return
                    t0, k = chunks[c]
                    src = K.XN if rnd else K.X
                    v.wait_ge(rstd_ready, i + 1)
                    for t in range(t0, t0 + k):
                        last = nc.vector.tensor_scalar(K.XN[:, t, :], src[:, t, :], M[:, 0, t:t + 1], M[:, 5, t:t + 1],
                                                       ALU.subtract, ALU.mult)
                    last.then_inc(normed, 1)

                def take(c):
                    for g, t, k in ending_in(pgroups, c):
                        v.wait_ge(projected, g + 1)
                        nc.vector.tensor_tensor(dest(t, k), bank(g, k), bcast_mid(bias, k), ALU.add).then_inc(taken, 1)

                variance(*items[0])
                for i, (rnd, c) in enumerate(items):
                    if i + 1 < len(items):
                        variance(*items[i + 1])
                    norm(i)
                    if bias is not None and rnd == passes - 1 and c:
                        take(c - 1)
                if bias is not None:
                    take(len(chunks) - 1)

            @block.sync
            def _(sp):
                for dst, src in loads:
                    sp.dma_start(dst, src).then_inc(loaded, 16)
                if loads:
                    sp.wait_ge(loaded, 16 * len(loads))
                if row is not None:
                    sp.wait_ge(row_taken, len(tgroups))
                    sp.dma_start(row[3], row[2]).then_inc(row_stored, 16)
                    sp.wait_ge(row_stored, 16)

            @block.gpsimd
            def _(pool):
                if arrival:
                    arrival.fetch(pool, 0)
                for i, (rnd, c) in enumerate(items):
                    if arrival and c + 1 < len(chunks):
                        arrival.fetch(pool, c + 1)
                    t0, k = chunks[c]
                    pool.wait_ge(var_ready, i + 1)
                    power = nc.gpsimd.tensor_tensor(M[:, 5, t0:t0 + k], M[:, 4, t0:t0 + k], K.NEG_HALF[:, 0:k], ALU.pow)
                    if rnd < passes - 1:
                        power.then_inc(powered, 1)
                        pool.wait_ge(powered, c + 1)
                        nc.gpsimd.tensor_tensor(M[:, 3, t0:t0 + k], M[:, 0, t0:t0 + k], M[:, 5, t0:t0 + k], ALU.mult)\
                            .then_inc(powered_mean, 1)
                        pool.wait_ge(powered_mean, c + 1)
                        nc.gpsimd.tensor_tensor(M[:, 3, t0:t0 + k], K.ZERO[:, 0:k], M[:, 3, t0:t0 + k], ALU.subtract)\
                            .then_inc(rstd_ready, 1)
                    else:
                        power.then_inc(rstd_ready, 1)

            @block.tensor
            def _(pe):
                for c in range(len(chunks)):
                    pe.wait_ge(normed, c + 1)
                    for g, t, k in ending_in(tgroups, c):
                        if g >= 3:
                            pe.wait_ge(xt_ready, g - 2)
                        for j in range(k):
                            last = nc.tensor.transpose(K.PS[:, g % 3, j * P:(j + 1) * P], K.XN[:, t + j, :], K.IDENT[:])
                        last.then_inc(transposed, 1)
                    for g, t, k in ending_in(pgroups, c):
                        pe.wait_ge(xt_ready, (t + k - 1) // 4 + 1)
                        if g >= 4:
                            pe.wait_ge(taken, g - 3)
                        for j in range(k):
                            last = nc.tensor.matmul(K.PS[:, 4 + g % 4, j * n:(j + 1) * n],
                                                    K.XT[:, (t + j) * P:(t + j + 1) * P], W, start=True, stop=True)
                        last.then_inc(projected, 1)
                    if row is not None:
                        m = row[0].shape[1]
                        for g, t, k in ending_in(tgroups, c):
                            pe.wait_ge(xt_ready, g + 1)
                            if g:
                                pe.wait_ge(row_taken, g)
                            nc.tensor.matmul(K.PS[0:m, 3, 0:k * P], row[0], K.XT[:, t * P:(t + k) * P],
                                             start=True, stop=True).then_inc(row_done, 1)

            @block.scalar
            def _(act):
                for i in range((passes - 1) * len(chunks)):
                    t0, k = chunks[i]
                    act.wait_ge(rstd_ready, i + 1)
                    for t in range(t0, t0 + k):
                        last = nc.scalar.activation(K.XN[:, t, :], K.X[:, t, :], ACT.Identity, bias=M[:, 3, t:t + 1],
                                                    scale=M[:, 5, t:t + 1])
                    last.then_inc(normed_once, 1)
                for c in range(len(chunks)):
                    for g, t, k in ending_in(tgroups, c):
                        act.wait_ge(transposed, g + 1)
                        out, ps = K.XT[:, t * P:(t + k) * P], K.PS[:, g % 3, 0:k * P]
                        if affine:
                            nc.scalar.activation(out, ps, ACT.Identity, bias=K.GB[:, 1:2], scale=K.GB[:, 0:1])\
                                .then_inc(xt_ready, 1)
                        else:
                            nc.scalar.activation(out, ps, ACT.Copy).then_inc(xt_ready, 1)
                    if bias is None:
                        for g, t, k in ending_in(pgroups, c):
                            act.wait_ge(projected, g + 1)
                            nc.scalar.activation(dest(t, k), bank(g, k), ACT.Copy).then_inc(taken, 1)
                    if row is not None:
                        m = row[0].shape[1]
                        for g, t, k in ending_in(tgroups, c):
                            act.wait_ge(row_done, g + 1)
                            nc.scalar.activation(row[2][0:m, t * P:(t + k) * P], K.PS[0:m, 3, 0:k * P], ACT.Identity,
                                                 bias=row[1], scale=1.0).then_inc(row_taken, 1)


def global_max(nc, eng_link, v, pe_done, ready, d, n, K, tmp):
    link = eng_link
    nc.vector.tensor_reduce(tmp.PM[:, 0:n], d, AX.X, ALU.max).then_inc(ready, 1)
    v.wait_ge(pe_done, 1)
    link(nc.vector.tensor_reduce(tmp.G8[0:n, :], K.PS[0:n, 0, 0:P], AX.X, ALU.max))
    nc.vector.tensor_scalar(tmp.DG[0:n, 0:n], K.IDENT[0:n, 0:n], tmp.G8[0:n, 0:1], None, ALU.mult).then_inc(ready, 1)
    v.wait_ge(pe_done, 2)
    link(nc.vector.tensor_copy(tmp.GB[:, 0:n], K.PS[:, 1, 0:n]))


def global_max_products(nc, pe, pe_done, ready, n, K, tmp):
    pe.wait_ge(ready, 1)
    nc.tensor.transpose(K.PS[0:n, 0, 0:P], tmp.PM[:, 0:n], K.IDENT[:]).then_inc(pe_done, 1)
    pe.wait_ge(ready, 2)
    nc.tensor.matmul(K.PS[:, 1, 0:n], K.ONES[0:n, :], tmp.DG[0:n, 0:n], start=True, stop=True).then_inc(pe_done, 1)


def max_buffers(sb, n):
    tmp = Core()
    tmp.PM, tmp.G8 = sb("pm", [P, n], F32), sb("g8", [n, 1], F32)
    tmp.DG, tmp.GB = sb("dg", [n, n], F32), sb("gb", [P, n], F32)
    return tmp


def split_stage(nc, K, name, HP, heads, hd, score_col, sets, XS, V, coef=None, keep=None, first_loads=(),
                store=None, then_load=None):
    ctx, sb, sem = open_stage(nc, name)
    with ctx:
        tmp = max_buffers(sb, heads)
        DM = sb("dm", [P, heads, T], F32)
        EX = sb("ex", [P, len(sets), T, heads], F32)
        Y = sb("y", [P, 4, T, heads], F32) if coef else None
        ready, pe_done, dve = sem("ready"), sem("pe_done"), sem("dve")
        dm_ready, ex_ready, y_ready, coef_ready = sem("dm_ready"), sem("ex_ready"), sem("y_ready"), sem("coef_ready")
        v_ready, part_ready, stored, loaded = sem("v_ready"), sem("part_ready"), sem("stored"), sem("loaded")
        H4 = HP[:, :, 0:heads * hd].rearrange("p t (h c) -> p t h c", c=hd)
        D = HP[:, :, score_col:score_col + heads]
        halves = (slice(0, HALF), slice(HALF, T))
        with nc.Block() as block:

            @block.sync
            def _(sp):
                for dst, src in first_loads:
                    sp.dma_start(dst, src).then_inc(loaded, 16)
                if first_loads and store is None:
                    sp.wait_ge(loaded, 16 * len(first_loads))
                if store is not None:
                    sp.dma_start(*store).then_inc(stored, 16)
                    sp.wait_ge(stored, 16)
                    sp.dma_start(*then_load).then_inc(loaded, 16)
                    sp.wait_ge(loaded, 16 * len(first_loads) + 16)

            @block.tensor
            def _(pe):
                global_max_products(nc, pe, pe_done, ready, heads, K, tmp)

            @block.vector
            def _(v):
                link = Link(v, dve)
                global_max(nc, link, v, pe_done, ready, D.rearrange("p t h -> p h t"), heads, K, tmp)
                nc.vector.tensor_tensor(DM[:].rearrange("p h t -> p t h"), D, bcast_mid(tmp.GB[:, 0:heads], T),
                                        ALU.subtract).then_inc(dm_ready, 1)
                if coef:
                    S = HP[:, :, score_col - heads:score_col]
                    link(nc.vector.tensor_tensor(Y[:, 0], S, bcast_mid(tmp.GB[:, 0:heads], T), ALU.add))
                    link(nc.vector.scalar_tensor_tensor(Y[:, 1], Y[:, 0], SLOPE, Y[:, 0], ALU.mult, ALU.max))
                    link(nc.vector.tensor_tensor(Y[:, 2], Y[:, 0], Y[:, 1], ALU.subtract))
                    nc.vector.scalar_tensor_tensor(Y[:, 3], Y[:, 0], SLOPE, Y[:, 1], ALU.mult, ALU.subtract)\
                        .then_inc(y_ready, 1)
                if keep is not None:
                    nc.vector.tensor_copy(keep[:], D)
                for k in range(len(sets)):
                    v.wait_ge(ex_ready, k + 1)
                    for half, ts in enumerate(halves):
                        if k:
                            v.wait_ge(v_ready, 6 * k - 1 + half)
                        nc.vector.tensor_copy(V[:, ts, :, hd], EX[:, k, ts])
                        nc.vector.tensor_tensor(V[:, ts, :, 0:hd], H4[:, ts],
                                                bcast_last(EX[:, k, ts].rearrange("p t h -> p (t h)"), hd)
                                                .rearrange("p (t h) c -> p t h c", t=HALF), ALU.mult).then_inc(v_ready, 1)
                    for part in range(2):
                        for half, ts in enumerate(halves):
                            v.wait_ge(part_ready, 4 * k + 2 * part + half + 1)
                            left = (V[:, ts], XS[k](2)[:, ts])[part]
                            nc.vector.tensor_tensor(left, V[:, ts], XS[k](part)[:, ts], ALU.subtract).then_inc(v_ready, 1)

            @block.scalar
            def _(act):
                act.wait_ge(dm_ready, 1)
                for k, slope in enumerate(sets):
                    nc.scalar.activation(EX[:, k], DM[:].rearrange("p h t -> p t h"), ACT.Exp, scale=slope)\
                        .then_inc(ex_ready, 1)
                if coef:
                    act.wait_ge(y_ready, 1)
                    nc.scalar.activation(coef[0], Y[:, 2].rearrange("p (a t) h -> p a t h", a=2), ACT.Exp)
                    nc.scalar.activation(coef[1], Y[:, 3].rearrange("p (a t) h -> p a t h", a=2), ACT.Exp)
                for k in range(len(sets)):
                    for part in range(2):
                        for half, ts in enumerate(halves):
                            act.wait_ge(v_ready, 6 * k + 2 * part + half + 1)
                            nc.scalar.activation(XS[k](part)[:, ts], V[:, ts], ACT.Copy).then_inc(part_ready, 1)


def edge_sum_stage(nc, K, name, moving, n, finish, links, bufs=None, adj=None, landing=None, ahead=None,
                   store=None):
    ctx, sb, sem = open_stage(nc, name)
    with ctx:
        adj_in, edges_made = [sem("adj_in0"), sem("adj_in1")], sem("edges_made")
        ED = sb("edges", [P, 2, T, P], U8)
        TMP = bufs(sb) if bufs else None
        staged, summed, sum_free, dve = sem("staged"), sem("summed"), sem("sum_free"), sem("dve")
        passed, stored = sem("passed"), sem("stored")
        with nc.Block() as block:

            @block.sync
            def _(sp):
                if adj is not None:
                    def load(it, q, again=True):
                        if again:
                            sp.wait_ge(edges_made, it + 1)
                        sp.dma_start(landing[q], adj[bass.ds(it, 1), :, :].rearrange("a p (b i) -> p (a b) i", i=P))\
                            .then_inc(adj_in[q], 16)

                    load(4, 0, again=False)
                    sp.dma_start(*store).then_inc(stored, 16)
                    load(5, 1)
                    with sp.Fori(3, T // 2) as t:
                        for q in range(2):
                            load(2 * t + q, q)
                    sp.wait_ge(stored, 16)

            @block.scalar
            def _(act):
                with act.Fori(0, T // 2) as t:
                    for q in range(2):
                        if adj is not None:
                            act.wait_ge(edges_made, 2 * t + q + 3)
                        act.wait_ge(summed, 2 * t + q + 1)
                        nc.scalar.activation(
                            ED[:, q].rearrange("p b i -> p (b i)").bitcast(U16),
                            K.EDGE[:, bass.ds(2 * t + q, 1)].rearrange("p a b i -> p (a b i)").bitcast(U16),
                            ACT.Copy).then_inc(staged, 1)

            @block.tensor
            def _(pe):
                with pe.Fori(0, T // 2) as t:
                    for q in range(2):
                        pe.wait_ge(staged, 2 * t + q + 1)
                        pe.wait_ge(sum_free, 2 * t + q + 1)
                        pe.sem_inc(passed, 1)
                        for j in range(T):
                            last = nc.tensor.matmul(K.PS[:, q, 0:n], ED[:, q, j, :].bitcast(FP8), moving(j),
                                                    start=(j == 0), stop=(j == T - 1))
                        last.then_inc(summed, 1)

            @block.vector
            def _(v):
                link = Link(v, dve)
                v.sem_inc(sum_free, 2)
                v.sem_inc(summed, 2)
                v.sem_inc(edges_made, 2)

                def make_edges(it, source):
                    nc.vector.tensor_scalar(K.EDGE[:, bass.ds(it, 1), :, :].rearrange("p a b i -> p (a b i)"),
                                            source.rearrange("p b i -> p (b i)"),
                                            float(ONE8), None, ALU.mult).then_inc(edges_made, 1)

                def total(it, q):
                    v.wait_ge(summed, it + 3)
                    v.wait_ge(sum_free, it + 2)
                    finish(v, link, it, K.PS[:, q, 0:n], 0, sum_free, TMP)

                if adj is not None:
                    make_edges(0, ahead[0])
                    for it in range(4):
                        if it < 3:
                            make_edges(it + 1, (*ahead, landing[1])[it + 1])
                        else:
                            v.wait_ge(adj_in[0], 16)
                            make_edges(4, landing[0])
                        total(it, it % 2)
                    with v.Fori(2, T // 2 - 1) as t:
                        for q in range(2):
                            v.wait_ge(adj_in[1 - q], (16 * t - 16, 16 * t)[q])
                            make_edges(2 * t + q + 1, landing[1 - q])
                            total(2 * t + q, q)
                    v.wait_ge(adj_in[1], 16 * (T // 2 - 2))
                    make_edges(T - 1, landing[1])
                    for q in range(2):
                        total(T - 2 + q, q)
                    return
                with v.Fori(0, T // 2) as t:
                    for q in range(2):
                        v.wait_ge(summed, 2 * t + q + 3)
                        v.wait_ge(sum_free, 2 * t + q + 2)
                        finish(v, link, 2 * t + q, K.PS[:, q, 0:n], 2 * links * t, sum_free, TMP)
                link.skip(2 * links * (T // 2 - 1))


def head_loop_stage(nc, K, XD, SD, XN0, D0, C1, C2, NAT, A0, RES, slots):
    ctx, sb, sem = open_stage(nc, "head_loop")
    with ctx:
        RING, MRING = 8, 6
        back, mback = ([ring_distance(g, 2 * T, ring) for g in range(2 * T)] for ring in (RING, MRING))
        N_ACT = 15
        ON_ACT = [j for j in range(T) if (j * N_ACT) % T < N_ACT]
        EVAC_AT, COMB_AT, FIN_AT = 10, 12, 18
        BIAS_AT = 6
        C = 6 * HC
        SB = sb("scores", [P, 2, HN], F32)
        XH = sb("parts", [P, 2, T, C], BF16)
        ST = sb("step", [P, RING, HN], U8)
        ME = sb("masked", [P, MRING, HN], U8)
        EV = sb("sums", [C, HN], F32)
        T1 = sb("t1", [P, HALF, HC], F32)
        T2 = sb("t2", [P, HALF, HC], F32)
        ND = sb("negd", [P, T, HEADS], F32)
        BD = sb("bigd", [P, T, HEADS + 1], F32)
        BT = sb("turn_bigd", [P, 2, T], F32)
        in_x, in_s = [sem("in_x0"), sem("in_x1")], [sem("in_s0"), sem("in_s1")]
        consts, compared, masked, summed = sem("consts"), sem("compared"), sem("masked"), sem("summed")
        turn_done, evacuated, combined, finished, dve = (sem("turn_done"), sem("evacuated"), sem("combined"),
                                                         sem("finished"), sem("dve"))
        passed, sent, bias_ready = sem("passed"), sem("sent"), sem("bias_ready")
        go, reloaded = sem("go"), sem("reloaded")
        M0, S0 = 2 * T, 2 * N_ACT
        U0 = M0
        pieces = [(512 * b, min(512, HN - 512 * b)) for b in range(4)]

        def banks(q):
            return K.PS[:, 4 * q:4 * q + 4, :].rearrange("p b n -> p (b n)")

        def evacuate(act, q, n):
            act.wait_ge(turn_done, n + 2)
            act.wait_ge(combined, n + 1)
            nc.scalar.activation(EV[:], banks(q)[0:C, 0:HN], ACT.Copy).then_inc(evacuated, 1)

        def combine(pe, q, n):
            pe.wait_ge(evacuated, n + 1)
            for i in range(HALF):
                last = nc.tensor.matmul(K.PS[:, 4 * q + 3, i * 2 * HC:(i + 1) * 2 * HC], EV[:, i * P:(i + 1) * P],
                                        K.COMB[0:C, :], start=True, stop=True)
            last.then_inc(combined, 1)

        def finish(v, link, q, n, slot, base):
            v.wait_ge(combined, n + 2)
            sums = K.PS[:, 4 * q + 3, 0:HALF * 2 * HC].rearrange("p (t c) -> p t c", c=2 * HC)
            c1, c2 = (bcast_last(c[:, slot, :].rearrange("p a t -> p (a t)"), HC) for c in (C1, C2))
            a0, res = (a[:, slot, :, :].rearrange("p a t c -> p (a t) c") for a in (A0, RES))
            nc.vector.tensor_tensor(T1[:], sums[:, :, 0:HC], c1, ALU.mult)
            link(nc.vector.tensor_tensor(T2[:], a0, sums[:, :, HC:2 * HC], ALU.subtract), base)
            link(nc.vector.tensor_tensor(T2[:], T2[:], c2, ALU.mult), base)
            nc.vector.tensor_tensor(res, T1[:], T2[:], ALU.add).then_inc(finished, 1)

        with nc.Block() as block:

            @block.sync
            def _(sp):
                with sp.Fori(0, 2) as half:
                    with sp.Fori(0, HEADS // 2) as pair:
                        for q in range(2):
                            n = 8 * half + 2 * pair + q
                            sp.wait_ge(compared, N_ACT * n + N_ACT)
                            sp.sem_inc(sent, 1)
                            sp.wait_ge(masked, T * n + T)
                            sp.sem_inc(sent, 1)
                            sp.wait_ge(turn_done, n + 1)
                            sp.sem_inc(sent, 1)
                            sp.dma_start(SB[:, q, :], SD[bass.ds(2 * pair + q, 1), bass.ds(HN * half, HN)]
                                         .rearrange("a n -> (a n)").partition_broadcast(P)).then_inc(in_s[q], 16)
                            sp.dma_start(XH[:, q, :, :],
                                         XD[:, :, bass.ds(2 * pair + q, 1), :].rearrange("p t a c -> p t (a c)")).then_inc(in_x[q], 16)
                sp.dma_start(K.XN[:], XN0).then_inc(reloaded, 16)
                sp.dma_start(*empty_slots(K, slots, P)).then_inc(reloaded, 16)
                sp.wait_ge(reloaded, 32)

            @block.scalar
            def _(act):
                act.wait_ge(consts, 2)
                with act.Fori(0, 2) as half:
                    with act.Fori(0, HEADS // 2) as pair:
                        w = 4 * half + pair
                        for q in range(2):
                            act.wait_ge(bias_ready, 2 * w + q + 1)
                            act.wait_ge(in_s[q], 16 * w + 16)
                            act.sem_inc(go, 1)
                            for j in range(T):
                                if j == EVAC_AT:
                                    evacuate(act, 1 - q, 2 * w + q)
                                if j in ON_ACT:
                                    slot = (T * q + j) % RING
                                    act.wait_ge(masked, 2 * T * w + (T * q + j + 1 + M0 - back[T * q + j]))
                                    act.sem_inc(go, 1)
                                    nc.scalar.activation(ST[:, slot, :].bitcast(FP8), SB[:, q, :], ACT.Sigmoid,
                                                         bias=BT[:, q, j:j + 1], scale=BIG,
                                                         saturate=False).then_inc(compared, 1)
                evacuate(act, 1, 2 * HEADS)

            @block.vector
            def _(v):
                link = Link(v, dve)
                for k, prime in ((S0, compared), (M0, masked), (U0, summed), (2, turn_done), (1, combined),
                                 (1, finished)):
                    v.sem_inc(prime, k)
                nc.vector.memset(K.PS[:, 4:8, :], 0.0).then_inc(consts, 1)
                for half in range(2):
                    for h in range(HEADS):
                        nc.vector.tensor_copy(A0[:, 1 + 8 * half + h, :, :], NAT[:, HALF * half:HALF * (half + 1), h, :])
                for a in (A0[:, 0, :, :], C1[:, 0, :], C2[:, 0, :]):
                    last = nc.vector.memset(a, 0.0)
                link(last)
                nc.vector.tensor_scalar(BD[:, :, 0:HEADS], D0, BIG, None, ALU.mult)
                nc.vector.tensor_scalar(BD[:, :, HEADS], D0[:, :, 0], BIG, None, ALU.mult).then_inc(consts, 1)
                nc.vector.tensor_scalar(BT[:, 0, :], D0[:, :, 0], BIG, None, ALU.mult).then_inc(bias_ready, 1)
                v.wait_ge(consts, 2)
                link(nc.vector.tensor_scalar(ND[:], D0, -1.0, None, ALU.mult))
                links = 2 * (T - N_ACT + 2)

                with v.Fori(0, 2) as half:
                    with v.Fori(0, HEADS // 2) as pair:
                        w = 4 * half + pair
                        for q in range(2):
                            made = {}

                            def mask(j):
                                slot = (T * q + j) % RING
                                if j in ON_ACT:
                                    v.wait_ge(compared, 2 * N_ACT * w + (N_ACT * q + ON_ACT.index(j) + 1 + S0))
                                else:
                                    v.wait_ge(dve, links * w + made[j])
                                v.wait_ge(summed, 2 * T * w + (T * q + j + 1 + U0 - mback[T * q + j]))
                                nc.vector.tensor_tensor(
                                    ME[:, (T * q + j) % MRING, :].rearrange("p (t i) -> p t i", i=P).bitcast(U32),
                                    ST[:, slot, :].rearrange("p (t i) -> p t i", i=P).bitcast(U32),
                                    K.EDGE[:, bass.ds(HALF * half, HALF), j, :].bitcast(U32),
                                    ALU.bitwise_and).then_inc(masked, 1)

                            v.wait_ge(in_s[q], 16 * w + 16)
                            for j in range(T):
                                if j == BIAS_AT:
                                    nc.vector.tensor_scalar(BT[:, 1 - q, :], BD[:, :, bass.ds(2 * pair + q + 1, 1)]
                                                            .rearrange("p t a -> p (t a)"), 1.0, None, ALU.mult)\
                                        .then_inc(bias_ready, 1)
                                if j == FIN_AT:
                                    n = 2 * w + q
                                    finish(v, link, 1 - q, n, bass.ds(n, 1), links * w)
                                if j not in ON_ACT:
                                    v.wait_ge(masked, 2 * T * w + (T * q + j + 1 + M0 - back[T * q + j]))
                                    nc.vector.tensor_scalar(ST[:, (T * q + j) % RING, :], SB[:, q, :],
                                                            ND[:, j, bass.ds(2 * pair + q, 1)], float(ONE8),
                                                            ALU.is_ge, ALU.mult).then_inc(dve, 1)
                                    link.n += 1
                                    made[j] = link.n
                                if j >= 1:
                                    mask(j - 1)
                            mask(T - 1)
                link.skip(links * 7)
                finish(v, link, 1, 2 * HEADS, slice(2 * HEADS, 2 * HEADS + 1), 0)

            @block.tensor
            def _(pe):
                with pe.Fori(0, 2 * HEADS // 2) as w:
                    for q in range(2):
                        pe.wait_ge(in_x[q], 16 * w + 16)
                        pe.wait_ge(finished, 2 * w + q + 1)
                        for j in range(T):
                            if j == COMB_AT:
                                combine(pe, 1 - q, 2 * w + q)
                            slot = (T * q + j) % MRING
                            pe.wait_ge(masked, 2 * T * w + (T * q + j + 1 + M0))
                            pe.sem_inc(passed, 1)
                            for b, (at, n) in enumerate(pieces):
                                last = nc.tensor.matmul(K.PS[0:C, 4 * q + b, 0:n], XH[:, q, j, :],
                                                        ME[:, slot, at:at + n].bitcast(FP8),
                                                        start=(j == 0), stop=(j == T - 1))
                            last.then_inc(summed, 1)
                        pe.wait_ge(summed, 2 * T * w + (T * q + T + U0))
                        nc.tensor.sem_inc(turn_done, 1)
                combine(pe, 1, 2 * HEADS)


def head_merge_stage(nc, K, RES):
    ctx, sb, sem = open_stage(nc, "head_merge")
    with ctx:
        RD = sb("rden", [P, 16, HALF], F32)
        H = sb("h", [P, T, P], F32)
        E = sb("e", [P, T, P], F32)
        dve, low, expd = sem("dve"), sem("low"), sem("expd")
        with nc.Block() as block:

            @block.vector
            def _(v):
                link = Link(v, dve)
                link(nc.vector.tensor_scalar(RD[:], RES[:, 1:17, :, HD], TINY, None, ALU.max))
                link(nc.vector.reciprocal(RD[:], RD[:]))
                for half in range(2):
                    ts = slice(HALF * half, HALF * (half + 1))
                    for h in range(HEADS):
                        n = 8 * half + h
                        last = nc.vector.tensor_tensor(H[:, ts, HD * h:HD * (h + 1)], RES[:, 1 + n, :, 0:HD],
                                                       bcast_last(RD[:, n, :], HD), ALU.mult)
                    link(last)
                    link(nc.vector.tensor_tensor(H[:, ts, :], H[:, ts, :], K.XN[:, ts, :], ALU.add))
                    nc.vector.tensor_scalar(E[:, ts, :], H[:, ts, :], 0.0, None, ALU.min).then_inc(low, 1)
                for half in range(2):
                    ts = slice(HALF * half, HALF * (half + 1))
                    v.wait_ge(expd, half + 1)
                    link(nc.vector.scalar_tensor_tensor(H[:, ts, :], H[:, ts, :], 0.0, E[:, ts, :], ALU.max, ALU.add))
                    link(nc.vector.scalar_tensor_tensor(K.X[:, ts, :], H[:, ts, :], 1.0, K.X[:, ts, :],
                                                        ALU.subtract, ALU.add))

            @block.scalar
            def _(act):
                for half in range(2):
                    ts = slice(HALF * half, HALF * (half + 1))
                    act.wait_ge(low, half + 1)
                    nc.scalar.activation(E[:, ts, :], E[:, ts, :], ACT.Exp).then_inc(expd, 1)


def layer0_gnn(nc, K, D):
    ctx = ExitStack()
    with ctx:
        sb = lambda n, shape, dt: ctx.enter_context(nc.sbuf_tensor(f"g0_{n}", shape, dt))
        A0 = sb("a0", [P, 17, HALF, HC], F32)
        C1 = sb("c1", [P, 17, HALF], F32)
        C2 = sb("c2", [P, 17, HALF], F32)
        D0 = sb("d0", [P, T, HEADS], F32)
        flat = A0[:].rearrange("p a t c -> p (a t c)")
        HP = flat[:, 0:T * 144].rearrange("p (t c) -> p t c", c=144)
        xt = K.XT[:]
        V = xt[:, 0:T * HEADS * HC].rearrange("p (t h c) -> p t h c", h=HEADS, c=HC)
        NAT = xt[:, 0:T * HEADS * HC].rearrange("p (t h c) -> p t h c", h=HEADS, c=HC)
        RES = xt[:, 0:17 * HALF * HC].rearrange("p (a t c) -> p a t c", t=HALF, c=HC)
        ahead = [K.EDGE[:, t:t + 4].rearrange("p a b i -> p (a b i)").bitcast(I32).rearrange("p (b i) -> p b i", i=P)
                 for t in (T - 12, T - 8, T - 4)]
        landing = [b.rearrange("p (b i) -> p b i", i=P).bitcast(I32)
                   for b in (flat[:, 0:NP], K.XN[:].rearrange("p t d -> p (t d)"))]

        def adj_tile(it):
            return D["adj"][it].rearrange("p (b i) -> p b i", i=P)

        inner = ExitStack()
        with inner:
            XALL = inner.enter_context(nc.sbuf_tensor("g0_xall", [P, T, HEADS, 6 * HC], BF16))
            SROW = XALL[0:HEADS, :, :, :].rearrange("p t h c -> p (t h c)")[:, 0:2 * NP].bitcast(F32)
            norm_project_stage(nc, K, "p0", K.WP0[:], 144, 3, lambda t, k: HP[:, t:t + k, :], bias=K.BP0[:],
                               row=(K.WP0[:, P:P + HEADS], K.SB8[:], SROW, D["sd"]))

            def parts(k):
                return lambda s: XALL[:, :, :, (3 * k + s) * HC:(3 * k + s + 1) * HC]

            def natural(c):
                return c[:, 1:17, :].rearrange("p (a h) t -> p a t h", a=2)

            split_stage(nc, K, "x0", HP, HEADS, HD, P + HEADS, (1.0, SLOPE), (parts(0), parts(1)), V,
                        coef=(natural(C1), natural(C2)), keep=D0,
                        first_loads=[(ahead[it], adj_tile(it)) for it in range(3)],
                        store=(D["xn0"], K.XN[:]), then_load=(landing[1], adj_tile(3)))

            def sum_parts(v, link, it, ps, base, done, tmp):
                nc.vector.tensor_reduce(NAT[:, bass.ds(it, 1), :, :].rearrange("p a h c -> p (a h) c"),
                                        ps.rearrange("p (h s c) -> p h c s", h=HEADS, s=3), AX.X, ALU.add).then_inc(done, 1)

            edge_sum_stage(nc, K, "a0", lambda j: XALL[:, j, :, 3 * HC:6 * HC], 3 * HEADS * HC, sum_parts, 0,
                           adj=D["adj"], landing=landing, ahead=ahead, store=(D["xd"], XALL[:]))
        head_loop_stage(nc, K, D["xd"], D["sd"], D["xn0"], D0[:], C1, C2, NAT, A0, RES,
                        D["slots"][0:pair_blocks(ROUTED0) * PAIR_BLOCK, :])
        head_merge_stage(nc, K, RES)


def cosine_prepare_stage(nc, K, QK, QT, KT):
    ctx, sb, sem = open_stage(nc, "cos_prep")
    with ctx:
        COS_EPS = 1e-4
        SS = sb("ss", [P, 2, 2 * T], F32)
        POWER = sb("power", [P, T], F32)
        SQ = sb("sq", [P, T, 2 * P], F32)
        squared, ss_ready, norm_ready, normed = sem("squared"), sem("ss_ready"), sem("norm_ready"), sem("normed")
        transposed, act_taken, dve_taken, dve = sem("transposed"), sem("act_taken"), sem("dve_taken"), sem("dve")
        consts = sem("consts")
        groups = [(m, t, min(4, T - t)) for t in range(0, T, 4) for m in range(2)]
        with nc.Block() as block:

            @block.scalar
            def _(act):
                for h in range(2):
                    ts = slice(HALF * h, HALF * (h + 1))
                    for m in range(2):
                        nc.scalar.activation(SQ[:, ts, m * P:(m + 1) * P], QK[:, ts, m * P:(m + 1) * P], ACT.Square)\
                            .then_inc(squared, 1)
                for g, (m, t, k) in enumerate(groups):
                    if m == 0:
                        act.wait_ge(transposed, g + 1)
                        nc.scalar.activation(QT[:, t * P:(t + k) * P], K.PS[:, g % 8, 0:k * P], ACT.Copy)\
                            .then_inc(act_taken, 1)

            @block.gpsimd
            def _(pool):
                nc.gpsimd.memset(POWER[:], -0.5).then_inc(consts, 1)
                pool.wait_ge(consts, 1)
                for h in range(2):
                    ts = slice(2 * HALF * h, 2 * HALF * (h + 1))
                    pool.wait_ge(ss_ready, h + 1)
                    nc.gpsimd.tensor_tensor(SS[:, 1, ts], SS[:, 0, ts], POWER[:], ALU.pow).then_inc(norm_ready, 1)

            @block.vector
            def _(v):
                link = Link(v, dve)
                ss, inv = (SS[:, k, :].rearrange("p (t m) -> p t m", m=2) for k in range(2))
                for h in range(2):
                    ts = slice(HALF * h, HALF * (h + 1))
                    for m in range(2):
                        v.wait_ge(squared, 2 * h + m + 1)
                        last = nc.vector.tensor_reduce(ss[:, ts, m], SQ[:, ts, m * P:(m + 1) * P], AX.X, ALU.add)
                    link(last)
                    nc.vector.tensor_scalar(ss[:, ts, :], ss[:, ts, :], COS_EPS ** 2, None, ALU.max).then_inc(ss_ready, 1)
                for h in range(2):
                    v.wait_ge(norm_ready, h + 1)
                    for t in range(HALF * h, HALF * (h + 1)):
                        for m in range(2):
                            last = nc.vector.tensor_scalar(QK[:, t, m * P:(m + 1) * P], QK[:, t, m * P:(m + 1) * P],
                                                           inv[:, t, m:m + 1], None, ALU.mult)
                    last.then_inc(normed, 1)
                for g, (m, t, k) in enumerate(groups):
                    if m == 1:
                        v.wait_ge(transposed, g + 1)
                        nc.vector.tensor_copy(KT[:, t * P:(t + k) * P], K.PS[:, g % 8, 0:k * P]).then_inc(dve_taken, 1)

            @block.tensor
            def _(pe):
                for g, (m, t, k) in enumerate(groups):
                    pe.wait_ge(normed, 1 if t + k <= HALF else 2)
                    if g >= 8:
                        pe.wait_ge((act_taken, dve_taken)[m], (g - 8) // 2 + 1)
                    for j in range(k):
                        last = nc.tensor.transpose(K.PS[:, g % 8, j * P:(j + 1) * P], QK[:, t + j, m * P:(m + 1) * P],
                                                   K.IDENT[:])
                    last.then_inc(transposed, 1)


def ring_distance(g, steps, ring):
    if g >= ring:
        return ring
    return steps - ((steps - 1 - g) // ring) * ring


def empty_slots(K, slots, parts):
    per = slots.shape[0] // parts
    return slots.rearrange("(p k) d -> p k d", p=parts), K.ZERO[0:parts, :].unsqueeze(1).to_broadcast([parts, per, P])


def cosine_stage(nc, K, QT, KT, X1, slots):
    ctx, sb, sem = open_stage(nc, "cosine")
    with ctx:
        RING, STEPS, TURNS, LAG = 5, T // 2, T // 2, 2
        PB = sb("probs", [P, RING, 4 * P], F32)
        PA = sb("masked", [P, RING, 4 * P], F32)
        NUM = sb("num", [P, 2, P + 1], F32)
        S = sb("s", [P, 3, 2], F32)
        TM = sb("tm", [P, 2, P], F32)
        ready, scored, expd, masked, summed = sem("ready"), sem("scored"), sem("expd"), sem("masked"), sem("summed")
        taken, scales, added, dve, pool_own = sem("taken"), sem("scales"), sem("added"), sem("dve"), sem("pool_own")
        PRIME = STEPS
        back = [ring_distance(g, STEPS, RING) for g in range(STEPS)]
        emptied = sem("emptied")
        with nc.Block() as block:

            @block.sync
            def _(sp):
                sp.dma_start(*empty_slots(K, slots, P)).then_inc(emptied, 16)
                sp.wait_ge(emptied, 16)

            @block.scalar
            def _(act):
                with act.Fori(0, TURNS) as c:
                    for g in range(STEPS):
                        act.wait_ge(scored, STEPS * c + g + 1)
                        act.wait_ge(masked, STEPS * c + (g + 1 - back[g] + PRIME))
                        nc.scalar.activation(PB[:, g % RING, :], K.PS[:, g % RING, :], ACT.Exp).then_inc(expd, 1)

            @block.vector
            def _(v):
                v.sem_inc(masked, PRIME)
                v.sem_inc(summed, PRIME)
                v.sem_inc(taken, 1)
                v.sem_inc(added, 1)
                link = Link(v, dve)
                nc.vector.tensor_copy(X1[:, :, 0:P], K.XN[:])
                nc.vector.memset(X1[:, :, P:P + 1], 1.0)
                nc.vector.memset(KT[:, NP:NP + 2 * P], 0.0).then_inc(ready, 1)
                v.wait_ge(ready, 1)
                v.sem_inc(ready, 1)

                def mask(c, g):
                    v.wait_ge(expd, STEPS * c + g + 1)
                    v.wait_ge(summed, STEPS * c + (g + 1 - back[g] + PRIME))
                    nc.vector.scalar_tensor_tensor(
                        PA[:, g % RING, :].rearrange("p (a n) -> p a n", a=2),
                        K.EDGE[:, bass.ds(2 * c, 2), 2 * g:2 * g + 2, :].rearrange("p a b i -> p a (b i)"), 1.0,
                        PB[:, g % RING, :].rearrange("p (a n) -> p a n", a=2), ALU.min, ALU.mult).then_inc(masked, 1)

                def take(c):
                    v.wait_ge(summed, STEPS * c + STEPS + PRIME)
                    v.wait_ge(added, c + 1)
                    nc.vector.tensor_copy(NUM[:], K.PS[:, 5:7, 0:P + 1]).then_inc(taken, 1)

                def scale(c, base):
                    v.wait_ge(taken, c + 2)
                    link(nc.vector.tensor_scalar(S[:, 0, :], NUM[:, :, P], TINY, None, ALU.max), base)
                    link(nc.vector.reciprocal(S[:, 0, :], S[:, 0, :]), base)
                    link(nc.vector.tensor_scalar(S[:, 2, :], NUM[:, :, P], 0.0, -0.5, ALU.is_gt, ALU.mult), base)
                    nc.vector.tensor_scalar(S[:, 0, :], S[:, 0, :], 0.5, None, ALU.mult).then_inc(scales, 1)
                    nc.vector.tensor_scalar(S[:, 1, :], S[:, 2, :], 1.0, None, ALU.add).then_inc(scales, 1)

                for g in range(2):
                    mask(0, g)
                with v.Fori(0, TURNS - 1) as c:
                    for g in range(2, STEPS):
                        mask(c, g)
                    mask(c + 1, 0)
                    take(c)
                    mask(c + 1, 1)
                    scale(c, 3 * c)
                link.skip(3 * (TURNS - 2))
                for g in range(2, STEPS):
                    mask(TURNS - 1, g)
                take(TURNS - 1)
                scale(TURNS - 1, 0)

            @block.gpsimd
            def _(pool):
                link = Link(pool, pool_own)
                with pool.Fori(0, TURNS) as c:
                    pool.wait_ge(scales, 2 * c + 2)
                    link(nc.gpsimd.tensor_tensor(NUM[:, :, 0:P], NUM[:, :, 0:P], bcast_last(S[:, 0, :], P), ALU.mult), 3 * c)
                    link(nc.gpsimd.tensor_tensor(TM[:], K.XN[:, bass.ds(2 * c, 2), :], bcast_last(S[:, 1, :], P), ALU.mult), 3 * c)
                    link(nc.gpsimd.tensor_tensor(TM[:], TM[:], NUM[:, :, 0:P], ALU.add), 3 * c)
                    nc.gpsimd.tensor_tensor(K.X[:, bass.ds(2 * c, 2), :], K.X[:, bass.ds(2 * c, 2), :], TM[:], ALU.add)\
                        .then_inc(added, 1)

            @block.tensor
            def _(pe):
                pe.wait_ge(ready, 2)

                def score(g, nodes):
                    for b in range(2):
                        last = nc.tensor.matmul(
                            K.PS[:, g % RING, :].rearrange("p (a b i) -> p b a i", a=2, b=2)[:, b],
                            QT[:, (2 * g + b) * P:(2 * g + b + 1) * P],
                            KT[:, nodes].rearrange("p (a i) -> p a i", a=2), start=True, stop=True)
                    last.then_inc(scored, 1)

                for g in range(LAG):
                    score(g, bass.ds(0, 2 * P))
                with pe.Fori(0, TURNS) as c:
                    for g in range(STEPS):
                        ahead = g + LAG
                        score(ahead % STEPS, bass.ds(2 * P * c + 2 * P * (ahead // STEPS), 2 * P))
                        if g == 0:
                            pe.wait_ge(taken, c + 1)
                        pe.wait_ge(masked, STEPS * c + (g + 1 + PRIME))
                        for a in range(2):
                            for b in range(2):
                                last = nc.tensor.matmul(
                                    K.PS[:, 5 + a, 0:P + 1], PA[:, g % RING, (2 * a + b) * P:(2 * a + b + 1) * P],
                                    X1[:, 2 * g + b, :], start=(g == 0 and b == 0), stop=(g == STEPS - 1 and b == 1))
                        last.then_inc(summed, 1)


def layer1_gnn(nc, K, D):
    ctx = ExitStack()
    with ctx:
        sb = lambda n, shape, dt: ctx.enter_context(nc.sbuf_tensor(f"g1_{n}", shape, dt))
        QT = sb("qt", [P, NP], F32)
        inner = ExitStack()
        with inner:
            QK = inner.enter_context(nc.sbuf_tensor("g1_qk", [P, T, 2 * P], F32))
            norm_project_stage(nc, K, "p1", K.WP1[:], 2 * P, 2, lambda t, k: QK[:, t:t + k, :])
            cosine_prepare_stage(nc, K, QK, QT, K.XT)
        X1 = sb("x1", [P, T, P + 1], F32)
        cosine_stage(nc, K, QT, K.XT, X1, D["slots"][0:pair_blocks(T) * PAIR_BLOCK, :])


def add_softmax(v, link, nc, K, it, num, S, base, done):
    link(nc.vector.tensor_scalar(S[:, 0:1], num[:, P:P + 1], TINY, None, ALU.max), base)
    link(nc.vector.reciprocal(S[:, 1:2], S[:, 0:1]), base)
    x = K.X[:, bass.ds(it, 1), :].rearrange("p a d -> p (a d)")
    nc.vector.scalar_tensor_tensor(x, num[:, 0:P], S[:, 1:2], x, ALU.mult, ALU.add).then_inc(done, 1)


def layer2_gnn(nc, K, arrival):
    ctx = ExitStack()
    C = P + 1
    with ctx:
        sb = lambda n, shape, dt: ctx.enter_context(nc.sbuf_tensor(f"g2_{n}", shape, dt))
        XS = sb("xs", [P, T, 3 * C], BF16)
        inner = ExitStack()
        with inner:
            HP = inner.enter_context(nc.sbuf_tensor("g2_hp", [P, T, C], F32))
            norm_project_stage(nc, K, "p2", K.WP2[:], C, 3, lambda t, k: HP[:, t:t + k, :], bias=K.BP2[:],
                               arrival=arrival)
            V = K.XT[:, 0:T * C].rearrange("p (t a c) -> p t a c", t=T, a=1)
            split_stage(nc, K, "x2", HP, 1, P, P, (1.0,),
                        (lambda s: XS[:, :, s * C:(s + 1) * C].unsqueeze(2),), V)

        def finish(v, link, it, ps, base, done, tmp):
            link(nc.vector.tensor_reduce(tmp[0][:], ps.rearrange("p (s c) -> p c s", s=3), AX.X, ALU.add), base)
            add_softmax(v, link, nc, K, it, tmp[0], tmp[1], base, done)

        edge_sum_stage(nc, K, "a2", lambda j: XS[:, j, :], 3 * C, finish, 3,
                       bufs=lambda sb: (sb("sum", [P, C], F32), sb("s", [P, 2], F32)))


def layer3_gnn(nc, K, D):
    ctx = ExitStack()
    C = P + 1
    with ctx:
        sb = lambda n, shape, dt: ctx.enter_context(nc.sbuf_tensor(f"g3_{n}", shape, dt))
        XF = sb("xs", [P, T * 6 * C], BF16)
        SB = sb("scores", [P, NP], F32)
        XS = XF[:].rearrange("p (t a c) -> p t a c", a=2, c=3 * C)
        C1 = sb("c1", [P, T, 1], F32)
        C2 = sb("c2", [P, T, 1], F32)
        D0 = sb("d0", [P, T, 1], F32)
        inner = ExitStack()
        with inner:
            HP = inner.enter_context(nc.sbuf_tensor("g3_hp", [P, T, P + 2], F32))
            SROW = XF[0:1, 0:2 * NP].bitcast(F32)
            norm_project_stage(nc, K, "p3", K.WP3[:], P + 2, 3, lambda t, k: HP[:, t:t + k, :], bias=K.BP3[:],
                               row=(K.WP3[:, P:P + 1], K.BP3[0:1, P:P + 1], SROW, D["sd3"]))
            V = K.XT[:, 0:T * C].rearrange("p (t a c) -> p t a c", t=T, a=1)

            def parts(k):
                return lambda s: XS[:, :, k, s * C:(s + 1) * C].unsqueeze(2)

            def natural(c):
                return c[:].rearrange("p (a t) h -> p a t h", a=2)

            split_stage(nc, K, "x3", HP, 1, P, P + 1, (1.0, SLOPE), (parts(0), parts(1)), V,
                        coef=(natural(C1), natural(C2)), keep=D0,
                        first_loads=[(SB[:], D["sd3"].rearrange("a n -> (a n)").partition_broadcast(P))])
        signed_sum_stage(nc, K, SB, XS, C1, C2, D0, D["slots"][0:8 * CAPACITY, :])


def signed_sum_stage(nc, K, SB, XS, C1, C2, D0, slots):
    ctx, sb, sem = open_stage(nc, "signed")
    with ctx:
        C = P + 1
        SN = sb("tile_scores", [P, 2, P], F32)
        ST = sb("above", [P, 2, T, P], U8)
        ED = sb("below", [P, 2, T, P], U8)
        ND = sb("negd", [P, T], F32)
        U = sb("u", [P, 2, C], F32)
        S = sb("s", [P, 2], F32)
        staged, parted = sem("staged"), sem("parted")
        summed, finished, dve, passed = sem("summed"), sem("finished"), sem("dve"), sem("passed")
        emptied = sem("emptied")
        with nc.Block() as block:

            @block.sync
            def _(sp):
                sp.dma_start(*empty_slots(K, slots, CAPACITY // 5)).then_inc(emptied, 16)
                sp.wait_ge(emptied, 16)

            @block.scalar
            def _(act):
                with act.Fori(0, T // 2) as t:
                    for q in range(2):
                        act.wait_ge(summed, 2 * t + q + 1)
                        nc.scalar.activation(ED[:, q].rearrange("p b i -> p (b i)").bitcast(U16),
                                             K.EDGE[:, bass.ds(2 * t + q, 1)].rearrange("p a b i -> p (a b i)").bitcast(U16),
                                             ACT.Copy).then_inc(staged, 1)
                        nc.scalar.activation(SN[:, q, :], SB[:, bass.ds(P * (2 * t + q), P)], ACT.Copy).then_inc(staged, 1)

            @block.vector
            def _(v):
                link = Link(v, dve)
                v.sem_inc(summed, 2)
                v.sem_inc(finished, 2)
                link(nc.vector.tensor_scalar(ND[:], D0[:, :, 0], -1.0, None, ALU.mult))

                def part(it, q, base):
                    v.wait_ge(staged, 2 * it + 2)
                    v.sem_inc(passed, 1)
                    link(nc.vector.tensor_tensor(ST[:, q].bitcast(FP8), bcast_mid(SN[:, q, :], T),
                                                 bcast_last(ND[:], P), ALU.is_ge, saturate=False), base)
                    st, ed = (x[:, q].rearrange("p b i -> p (b i)").bitcast(U32) for x in (ST, ED))
                    link(nc.vector.tensor_tensor(st, st, ed, ALU.bitwise_and), base)
                    nc.vector.tensor_tensor(ed, ed, st, ALU.bitwise_xor).then_inc(parted, 1)

                def finish(it, q, base):
                    v.wait_ge(summed, it + 3)
                    v.wait_ge(finished, it + 2)
                    for k in range(2):
                        link(nc.vector.tensor_reduce(U[:, k, :], K.PS[:, 2 * q + k, 0:3 * C].rearrange("p (s c) -> p c s", s=3),
                                                     AX.X, ALU.add), base)
                    c1, c2 = (c[:, bass.ds(it, 1), :].rearrange("p a b -> p (a b)") for c in (C1, C2))
                    link(nc.vector.tensor_scalar(U[:, 1, :], U[:, 1, :], c2, None, ALU.mult), base)
                    link(nc.vector.scalar_tensor_tensor(U[:, 0, :], U[:, 0, :], c1, U[:, 1, :], ALU.mult, ALU.add), base)
                    add_softmax(v, link, nc, K, it, U[:, 0, :], S, base, finished)

                per = 2 * (2 + 6)
                for q in range(2):
                    part(q, q, 0)
                with v.Fori(0, T // 2 - 1) as t:
                    for q in range(2):
                        finish(2 * t + q, q, per * t)
                        part(2 * t + q + 2, q, per * t)
                link.skip(per * (T // 2 - 2))
                for q in range(2):
                    finish(T - 2 + q, q, 0)

            @block.tensor
            def _(pe):
                with pe.Fori(0, T // 2) as t:
                    for q in range(2):
                        pe.wait_ge(parted, 2 * t + q + 1)
                        pe.wait_ge(finished, 2 * t + q + 1)
                        pe.sem_inc(passed, 1)
                        for j in range(T):
                            for k, e in enumerate((ST, ED)):
                                last = nc.tensor.matmul(K.PS[:, 2 * q + k, 0:3 * C], e[:, q, j, :].bitcast(FP8),
                                                        XS[:, j, k, :], start=(j == 0), stop=(j == T - 1))
                        last.then_inc(summed, 1)


def choose(nc, K, link, LG, E, best, onehot, first):
    iota = bcast_mid(K.IOTA[:, 0:E], T)
    link(nc.vector.tensor_reduce(best, LG, AX.X, ALU.max))
    link(nc.vector.tensor_tensor(onehot, LG, bcast_last(best, E), ALU.is_equal))
    link(nc.vector.tensor_tensor(onehot, onehot, iota, ALU.mult))
    link(nc.vector.tensor_reduce(first, onehot, AX.X, ALU.min))
    link(nc.vector.tensor_tensor(onehot, iota, bcast_last(first, E), ALU.is_equal))


def argmax_route_stage(nc, K, name, LG, E, W, OHT):
    ctx, sb, sem = open_stage(nc, name)
    with ctx:
        S = sb("s", [P, 2, T], F32)
        dve, chosen, transposed = sem("dve"), sem("chosen"), sem("transposed")
        groups = [(t, min(4, T - t)) for t in range(0, T, 4)]
        with nc.Block() as block:

            @block.vector
            def _(v):
                choose(nc, K, Link(v, dve), LG[:], E, S[:, 0, :], W[:], S[:, 1, :])
                nc.vector.sem_inc(chosen, 1)

            @block.tensor
            def _(pe):
                pe.wait_ge(chosen, 1)
                for g, (t, k) in enumerate(groups):
                    for j in range(k):
                        last = nc.tensor.transpose(K.PS[0:E, g, j * P:(j + 1) * P], W[:, t + j, :], K.IDENT[:])
                    last.then_inc(transposed, 1)

            @block.scalar
            def _(act):
                for g, (t, k) in enumerate(groups):
                    act.wait_ge(transposed, g + 1)
                    nc.scalar.activation(OHT[:, t * P:(t + k) * P], K.PS[0:E, g, 0:k * P], ACT.Copy)


class Dense:
    LAG, RING = 2, 4

    def __init__(self, nc, K, sem, tag, weights, G, E, HT, c0, turns):
        self.nc, self.K, self.G, self.E, self.HT, self.c0, self.turns = nc, K, G, E, HT, c0, turns
        self.W1, self.B1, self.W2, self.W = weights
        self.hidden, self.active, self.used, self.added = (sem(f"{tag}_{n}") for n in ("hidden", "active", "used", "added"))

    def tensor(self, pe):
        nc, K, E, HT, LAG, RING = self.nc, self.K, self.E, self.HT, self.LAG, self.RING
        STEPS = E * HT

        def up(k, nodes):
            nc.tensor.matmul(K.PS[:, k % RING, 0:2 * P], self.W1[:, k * P:(k + 1) * P], K.XT[:, nodes],
                             start=True, stop=True).then_inc(self.hidden, 1)

        first = 2 * P * self.c0
        for k in range(LAG):
            up(k, bass.ds(first, 2 * P))
        with pe.Fori(0, self.turns) as c:
            for k in range(STEPS):
                e, h = divmod(k, HT)
                ahead = k + LAG
                up(ahead % STEPS, bass.ds(2 * P * c + (first + 2 * P * (ahead // STEPS)), 2 * P))
                pe.wait_ge(self.active, STEPS * c + k + 1)
                if h == 0:
                    pe.wait_ge(self.added, E * c + e + 1)
                for a in range(2):
                    last = nc.tensor.matmul(K.PS[:, 4 + 2 * (e % 2) + a, 0:P], self.G[:, k % RING, a * P:(a + 1) * P],
                                            self.W2[:, k, :], start=(h == 0), stop=(h == HT - 1))
                last.then_inc(self.used, 1)
        pe.wait_ge(self.added, E * self.turns + 2)

    def scalar(self, act):
        STEPS, RING = self.E * self.HT, self.RING
        with act.Fori(0, self.turns) as c:
            for k in range(STEPS):
                act.wait_ge(self.hidden, STEPS * c + k + 1)
                act.wait_ge(self.used, STEPS * c + k + 1)
                self.nc.scalar.activation(self.G[:, k % RING, :], self.K.PS[:, k % RING, 0:2 * P], ACT.Gelu,
                                          bias=self.B1[:, k:k + 1]).then_inc(self.active, 1)

    def prime(self, v):
        v.sem_inc(self.used, self.RING)
        v.sem_inc(self.added, 2)

    def vector(self, v):
        K, E, HT, RING = self.K, self.E, self.HT, self.RING
        with v.Fori(0, self.turns) as c:
            for e in range(E):
                v.wait_ge(self.used, E * HT * c + (HT * (e + 1) + RING))
                v.wait_ge(self.added, E * c + e + 2)
                for a in range(2):
                    tile = bass.ds(2 * c + (2 * self.c0 + a), 1)
                    x = K.X[:, tile, :].rearrange("p a d -> p (a d)")
                    last = self.nc.vector.scalar_tensor_tensor(x, K.PS[:, 4 + 2 * (e % 2) + a, 0:P], self.W[:, tile, e], x,
                                                               ALU.mult, ALU.add)
                last.then_inc(self.added, 1)


def moe32_layer(nc, K, D):
    ctx = ExitStack()
    with ctx:
        E, HT, RING, LAG = 32, 8, 4, 3
        sb = lambda n, shape, dt: ctx.enter_context(nc.sbuf_tensor(f"f2_{n}", shape, dt))
        W1 = sb("w1", [P, HT * P], F32)
        W2 = sb("w2", [P, HT, P], F32)
        B1 = sb("b1", [P, HT], F32)
        B2 = sb("b2", [E, P], F32)
        BS = sb("b2_parts", [E, 3, P], BF16)
        SPREAD = sb("spread", [E, HT, P], F32)
        SP16 = sb("spread16", [E, HT, P], BF16)
        LG = sb("logits", [P, T, E], F32)
        W = sb("onehot", [P, T, E], F32)
        OHT = sb("oht", [E, NP + 2 * P], BF16)
        G0 = sb("relu", [P, RING, 2 * P], F32)
        G = sb("chosen", [P, RING, 2 * P], F32)
        loads = [(W1[:], D["f2_w1"]), (W2[:], D["f2_w2"]), (B1[:], D["f2_b1"]), (B2[:], D["f2_b2"]), (SPREAD[:], D["spread"])]
        norm_project_stage(nc, K, "f2p", K.R[:, 16:48], E, 4, lambda t, k: LG[:, t:t + k, :], bias=K.BR[:, 16:48], loads=loads)
        argmax_route_stage(nc, K, "f2r", LG, E, W, OHT)
        sems, _, sem = open_stage(nc, "f2m")
        with sems:
            ready, hidden, active, chosen, used, added, dve = (sem("ready"), sem("hidden"), sem("active"), sem("chosen"),
                                                               sem("used"), sem("added"), sem("dve"))
            biased = sem("biased")
            with nc.Block() as block:

                @block.tensor
                def _(pe):
                    pe.wait_ge(ready, 1)

                    def up(k, nodes):
                        nc.tensor.matmul(K.PS[:, k % RING, 0:2 * P], W1[:, k * P:(k + 1) * P], K.XT[:, nodes],
                                         start=True, stop=True)
                        nc.tensor.matmul(K.PS[:, k % RING, 2 * P:4 * P], SP16[:, k, :], OHT[:, nodes],
                                         start=True, stop=True).then_inc(hidden, 1)

                    for k in range(LAG):
                        up(k, bass.ds(0, 2 * P))
                    with pe.Fori(0, T // 2) as c:
                        for k in range(HT):
                            ahead = k + LAG
                            up(ahead % HT, bass.ds(2 * P * c + 2 * P * (ahead // HT), 2 * P))
                            if k == 0:
                                pe.wait_ge(added, c + 1)
                            pe.wait_ge(chosen, HT * c + (k + 1 + RING))
                            for a in range(2):
                                last = nc.tensor.matmul(K.PS[:, 4 + a, 0:P], G[:, k % RING, a * P:(a + 1) * P], W2[:, k, :],
                                                        start=(k == 0), stop=False)
                            last.then_inc(used, 1)
                        for a in range(2):
                            for s in range(3):
                                last = nc.tensor.matmul(K.PS[:, 4 + a, 0:P], OHT[:, bass.ds(2 * P * c + a * P, P)], BS[:, s, :],
                                                        start=False, stop=(s == 2))
                        last.then_inc(biased, 1)

                @block.scalar
                def _(act):
                    with act.Fori(0, T // 2) as c:
                        for k in range(HT):
                            act.wait_ge(hidden, HT * c + k + 1)
                            act.wait_ge(chosen, HT * c + k + 1)
                            nc.scalar.activation(G0[:, k % RING, :], K.PS[:, k % RING, 0:2 * P], ACT.Relu,
                                                 bias=B1[:, k:k + 1]).then_inc(active, 1)

                @block.vector
                def _(v):
                    link = Link(v, dve)
                    for part in range(3):
                        link(nc.vector.tensor_copy(BS[:, part, :], B2[:]))
                        if part < 2:
                            link(nc.vector.tensor_tensor(B2[:], B2[:], BS[:, part, :], ALU.subtract))
                    link(nc.vector.memset(OHT[:, NP:NP + 2 * P], 0.0))
                    nc.vector.tensor_copy(SP16[:], SPREAD[:]).then_inc(ready, 1)
                    v.sem_inc(chosen, RING)
                    v.sem_inc(used, RING)
                    v.sem_inc(added, 1)
                    with v.Fori(0, T // 2) as c:
                        for k in range(HT):
                            v.wait_ge(active, HT * c + k + 1)
                            v.wait_ge(used, HT * c + k + 1)
                            nc.vector.tensor_tensor(G[:, k % RING, :], G0[:, k % RING, :],
                                                    K.PS[:, k % RING, 2 * P:4 * P], ALU.mult).then_inc(chosen, 1)
                        v.wait_ge(biased, c + 1)
                        x = K.X[:, bass.ds(2 * c, 2), :]
                        nc.vector.scalar_tensor_tensor(x, K.PS[:, 4:6, 0:P], 0.0, x, ALU.max, ALU.add).then_inc(added, 1)


def pair_route_stage(nc, K, name, LG, E, R, BLOCK, NB, W, SHARE, SEND, FETCH, WROW):
    ctx, sb, sem = open_stage(nc, name)
    with ctx:
        OH = sb("onehot", [P, 3, T, E], F32)
        REST = sb("rest", [P, T, E], F32)
        CUM = sb("cum", [P, 4, E * R], F32)
        S = sb("s", [P, 6, T], F32)
        KMAX = R * P // BLOCK
        STEP = sb("steps", [P, KMAX], F32)
        MANY = sb("many", [P, E, KMAX], F32)
        BI = sb("block", [P, NB], F32)
        PAST = sb("past", [P, NB, E], F32)
        WR = sb("weight_row", [P, NB], F32)
        PART = sb("partition", [P, 1], F32)
        N8 = sb("blocks", [P, 3, E], F32)
        ROW = sb("row", [P, 2, R], F32)
        NONE = sb("none", [P, 2, R], F32)
        dve, act_in, act_out, pe_in, pe_out = sem("dve"), sem("act_in"), sem("act_out"), sem("pe_in"), sem("pe_out")
        consts = sem("consts")
        with nc.Block() as block:

            @block.gpsimd
            def _(pool):
                for dst, step, p in ((STEP, BLOCK, 0), (BI, 1, 0), (PART, 1, 1)):
                    nc.gpsimd.iota(dst[:], pattern=[[step, dst.shape[1]]], base=0, channel_multiplier=p,
                                   allow_small_or_imprecise_dtypes=True).then_inc(consts, 1)

            @block.vector
            def _(v):
                link = Link(v, dve)
                choose(nc, K, link, LG[:], E, S[:, 4, :], OH[:, 0], S[:, 5, :])
                link(nc.vector.scalar_tensor_tensor(REST[:], OH[:, 0], -3e38, LG[:], ALU.mult, ALU.add))
                choose(nc, K, link, REST[:], E, S[:, 3, :], OH[:, 1], S[:, 5, :])
                nc.vector.tensor_tensor(S[:, 0, :], S[:, 3, :], S[:, 4, :], ALU.subtract).then_inc(act_in, 1)
                nc.vector.tensor_tensor(OH[:, 2], OH[:, 0], OH[:, 1], ALU.add).then_inc(pe_in, 1)
                link(nc.vector.memset(CUM[:, 0, :], 1.0))
                link(nc.vector.memset(CUM[:, 0, :].rearrange("p (e t) -> p e t", t=R)[:, :, 0:1], 0.0))
                v.wait_ge(act_out, 1)
                link(nc.vector.tensor_scalar(S[:, 2, :], S[:, 1, :], 1.0, None, ALU.add))
                link(nc.vector.reciprocal(SHARE[:, 0, :], S[:, 2, :]))
                link(nc.vector.tensor_tensor(SHARE[:, 1, :], S[:, 1, :], SHARE[:, 0, :], ALU.mult))
                nc.vector.tensor_tensor(W[:], OH[:, 0], bcast_last(SHARE[:, 0, :], E), ALU.mult)
                link(nc.vector.tensor_tensor(REST[:], OH[:, 1], bcast_last(SHARE[:, 1, :], E), ALU.mult))
                link(nc.vector.tensor_tensor(W[:], W[:], REST[:], ALU.add))
                v.wait_ge(pe_out, 1)
                for k in range(2):
                    last = nc.vector.tensor_copy(CUM[:, 1 + k, :].rearrange("p (e t) -> p e t", t=R),
                                                 K.PS[:, k, 0:R * E].rearrange("p (t e) -> p e t", e=E))
                link(last)
                link(nc.vector.tensor_tensor_scan(CUM[:, 3, :], CUM[:, 0, :], CUM[:, 2, :], 0.0, ALU.mult, ALU.add))
                v.wait_ge(consts, 3)
                total = CUM[:, 3, :].rearrange("p (e t) -> p e t", t=R)[:, :, R - 1]
                link(nc.vector.tensor_tensor(MANY[:], bcast_last(total, KMAX), bcast_mid(STEP[:], E), ALU.is_gt))
                link(nc.vector.tensor_reduce(N8[:, 0, :], MANY[:], AX.X, ALU.add))
                link(nc.vector.tensor_tensor_scan(N8[:, 1, :], K.ONES[:, 0:E], N8[:, 0, :], 0.0, ALU.mult, ALU.add))
                link(nc.vector.tensor_tensor(N8[:, 2, :], N8[:, 1, :], N8[:, 0, :], ALU.subtract))
                link(nc.vector.tensor_scalar(N8[:, 2, :], N8[:, 2, :], float(BLOCK), None, ALU.mult))
                link(nc.vector.tensor_tensor(CUM[:, 3, :], CUM[:, 3, :], CUM[:, 2, :], ALU.subtract))
                link(nc.vector.tensor_tensor(CUM[:, 3, :], CUM[:, 3, :], CUM[:, 1, :], ALU.add))
                e3 = CUM[:, 3, :].rearrange("p (e t) -> p e t", t=R)
                link(nc.vector.tensor_tensor(e3, e3, bcast_last(N8[:, 2, :], R), ALU.add))
                for k in range(2):
                    last = nc.vector.tensor_tensor(OH[:, k, 0:R], OH[:, k, 0:R], CUM[:, 3, :].rearrange("p (e t) -> p t e", t=R),
                                                   ALU.mult)
                link(last)
                link(nc.vector.tensor_reduce(ROW[:], OH[:, 0:2, 0:R], AX.X, ALU.add))
                link(nc.vector.tensor_scalar(NONE[:], ROW[:], 0.5, NB * BLOCK + 1.0, ALU.is_lt, ALU.mult))
                link(nc.vector.tensor_scalar(ROW[:], ROW[:], 1.0, None, ALU.subtract))
                link(nc.vector.tensor_tensor(ROW[:], ROW[:], NONE[:], ALU.add))
                link(nc.vector.tensor_copy(SEND[:], ROW[:]))
                link(nc.vector.tensor_scalar(ROW[:], ROW[:], NB * BLOCK - 1.0, None, ALU.min))
                link(nc.vector.tensor_copy(FETCH[:], ROW[:]))
                link(nc.vector.tensor_tensor(PAST[:], bcast_mid(N8[:, 1, :], NB), bcast_last(BI[:], E), ALU.is_le))
                link(nc.vector.tensor_reduce(WR[:], PAST[:], AX.X, ALU.add))
                link(nc.vector.tensor_scalar(WR[:], WR[:], E - 1.0, float(P), ALU.min, ALU.mult))
                link(nc.vector.tensor_scalar(WR[:], WR[:], PART[:, 0:1], None, ALU.add))
                nc.vector.tensor_copy(WROW[:], WR[:])

            @block.scalar
            def _(act):
                act.wait_ge(act_in, 1)
                nc.scalar.activation(S[:, 1, :], S[:, 0, :], ACT.Exp).then_inc(act_out, 1)

            @block.tensor
            def _(pe):
                pe.wait_ge(pe_in, 1)
                oh = OH[:, 2, 0:R].rearrange("p t e -> p (t e)")
                nc.tensor.matmul(K.PS[:, 0, 0:R * E], K.LOWER[:], oh, start=True, stop=True)
                nc.tensor.matmul(K.PS[:, 1, 0:R * E], K.ONES[:], oh, start=True, stop=True).then_inc(pe_out, 1)


class Bias:

    def __init__(self, nc, K, sb, sem, W, B2, E):
        self.nc, self.K, self.W, self.B2, self.E = nc, K, W, B2, E
        self.WT = sb("wt", [E, NP], F32)
        self.transposed, self.wt_ready = sem("transposed_w"), sem("wt_ready")
        self.biased, self.taken = sem("biased"), sem("bias_taken")
        self.groups = [(t, min(4, T - t)) for t in range(0, T, 4)]

    def tensor(self, pe):
        nc, K, E = self.nc, self.K, self.E
        for g, (t, k) in enumerate(self.groups):
            if g >= 4:
                pe.wait_ge(self.wt_ready, g - 3)
            for j in range(k):
                last = nc.tensor.transpose(K.PS[0:E, g % 4, j * P:(j + 1) * P], self.W[:, t + j, :], K.IDENT[:])
            last.then_inc(self.transposed, 1)
        for g, (t, k) in enumerate(self.groups):
            pe.wait_ge(self.wt_ready, g + 1)
            if g >= 4:
                pe.wait_ge(self.taken, g - 3)
            for j in range(k):
                last = nc.tensor.matmul(K.PS[:, 4 + g % 4, j * P:(j + 1) * P], self.WT[:, (t + j) * P:(t + j + 1) * P],
                                        self.B2[:], start=True, stop=True)
            last.then_inc(self.biased, 1)
        pe.wait_ge(self.taken, len(self.groups))

    def scalar(self, act):
        for g, (t, k) in enumerate(self.groups):
            act.wait_ge(self.transposed, g + 1)
            self.nc.scalar.activation(self.WT[:, t * P:(t + k) * P], self.K.PS[0:self.E, g % 4, 0:k * P], ACT.Copy)\
                .then_inc(self.wt_ready, 1)

    def vector(self, v):
        for g, (t, k) in enumerate(self.groups):
            v.wait_ge(self.biased, g + 1)
            ps, x = self.K.PS[:, 4 + g % 4, 0:k * P].rearrange("p (k d) -> p k d", d=P), self.K.X[:, t:t + k, :]
            self.nc.vector.tensor_tensor(x, x, ps, ALU.add).then_inc(self.taken, 1)


class PairArrival:

    def __init__(self, nc, K, results, SHARE, FETCH, R):
        self.nc, self.K, self.results, self.SHARE, self.FETCH = nc, K, results, SHARE, FETCH
        self.pieces = [(t0, min(m, R - t0)) for t0, m in ARRIVING if t0 < R]
        self.into = [K.XN[:], K.XT[:, 0:NP].rearrange("p (t d) -> p t d", d=P)]

    def open(self, sem):
        self.fetched, self.added = [sem(f"fetched{c}") for c in range(len(self.pieces))], sem("results_added")

    def fetch(self, pool, c):
        if c >= len(self.pieces):
            return
        t0, m = self.pieces[c]
        for t in range(t0, t0 + m):
            for k in range(2):
                self.nc.gpsimd.indirect_dma_start(
                    out=self.into[k][:, t, :], out_offset=None, in_=self.results,
                    in_offset=bass.IndirectOffsetOnAxis(ap=self.FETCH[:, k, t:t + 1], axis=0)).then_inc(self.fetched[c], 16)

    def add(self, v, c):
        if c >= len(self.pieces):
            return
        t0, m = self.pieces[c]
        v.wait_ge(self.fetched[c], 16 * 2 * m)
        for k in range(2):
            for t in range(t0, t0 + m):
                x = self.K.X[:, t, :]
                last = self.nc.vector.scalar_tensor_tensor(x, self.into[k][:, t, :], self.SHARE[:, k, t:t + 1], x,
                                                           ALU.mult, ALU.add)
            last.then_inc(self.added, 1)
            v.wait_ge(self.added, 2 * c + k + 1)


def pair_experts_stage(nc, K, D, name, E, HT, R, BLOCK, NB, W, B2, SEND, WROW, affine=False, dense=None, arrival=None):
    ctx, sb, sem = open_stage(nc, f"{name}m")
    with ctx:
        RING, A = 3, BLOCK // P
        H = HT * P
        XE = sb("rows", [P, RING, A, P], F32)
        XET = sb("rows_t", [P, RING, BLOCK], F32)
        WB = sb("w", [P, RING, 2 * H + HT], F32)
        G = sb("hidden", [P, RING, HT, BLOCK], F32)
        Y = sb("results", [P, RING, A, P], F32)
        sent, in_x, in_w = sem("sent"), [sem(f"in_x{q}") for q in range(RING)], [sem(f"in_w{q}") for q in range(RING)]
        transposed, xt_ready, hidden, active = sem("transposed"), sem("xt_ready"), sem("hidden"), sem("active")
        summed, y_ready, stored = sem("summed"), sem("y_ready"), [sem(f"stored{q}") for q in range(RING)]
        held = sem("held")
        bias = Bias(nc, K, sb, sem, W, B2, E)
        before, after = [], []
        if dense:
            GD = sb("dense_hidden", [P, Dense.RING, 2 * P], F32)
            pairs = (T - R) // 2
            first = pairs // 2
            before = [Dense(nc, K, sem, "before", (*dense, W), GD, E, HT, R // 2, first)]
            last = 1
            after = [Dense(nc, K, sem, "after", (*dense, W), GD, E, HT, R // 2 + first, pairs - first - last),
                     Dense(nc, K, sem, "last", (*dense, W), GD, E, HT, T // 2 - last, last)]
        if arrival:
            arrival.open(sem)
        slots, results = D["slots"], D[f"{name}_results"]
        TURNS = NB // RING
        with nc.Block() as block:

            @block.gpsimd
            def _(pool):
                def weights(b):
                    nc.gpsimd.indirect_dma_start(out=WB[:, b % RING, :], out_offset=None, in_=D[f"{name}_w"],
                                                 in_offset=bass.IndirectOffsetOnAxis(ap=WROW[:, b:b + 1], axis=0))\
                        .then_inc(in_w[b % RING], 16)

                for b in range(RING):
                    weights(b)
                for t in range(R):
                    for k in range(2):
                        nc.gpsimd.indirect_dma_start(
                            out=slots, out_offset=bass.IndirectOffsetOnAxis(ap=SEND[:, k, t:t + 1], axis=0),
                            in_=K.XN[:, t, :], in_offset=None).then_inc(sent, 16)
                for b in range(RING, NB):
                    pool.wait_ge(summed, b + 1)
                    weights(b)
                if arrival:
                    pool.wait_ge(sent, 16 * 2 * R)
                    for q in range(RING):
                        pool.wait_ge(stored[q], 16 * TURNS + 16)
                    for c in range(len(arrival.pieces)):
                        arrival.fetch(pool, c)

            @block.sync
            def _(sp):
                def load(b, q):
                    sp.dma_start(XE[:, q, :, :].rearrange("p a d -> p (a d)"),
                                 slots[bass.ds(BLOCK * b, BLOCK), :].rearrange("(p a) d -> p (a d)", a=A))\
                        .then_inc(in_x[q], 16)

                def store(b, q):
                    sp.dma_start(results[bass.ds(BLOCK * b, BLOCK), :].rearrange("(p a) d -> p (a d)", a=A),
                                 Y[:, q, :, :].rearrange("p a d -> p (a d)")).then_inc(stored[q], 16)

                sp.wait_ge(sent, 16 * 2 * R)
                for q in range(RING):
                    load(q, q)
                with sp.Fori(0, TURNS - 1) as t:
                    for q in range(RING):
                        sp.wait_ge(y_ready, RING * t + q + 2)
                        sp.sem_inc(held, 1)
                        store(RING * t + q, q)
                        load(RING * t + q + RING, q)
                for q in range(RING):
                    sp.wait_ge(y_ready, NB - RING + q + 2)
                    store(NB - RING + q, q)
                for q in range(RING):
                    sp.wait_ge(stored[q], 16 * TURNS + 16)

            @block.tensor
            def _(pe):
                bias.tensor(pe)
                for part in before:
                    part.tensor(pe)

                def turn(b, q, loads):
                    pe.wait_ge(in_x[q], loads)
                    pe.wait_ge(xt_ready, b + 1)
                    for a in range(A):
                        last = nc.tensor.transpose(K.PS[:, 0, a * P:(a + 1) * P], XE[:, q, a, :], K.IDENT[:])
                    last.then_inc(transposed, 1)

                def up(b, q, loads):
                    pe.wait_ge(in_w[q], loads)
                    pe.wait_ge(xt_ready, b + 2)
                    for h in range(HT):
                        nc.tensor.matmul(K.PS[:, 2 + h, 0:BLOCK], WB[:, q, h * P:(h + 1) * P], XET[:, q, :],
                                         start=True, stop=True).then_inc(hidden, 1)

                def down(b, q):
                    pe.wait_ge(active, HT * b + HT)
                    pe.wait_ge(y_ready, b + 1)
                    for a in range(A):
                        for h in range(HT):
                            last = nc.tensor.matmul(K.PS[:, 1, a * P:(a + 1) * P], G[:, q, h, a * P:(a + 1) * P],
                                                    WB[:, q, H + h * P:H + (h + 1) * P], start=(h == 0), stop=(h == HT - 1))
                    last.then_inc(summed, 1)

                turn(0, 0, 16)
                up(0, 0, 16)
                with pe.Fori(0, TURNS - 1) as t:
                    for q in range(RING):
                        b, nq = RING * t + q, (q + 1) % RING
                        loads = 16 * t + (32 if q == RING - 1 else 16)
                        turn(b + 1, nq, loads)
                        down(b, q)
                        up(b + 1, nq, loads)
                for q in range(RING):
                    b = NB - RING + q
                    if q < RING - 1:
                        turn(b + 1, q + 1, 16 * TURNS)
                    down(b, q)
                    if q < RING - 1:
                        up(b + 1, q + 1, 16 * TURNS)
                for part in after:
                    pe.wait_ge(y_ready, NB + 1)
                    part.tensor(pe)

            @block.scalar
            def _(act):
                bias.scalar(act)
                for part in before:
                    part.scalar(act)
                with act.Fori(0, TURNS) as t:
                    for q in range(RING):
                        b = RING * t + q
                        act.wait_ge(summed, b + 1)
                        for h in range(HT):
                            act.wait_ge(hidden, HT * b + (h + 1 + 2 * HT))
                            nc.scalar.activation(G[:, q, h, :], K.PS[:, 2 + h, 0:BLOCK], ACT.Gelu,
                                                 bias=WB[:, q, 2 * H + h:2 * H + h + 1]).then_inc(active, 1)
                for part in after:
                    part.scalar(act)

            @block.vector
            def _(v):
                v.sem_inc(xt_ready, 1)
                v.sem_inc(y_ready, 1)
                v.sem_inc(summed, RING)
                v.sem_inc(hidden, 2 * HT)
                for q in range(RING):
                    v.sem_inc(stored[q], 16)
                for part in before + after:
                    part.prime(v)
                bias.vector(v)
                if before:
                    v.wait_ge(bias.taken, len(bias.groups))
                    before[0].vector(v)

                def columns(b, q):
                    v.wait_ge(transposed, b + 1)
                    v.wait_ge(hidden, HT * b)
                    if affine:
                        nc.vector.tensor_scalar(XET[:, q, :], K.PS[:, 0, 0:BLOCK], K.GB[:, 0:1], K.GB[:, 1:2],
                                                ALU.mult, ALU.add).then_inc(xt_ready, 1)
                    else:
                        nc.vector.tensor_copy(XET[:, q, :], K.PS[:, 0, 0:BLOCK]).then_inc(xt_ready, 1)

                def result(b, q, stores):
                    v.wait_ge(summed, b + 1 + RING)
                    v.wait_ge(stored[q], stores)
                    nc.vector.tensor_copy(Y[:, q, :, :].rearrange("p a d -> p (a d)"), K.PS[:, 1, 0:BLOCK])\
                        .then_inc(y_ready, 1)

                columns(0, 0)
                with v.Fori(0, TURNS - 1) as t:
                    for q in range(RING):
                        b = RING * t + q
                        columns(b + 1, (q + 1) % RING)
                        result(b, q, 16 * t + 16)
                for q in range(RING):
                    b = NB - RING + q
                    if q < RING - 1:
                        columns(b + 1, q + 1)
                    result(b, q, 16 * TURNS)
                pieces = list(range(len(arrival.pieces))) if arrival else []
                for part in after:
                    part.vector(v)
                    arrival.add(v, pieces.pop(0))
                for c in pieces:
                    arrival.add(v, c)


def pair_layer(nc, K, D, name, r0, HT, R, SHARE, FETCH, twice=False, have_arrival=False):
    E, BLOCK, NB = 8, PAIR_BLOCK, pair_blocks(R)
    ctx = ExitStack()
    with ctx:
        sb = lambda n, shape, dt: ctx.enter_context(nc.sbuf_tensor(f"{name}_{n}", shape, dt))
        LG = sb("logits", [P, T, E], F32)
        W = sb("weights", [P, T, E], F32)
        B2 = sb("b2", [E, P], F32)
        SEND = sb("send", [P, 2, R], I32)
        WROW = sb("weight_rows", [P, NB], I32)
        loads, dense = [(B2[:], D[f"{name}_b2"])], None
        if R < T:
            W1 = sb("w1", [P, E * HT * P], F32)
            W2 = sb("w2", [P, E * HT, P], F32)
            B1 = sb("b1", [P, E * HT], F32)
            dense = (W1, B1, W2)
            loads += [(W1[:], D[f"{name}_w1"]), (W2[:], D[f"{name}_w2"]), (B1[:], D[f"{name}_b1"])]
        norm_project_stage(nc, K, f"{name}p", K.R[:, r0:r0 + E], E, 4, lambda t, k: LG[:, t:t + k, :],
                           bias=K.BR[:, r0:r0 + E], twice=twice, affine=twice, loads=loads)
        pair_route_stage(nc, K, f"{name}r", LG, E, R, BLOCK, NB, W, SHARE, SEND, FETCH, WROW)
        arrival = PairArrival(nc, K, D[f"{name}_results"], SHARE, FETCH, R)
        pair_experts_stage(nc, K, D, name, E, HT, R, BLOCK, NB, W, B2, SEND, WROW, affine=twice, dense=dense,
                           arrival=arrival if have_arrival else None)
    return arrival


def capacity_route_stage(nc, K, name, LG, E, capacity, SEND, FETCH, SHARE):
    ctx, sb, sem = open_stage(nc, name)
    with ctx:
        best, first = sb("best", [P, T], F32), sb("first", [P, T], F32)
        OH = sb("onehot", [P, T, E], F32)
        EX = sb("exp", [P, T, E], F32)
        CUM = sb("cum", [P, 4, E * T], F32)
        S = sb("s", [P, 6, T], F32)
        dve, act_in, act_out, pe_in, pe_out = sem("dve"), sem("act_in"), sem("act_out"), sem("pe_in"), sem("pe_out")
        with nc.Block() as block:

            @block.vector
            def _(v):
                link = Link(v, dve)
                choose(nc, K, link, LG[:], E, best[:], OH[:], first[:])
                nc.vector.tensor_tensor(EX[:], LG[:], bcast_last(best[:], E), ALU.subtract).then_inc(act_in, 1)
                nc.vector.sem_inc(pe_in, 1)
                link(nc.vector.memset(CUM[:, 0, :], 1.0))
                link(nc.vector.memset(CUM[:, 0, :].rearrange("p (e t) -> p e t", t=T)[:, :, 0:1], 0.0))
                v.wait_ge(pe_out, 1)
                for k in range(2):
                    last = nc.vector.tensor_copy(CUM[:, 1 + k, :].rearrange("p (e t) -> p e t", t=T),
                                                 K.PS[:, k, 0:T * E].rearrange("p (t e) -> p e t", e=E))
                link(last)
                link(nc.vector.tensor_tensor_scan(CUM[:, 3, :], CUM[:, 0, :], CUM[:, 2, :], 0.0, ALU.mult, ALU.add))
                link(nc.vector.tensor_tensor(CUM[:, 3, :], CUM[:, 3, :], CUM[:, 2, :], ALU.subtract))
                link(nc.vector.tensor_tensor(CUM[:, 3, :], CUM[:, 3, :], CUM[:, 1, :], ALU.add))
                link(nc.vector.tensor_tensor(OH[:], OH[:], CUM[:, 3, :].rearrange("p (e t) -> p t e", t=T), ALU.mult))
                place, kept, base, row, prob, send = (S[:, k, :] for k in range(6))
                link(nc.vector.tensor_reduce(place, OH[:], AX.X, ALU.add))
                link(nc.vector.tensor_scalar(kept, place, 1.0, None, ALU.is_ge))
                link(nc.vector.tensor_scalar(row, place, float(capacity), None, ALU.is_le))
                link(nc.vector.tensor_tensor(kept, kept, row, ALU.mult))
                link(nc.vector.tensor_scalar(base, first[:], float(capacity), 32.0 * capacity - 1, ALU.mult, ALU.add))
                link(nc.vector.tensor_scalar(row, place, float(capacity), None, ALU.min))
                link(nc.vector.tensor_tensor(row, row, base, ALU.add))
                link(nc.vector.tensor_scalar(row, row, E * capacity - 1.0, None, ALU.min))
                link(nc.vector.tensor_copy(FETCH[:], row))
                link(nc.vector.tensor_tensor(send, row, K.OVERFLOW[:], ALU.subtract))
                link(nc.vector.tensor_tensor(send, send, kept, ALU.mult))
                link(nc.vector.tensor_tensor(send, send, K.OVERFLOW[:], ALU.add))
                link(nc.vector.tensor_copy(SEND[:], send))
                v.wait_ge(act_out, 1)
                link(nc.vector.tensor_reduce(prob, EX[:], AX.X, ALU.add))
                link(nc.vector.reciprocal(prob, prob))
                link(nc.vector.tensor_tensor(SHARE[:], prob, kept, ALU.mult))

            @block.scalar
            def _(act):
                act.wait_ge(act_in, 1)
                nc.scalar.activation(EX[:], EX[:], ACT.Exp).then_inc(act_out, 1)

            @block.tensor
            def _(pe):
                pe.wait_ge(pe_in, 1)
                oh = OH[:].rearrange("p t e -> p (t e)")
                nc.tensor.matmul(K.PS[:, 0, 0:T * E], K.LOWER[:], oh, start=True, stop=True)
                nc.tensor.matmul(K.PS[:, 1, 0:T * E], K.ONES[:], oh, start=True, stop=True).then_inc(pe_out, 1)


def capacity_experts_stage(nc, K, D, name, E, HT, capacity, SEND, FETCH, SHARE, out):
    ctx, sb, sem = open_stage(nc, name)
    with ctx:
        B = 5
        R = capacity // B
        C2 = capacity // 2
        XE = sb("rows", [R, 2, B, P], F32)
        XET = sb("rows_t", [P, 2, B * R], F32)
        W1 = sb("w1", [P, 2, HT * P], F32)
        W2 = sb("w2", [P, 2, HT, P], F32)
        B1 = sb("b1", [P, 2, HT], F32)
        B2 = sb("b2", [R, 2, P], F32)
        G = sb("hidden", [P, 2, HT, B * R], F32)
        Y = sb("results", [R, 2, B, P], F32)
        groups = ARRIVING
        widest = max(k for _, k in groups)
        MASK = sb("mask", [P, widest * P], F32)
        VAL = sb("values", [P, 3, widest * P], F32)
        sent, in_x, in_w = sem("sent"), [sem("in_x0"), sem("in_x1")], [sem("in_rest0"), sem("in_rest1")]
        in_w1 = [sem("in_w1_0"), sem("in_w1_1")]
        transposed, xt_ready, hidden, active = sem("transposed"), sem("xt_ready"), sem("hidden"), sem("active")
        summed, y_ready, stored, dve = sem("summed"), sem("y_ready"), sem("stored"), sem("dve")
        fetched = [sem(f"fetched{g}") for g in range(len(groups))]
        values, taken, added, out_stored = sem("values"), sem("taken"), sem("added"), sem("out_stored")
        slots, results = D["slots"], D["results3"]
        with nc.Block() as block:

            @block.gpsimd
            def _(pool):
                for t in range(T):
                    nc.gpsimd.indirect_dma_start(out=slots, out_offset=bass.IndirectOffsetOnAxis(ap=SEND[:, t:t + 1], axis=0),
                                                 in_=K.XN[:, t, :], in_offset=None).then_inc(sent, 16)
                for k, value in enumerate((1e4, -1e4, 0.0)):
                    nc.gpsimd.memset(VAL[:, k, :], value).then_inc(values, 1)
                pool.wait_ge(sent, 16 * T)
                pool.wait_ge(stored, 16 * E)
                for g, (t0, k) in enumerate(groups):
                    for t in range(t0, t0 + k):
                        nc.gpsimd.indirect_dma_start(out=K.XN[:, t, :], out_offset=None, in_=results,
                                                     in_offset=bass.IndirectOffsetOnAxis(ap=FETCH[:, t:t + 1], axis=0))\
                            .then_inc(fetched[g], 16)

            @block.sync
            def _(sp):
                def load_rows(e, q):
                    sp.dma_start(XE[:, q, :, :].rearrange("p b d -> p (b d)"),
                                 slots[bass.ds(capacity * e, capacity), :].rearrange("(p b) d -> p (b d)", b=B))\
                        .then_inc(in_x[q], 16)

                def load_w1(e, q):
                    sp.dma_start(W1[:, q, :], D["f3_w1"][:, bass.ds(HT * P * e, HT * P)]).then_inc(in_w1[q], 16)

                def load_rest(e, q):
                    sp.dma_start(B1[:, q, :], D["f3_b1"][:, bass.ds(HT * e, HT)]).then_inc(in_w[q], 16)
                    sp.dma_start(W2[:, q, :, :], D["f3_w2"][:, bass.ds(HT * e, HT), :]).then_inc(in_w[q], 16)
                    sp.dma_start(B2[:, q, :], D["f3_b2"][bass.ds(e, 1), :].rearrange("a d -> (a d)")
                                 .partition_broadcast(R)).then_inc(in_w[q], 16)

                def store(e, q):
                    sp.dma_start(results[bass.ds(capacity * e, capacity), :].rearrange("(p b) d -> p (b d)", b=B),
                                 Y[:, q, :, :].rearrange("p b d -> p (b d)")).then_inc(stored, 16)

                for q in range(2):
                    load_w1(q, q)
                    load_rest(q, q)
                sp.wait_ge(sent, 16 * T)
                for q in range(2):
                    load_rows(q, q)
                with sp.Fori(0, E // 2 - 1) as t:
                    for q in range(2):
                        e = 2 * t + q
                        sp.wait_ge(transposed, e + 1)
                        sp.sem_inc(taken, 1)
                        load_rows(e + 2, q)
                        sp.wait_ge(hidden, HT * e + 2 * HT)
                        sp.sem_inc(taken, 1)
                        load_w1(e + 2, q)
                        sp.wait_ge(y_ready, e + 1)
                        sp.sem_inc(taken, 1)
                        store(e, q)
                        load_rest(e + 2, q)
                for q in range(2):
                    sp.wait_ge(y_ready, E - 2 + q + 1)
                    store(E - 2 + q, q)
                sp.wait_ge(stored, 16 * E)
                for g, (t0, k) in enumerate(groups):
                    sp.wait_ge(added, g + 1)
                    full = min(t0 + k, N // P) - t0
                    sp.dma_start(out[t0 * P:(t0 + full) * P, :].rearrange("(t p) d -> p t d", p=P),
                                 K.X[:, t0:t0 + full, :]).then_inc(out_stored, 16)
                sp.dma_start(out[N // P * P:N, :], K.X[0:N % P, N // P, :]).then_inc(out_stored, 16)
                sp.wait_ge(out_stored, 16 * len(groups) + 16)

            @block.tensor
            def _(pe):
                def turn(e, q, loads):
                    pe.wait_ge(in_x[q], loads)
                    pe.wait_ge(xt_ready, e + 1)
                    for b in range(B):
                        last = nc.tensor.transpose(K.PS[:, b // 4, (b % 4) * P:(b % 4) * P + R], XE[:, q, b, :],
                                                   K.IDENT[0:R, 0:R])
                    last.then_inc(transposed, 1)

                def up(e, q, loads):
                    pe.wait_ge(in_w1[q], loads)
                    pe.wait_ge(xt_ready, e + 2)
                    for h in range(HT):
                        pe.wait_ge(active, HT * e + h + 1)
                        for a in range(2):
                            last = nc.tensor.matmul(K.PS[:, 2 + 2 * (h % 2) + a, 0:C2], W1[:, q, h * P:(h + 1) * P],
                                                    XET[:, q, a * C2:(a + 1) * C2], start=True, stop=True)
                        last.then_inc(hidden, 1)

                def down(e, q):
                    pe.wait_ge(active, HT * e + HT + 2)
                    pe.wait_ge(y_ready, e)
                    for b in range(B):
                        for h in range(HT):
                            last = nc.tensor.matmul(K.PS[0:R, 6 + b // 4, (b % 4) * P:(b % 4 + 1) * P],
                                                    G[:, q, h, b * R:(b + 1) * R], W2[:, q, h, :],
                                                    start=(h == 0), stop=(h == HT - 1))
                    last.then_inc(summed, 1)

                turn(0, 0, 16)
                up(0, 0, 16)
                with pe.Fori(0, E // 2 - 1) as t:
                    for q in range(2):
                        e = 2 * t + q
                        turn(e + 1, 1 - q, 16 * t + 16 * q + 16)
                        down(e, q)
                        up(e + 1, 1 - q, 16 * t + 16 * q + 16)
                turn(E - 1, 1, 8 * E)
                down(E - 2, 0)
                up(E - 1, 1, 8 * E)
                down(E - 1, 1)

            @block.scalar
            def _(act):
                with act.Fori(0, E // 2) as t:
                    for q in range(2):
                        e = 2 * t + q
                        act.wait_ge(in_w[q], 48 * t + 48)
                        act.wait_ge(summed, e + 1)
                        for h in range(HT):
                            act.wait_ge(hidden, HT * e + (h + 1 + HT))
                            nc.scalar.activation(G[:, q, h, :].rearrange("p (a n) -> p a n", a=2),
                                                 K.PS[:, 2 + 2 * (h % 2):4 + 2 * (h % 2), 0:C2], ACT.Relu,
                                                 bias=B1[:, q, h:h + 1]).then_inc(active, 1)

            @block.vector
            def _(v):
                v.sem_inc(xt_ready, 1)
                v.sem_inc(active, 2)
                v.sem_inc(summed, 2)
                v.sem_inc(hidden, HT)
                link = Link(v, dve)

                def columns(e, q):
                    v.wait_ge(transposed, e + 1)
                    v.wait_ge(hidden, HT * e)
                    nc.vector.tensor_copy(XET[:, q, :].rearrange("p (b r) -> p b r", b=B),
                                          K.PS[:, 0:2, :].rearrange("p a n -> p (a n)")[:, 0:B * P]
                                          .rearrange("p (b r) -> p b r", b=B)[:, :, 0:R]).then_inc(xt_ready, 1)

                def result(e, q):
                    v.wait_ge(summed, e + 3)
                    v.wait_ge(stored, 16 * e)
                    nc.vector.tensor_tensor(Y[:, q, :, :], K.PS[0:R, 6:8, :].rearrange("p a n -> p (a n)")[:, 0:B * P]
                                            .rearrange("p (b d) -> p b d", b=B), bcast_mid(B2[:, q, :], B), ALU.add)\
                        .then_inc(y_ready, 1)

                columns(0, 0)
                with v.Fori(0, E // 2 - 1) as t:
                    for q in range(2):
                        columns(2 * t + q + 1, 1 - q)
                        result(2 * t + q, q)
                columns(E - 1, 1)
                for q in range(2):
                    result(E - 2 + q, q)

                v.wait_ge(values, 3)
                fmax = float(np.finfo(np.float32).max)
                for g, (t0, k) in enumerate(groups):
                    v.wait_ge(fetched[g], 16 * k)
                    y3, mask = K.XN[:, t0:t0 + k, :], MASK[:, 0:k * P]
                    y = y3.rearrange("p t d -> p (t d)")
                    link(nc.vector.tensor_tensor(y3, y3, bcast_last(SHARE[:, t0:t0 + k], P), ALU.mult))
                    for op, bound, value in ((ALU.is_gt, fmax, 0), (ALU.is_lt, -fmax, 1), (ALU.not_equal, None, 2)):
                        if bound is None:
                            link(nc.vector.tensor_tensor(mask, y, y, op))
                        else:
                            link(nc.vector.tensor_scalar(mask, y, bound, None, op))
                        link(nc.vector.copy_predicated(y, mask.bitcast(U32), VAL[:, value, 0:k * P]))
                    x = K.X[:, t0:t0 + k, :]
                    nc.vector.tensor_tensor(x, x, y3, ALU.add).then_inc(added, 1)


def capacity_layer(nc, K, D, out):
    E, HT = 8, 4
    ctx = ExitStack()
    with ctx:
        sb = lambda n, shape, dt: ctx.enter_context(nc.sbuf_tensor(f"f3_{n}", shape, dt))
        LG = sb("logits", [P, T, E], F32)
        SEND, FETCH = sb("send", [P, T], I32), sb("fetch", [P, T], I32)
        SHARE = sb("share", [P, T], F32)
        norm_project_stage(nc, K, "f3p", K.R[:, 48:48 + E], E, 4, lambda t, k: LG[:, t:t + k, :],
                           bias=K.BR[:, 48:48 + E])
        capacity_route_stage(nc, K, "f3r", LG, E, CAPACITY, SEND, FETCH, SHARE)
        capacity_experts_stage(nc, K, D, "f3m", E, HT, CAPACITY, SEND, FETCH, SHARE, out)


def program(nc, A, out):
    D = {"xd": nc.dram_tensor("head_parts", [P, T, HEADS, 6 * HC], BF16).ap(),
         "sd": nc.dram_tensor("head_scores", [HEADS, NP], F32).ap(),
         "slots": nc.dram_tensor("expert_slots", [SLOTS, P], F32).ap(),
         "f0_results": nc.dram_tensor("block_results0", [pair_blocks(ROUTED0) * PAIR_BLOCK, P], F32).ap(),
         "f1_results": nc.dram_tensor("block_results1", [pair_blocks(T) * PAIR_BLOCK, P], F32).ap(),
         "results3": nc.dram_tensor("slot_results", [8 * CAPACITY, P], F32).ap(),
         "xn0": nc.dram_tensor("normed0", [P, T, P], F32).ap(),
         "sd3": nc.dram_tensor("scores3", [1, NP], F32).ap(), **A}
    K = Core()
    RETIRED.clear()
    ctx = ExitStack()
    with ctx:
        sb = lambda n, shape, dt: ctx.enter_context(nc.sbuf_tensor(n, shape, dt))
        K.EDGE = sb("edge", [P, T, T, P], U8)
        K.X = sb("nodes", [P, T, P], F32)
        K.XN = sb("normed", [P, T, P], F32)
        K.XT = sb("normed_t", [P, NP + 4 * P], F32)
        K.IDENT = sb("ident", [P, P], F32)
        K.ONES = sb("ones", [P, P], F32)
        K.LOWER = sb("lower", [P, P], F32)
        K.COMB = sb("comb", [P, 2 * HC], F32)
        K.IOTA = sb("iota", [P, 32], F32)
        K.OVERFLOW = sb("overflow", [P, T], F32)
        K.ZERO = sb("zero", [P, P], F32)
        K.NEG_HALF = sb("neg_half", [P, T], F32)
        K.WEIGHTS = sb("weights", [P, sum(WEIGHT_COLS.values())], F32)
        K.BIASES = sb("biases", [P, sum(BIAS_COLS.values())], F32)
        K.WP0, K.WP1, K.WP2, K.WP3, K.R, K.GB = columns(K.WEIGHTS, WEIGHT_COLS)
        K.BP0, K.BP2, K.BP3, K.BR, K.AB = columns(K.BIASES, BIAS_COLS)
        K.SB8 = sb("sb8", [HEADS, 1], F32)
        K.PS = ctx.enter_context(nc.psum_tensor("psum", [P, 8, 512], F32))
        setup_stage(nc, K, A)
        layer0_gnn(nc, K, D)
        with ExitStack() as pair:
            SHARE = pair.enter_context(nc.sbuf_tensor("pair_share0", [P, 2, T], F32))
            FETCH = pair.enter_context(nc.sbuf_tensor("pair_fetch0", [P, 2, ROUTED0], I32))
            pair_layer(nc, K, D, "f0", 0, 2, ROUTED0, SHARE, FETCH, twice=True, have_arrival=True)
        layer1_gnn(nc, K, D)
        with ExitStack() as pair:
            SHARE = pair.enter_context(nc.sbuf_tensor("pair_share", [P, 2, T], F32))
            FETCH = pair.enter_context(nc.sbuf_tensor("pair_fetch", [P, 2, T], I32))
            arrival = pair_layer(nc, K, D, "f1", 8, 4, T, SHARE, FETCH)
            layer2_gnn(nc, K, arrival)
        moe32_layer(nc, K, D)
        layer3_gnn(nc, K, D)
        capacity_layer(nc, K, D, out)


def layouts(i):
    a = {k: np.asarray(v) for k, v in i.items()}
    x = np.zeros((NP, P), np.float32)
    x[:N] = a["x"]
    adj = np.zeros((NP, NP), np.int32)
    adj[:N, :N] = a["adj"]
    aw = a["L0_gnn_a_w"]
    sel = np.zeros((P, 2 * HEADS), np.float32)
    for h in range(HEADS):
        sel[HD * h:HD * (h + 1), h] = aw[0, :HD]
        sel[HD * h:HD * (h + 1), HEADS + h] = aw[0, HD:]
    c = np.ascontiguousarray
    experts = {}
    for name, w1, b1, w2, b2 in (("f0", "L0_ffn_W1", "L0_ffn_b1", "L0_ffn_W2", "L0_ffn_b2"),
                                 ("f1", "L1_ffn_W1", "L1_ffn_b1", "L1_ffn_W2", "L1_ffn_b2"),
                                 ("f2", "L2_ffn_W1", "L2_ffn_b1", "L2_ffn_W2", "L2_ffn_b2"),
                                 ("f3", "L3_ffn_w1", "L3_ffn_b1", "L3_ffn_w2", "L3_ffn_b2")):
        if name in ("f0", "f1"):
            experts[f"{name}_w"] = c(np.concatenate([a[w1].reshape(8 * P, -1),
                                                a[w2].reshape(8, -1, P, P).transpose(0, 2, 1, 3).reshape(8 * P, -1),
                                                a[b1].reshape(8, -1, P).transpose(0, 2, 1).reshape(8 * P, -1)], 1))
        if name == "f1":
            experts["f1_b2"] = a[b2]
            continue
        experts[f"{name}_w1"] = c(a[w1].transpose(1, 0, 2).reshape(P, -1))
        experts[f"{name}_w2"] = c(a[w2].reshape(-1, P, P).transpose(1, 0, 2))
        experts[f"{name}_b1"] = c(a[b1].reshape(-1, P).T)
        experts[f"{name}_b2"] = a[b2]
    spread = np.zeros((32, 8, P), np.float32)
    for e in range(32):
        spread[e, e // 4, 32 * (e % 4):32 * (e % 4 + 1)] = 1.0
    return {
        **experts, "spread": spread,
        "x": c(x.reshape(T, P, P).transpose(1, 0, 2)),
        "adj": c(adj.reshape(T, P, T, P).transpose(0, 3, 2, 1).reshape(T, P, NP)),
        "weights": c(np.concatenate([
            a["L0_gnn_W_w"].T, np.zeros((P, 2 * HEADS), np.float32), a["L1_gnn_Wq"].T, a["L1_gnn_Wk"].T,
            a["L2_gnn_W_fc"], np.zeros((P, 1), np.float32), a["L3_gnn_W_w"].T, np.zeros((P, 2), np.float32),
            a["L0_ffn_Wr"], a["L1_ffn_Wg"], a["L2_ffn_router_w"].T, a["L3_ffn_gate_w"],
            np.stack([a["L0_ffn_gamma"], a["L0_ffn_beta"]], 1)], 1)),
        "biases": c(np.concatenate([
            a["L0_gnn_W_b"], np.zeros(2 * HEADS, np.float32), a["L2_gnn_b_fc"], np.zeros(1, np.float32),
            a["L3_gnn_W_b"], np.zeros(2, np.float32),
            a["L0_ffn_br"], a["L1_ffn_bg"], a["L2_ffn_router_b"], a["L3_ffn_gate_b"],
            a["L0_gnn_a_b"].reshape(1), a["L3_gnn_a_b"].reshape(1)])),
        "setup": c(np.concatenate([
            a["L0_gnn_W_w"], a["L2_gnn_W_fc"].T, a["L3_gnn_W_w"], sel, a["L2_gnn_w_att"][P:].reshape(P, 1),
            np.stack([a["L3_gnn_a_src"], a["L3_gnn_a_dst"]], 1),
            np.stack([a["L0_gnn_W_b"], a["L2_gnn_b_fc"], a["L3_gnn_W_b"]], 1)], 1)),
    }


def kernel(**inputs):
    import concourse.bacc as bacc
    from concourse.bass_utils import run_bass_kernel_spmd

    nc = bacc.Bacc("TRN2", target_bir_lowering=False, num_devices=1)
    arrays = layouts(inputs)
    args = {n: nc.dram_tensor(f"in_{n}", a.shape, mybir.dt.from_np(a.dtype), kind="ExternalInput").ap()
            for n, a in arrays.items()}
    out = nc.dram_tensor("out", (N, P), F32, kind="ExternalOutput").ap()
    program(nc, args, out)
    r = run_bass_kernel_spmd(nc, [{f"in_{n}": a for n, a in arrays.items()}], core_ids=[0])
    return r.results[0]["out"]
```
